# Optimizing a Trainium2 kernel written in Bass

```python
import numpy as np
import jax
import jax.numpy as jnp

def _softmax(x, axis=-1):
    return jax.nn.softmax(x, axis=axis)

def _gelu(x):
    return jax.nn.gelu(x, approximate=True)

def _silu(x):
    return jax.nn.silu(x)

def _sigmoid(x):
    return jax.nn.sigmoid(x)

def _layernorm(x, axis=-1, eps=1e-05):
    m = jnp.mean(x, axis=axis, keepdims=True)
    v = jnp.var(x, axis=axis, keepdims=True)
    return (x - m) / jnp.sqrt(v + eps)

def _scatter_add(tgt, idx, src, axis=0):
    return tgt.at[idx].add(src)

def _segment_sum(src, seg, n):
    return jax.ops.segment_sum(src, seg, n)
kernel_name = 'mk_gps_d2_gnn_r16_a4d18e'

def setup_inputs(seed: int=0):
    np.random.seed(seed)
    _w = jnp.asarray

    def _rec_inputs():
        import jax
        import jax.numpy as jnp
        _gk = jax.random.key(seed)
        x = -0.0003713 + 1 * jax.random.normal(jax.random.fold_in(_gk, 1), (3125, 256), jnp.float32)
        src = jax.random.randint(jax.random.fold_in(_gk, 2), (50000,), 0, 3125, jnp.int32)
        dst = jnp.minimum((3125 * jax.random.uniform(jax.random.fold_in(_gk, 3), (50000,)) ** 2.0).astype(jnp.int32), 49999)
        _o = jnp.argsort(dst, stable=True)
        src = src[_o]
        dst = dst[_o]
        edge_attr_384 = -4.94225e-05 + 0.999873 * jax.random.normal(jax.random.fold_in(_gk, 12), (50000, 384), jnp.float32)
        return (x, src, dst, edge_attr_384)
    x, src, dst, edge_attr_384 = _rec_inputs()

    def _L0_gnn_setup():
        import jax, jax.numpy as jnp
        import numpy as np
        N = 3125
        E = 50000
        F = 256
        H = 4
        D = 64
        key = jax.random.key(seed)
        ks = jax.random.split(key, 10)
        s = 0.02
        HD = H * D
        return {'feat': jax.random.normal(ks[0], (N, F), jnp.float32), 'src': jax.random.randint(ks[1], (E,), 0, N), 'dst': jax.random.randint(ks[2], (E,), 0, N), 'Wq': jax.random.normal(ks[3], (HD, F), jnp.float32) * s, 'bq': jnp.zeros((HD,), jnp.float32), 'Wk': jax.random.normal(ks[4], (HD, F), jnp.float32) * s, 'bk': jnp.zeros((HD,), jnp.float32), 'Wv': jax.random.normal(ks[5], (HD, F), jnp.float32) * s, 'bv': jnp.zeros((HD,), jnp.float32), 'Wskip': jax.random.normal(ks[6], (HD, F), jnp.float32) * s, 'bskip': jnp.zeros((HD,), jnp.float32), 'Wgate': jax.random.normal(ks[7], (1, 3 * HD), jnp.float32) * s, 'bgate': jnp.zeros((1,), jnp.float32), 'ln_w': jnp.ones((HD,), jnp.float32), 'ln_b': jnp.zeros((HD,), jnp.float32), 'prelu_a': jnp.float32(0.25)}
    _L0_gnn_all = _L0_gnn_setup()
    _L0_gnn_in = {k: v for k, v in _L0_gnn_all.items() if k in ('Wq', 'bq', 'Wk', 'bk', 'Wv', 'bv', 'Wskip', 'bskip', 'Wgate', 'bgate', 'ln_w', 'ln_b', 'prelu_a')}
    del _L0_gnn_all

    def _L0_mix_setup():
        import jax, jax.numpy as jnp
        import numpy as np
        B, N, C, H = (8, 1024, 256, 8)
        D = C // H
        GH = C // 4
        key = jax.random.key(seed)
        ks = jax.random.split(key, 6)
        s = 0.02
        return {'x': jax.random.normal(ks[0], (B, N, C), dtype=jnp.float32), 'Wqkv': jax.random.normal(ks[1], (C, 3 * C), dtype=jnp.float32) * s, 'Wproj': jax.random.normal(ks[2], (C, C), dtype=jnp.float32) * s, 'bproj': jnp.zeros((C,), dtype=jnp.float32), 'ln_g': jnp.ones((C,), dtype=jnp.float32), 'ln_b': jnp.zeros((C,), dtype=jnp.float32), 'Wg1': jax.random.normal(ks[3], (C, GH), dtype=jnp.float32) * s, 'bg1': jnp.zeros((GH,), dtype=jnp.float32), 'Wg2': jax.random.normal(ks[4], (GH, C), dtype=jnp.float32) * s, 'bg2': jnp.zeros((C,), dtype=jnp.float32)}
    _L0_mix_all = _L0_mix_setup()
    _L0_mix_in = {k: v for k, v in _L0_mix_all.items() if k in ('Wqkv', 'Wproj', 'bproj', 'ln_g', 'ln_b', 'Wg1', 'bg1', 'Wg2', 'bg2')}
    del _L0_mix_all

    def _L0_ffn_setup():
        import jax, jax.numpy as jnp
        import numpy as np
        BN_EPS = 0.001

        def _bn(h, g, b, m, v):
            return g * (h - m) * jax.lax.rsqrt(v + BN_EPS) + b
        key = jax.random.key(seed)
        ks = jax.random.split(key, 8)
        B, F, Df = (256, 64, 256)
        E, H, D = (8, 256, 256)
        s1 = 1.0 / np.sqrt(Df)
        s2 = 1.0 / np.sqrt(H)
        return {'x': jax.random.normal(ks[0], (B, F, Df), jnp.float32), 'Wr': jax.random.normal(ks[1], (Df, E), jnp.float32) * s1, 'br': jnp.zeros((E,), jnp.float32), 'W1': jax.random.normal(ks[2], (E, Df, H), jnp.float32) * s1, 'b1': jnp.zeros((E, H), jnp.float32), 'g1': jnp.ones((E, H), jnp.float32), 'be1': jnp.zeros((E, H), jnp.float32), 'm1': jnp.zeros((E, H), jnp.float32), 'v1': jnp.ones((E, H), jnp.float32), 'W2': jax.random.normal(ks[3], (E, H, H), jnp.float32) * s2, 'b2': jnp.zeros((E, H), jnp.float32), 'g2': jnp.ones((E, H), jnp.float32), 'be2': jnp.zeros((E, H), jnp.float32), 'm2': jnp.zeros((E, H), jnp.float32), 'v2': jnp.ones((E, H), jnp.float32), 'Wo': jax.random.normal(ks[4], (E, H, D), jnp.float32) * s2, 'bo': jnp.zeros((E, D), jnp.float32)}
    _L0_ffn_all = _L0_ffn_setup()
    _L0_ffn_in = {k: v for k, v in _L0_ffn_all.items() if k in ('Wr', 'br', 'W1', 'b1', 'g1', 'be1', 'm1', 'v1', 'W2', 'b2', 'g2', 'be2', 'm2', 'v2', 'Wo', 'bo')}
    del _L0_ffn_all

    def _L1_gnn_setup():
        import jax, jax.numpy as jnp
        import numpy as np
        N_NODES = 625
        N_EDGES = 18750
        IN_FEAT = 256
        OUT_FEAT = 256
        EDGE_DIM = 384
        GRID_SIZE = 4
        SPLINE_ORDER = 3

        def _make_grid(in_features, grid_size=GRID_SIZE, k=SPLINE_ORDER, lo=-1.0, hi=1.0):
            h = (hi - lo) / grid_size
            g = jnp.arange(-k, grid_size + k + 1, dtype=jnp.float32) * h + lo
            return jnp.broadcast_to(g, (in_features, g.shape[0]))

        def _b_splines(x, grid, k=SPLINE_ORDER):
            xe = x[..., None]
            bases = ((xe >= grid[:, :-1]) & (xe < grid[:, 1:])).astype(x.dtype)
            for j in range(1, k + 1):
                left = (xe - grid[:, :-(j + 1)]) / (grid[:, j:-1] - grid[:, :-(j + 1)])
                right = (grid[:, j + 1:] - xe) / (grid[:, j + 1:] - grid[:, 1:-j])
                bases = left * bases[..., :-1] + right * bases[..., 1:]
            return bases
        key = jax.random.key(seed)
        ks = jax.random.split(key, 10)
        n_coef = GRID_SIZE + SPLINE_ORDER
        return {'x': jax.random.normal(ks[0], (N_NODES, IN_FEAT), jnp.float32), 'edge_attr': jax.random.normal(ks[1], (N_EDGES, EDGE_DIM), jnp.float32), 'edge_index': jax.random.randint(ks[2], (2, N_EDGES), 0, N_NODES, jnp.int64), 'W_edge': jax.random.normal(ks[3], (OUT_FEAT, EDGE_DIM), jnp.float32) * 0.03, 'b_edge': jnp.zeros((OUT_FEAT,), jnp.float32), 'W_node': jax.random.normal(ks[4], (OUT_FEAT, IN_FEAT), jnp.float32) * 0.03, 'b_node': jnp.zeros((OUT_FEAT,), jnp.float32), 'base_weight': jax.random.normal(ks[5], (OUT_FEAT, OUT_FEAT), jnp.float32) * 0.05, 'spline_weight': jax.random.normal(ks[6], (OUT_FEAT, OUT_FEAT, n_coef), jnp.float32) * 0.05, 'spline_scaler': jax.random.normal(ks[7], (OUT_FEAT, OUT_FEAT), jnp.float32) * 0.1 + 1.0}
    _L1_gnn_all = _L1_gnn_setup()
    _L1_gnn_in = {k: v for k, v in _L1_gnn_all.items() if k in ('W_edge', 'b_edge', 'W_node', 'b_node', 'base_weight', 'spline_weight', 'spline_scaler')}
    del _L1_gnn_all

    def _L1_mix_setup():
        import jax, jax.numpy as jnp
        import numpy as np
        C_CURV = 1.0
        MIN_NORM = 1e-15
        BALL_EPS = 1e-05
        ATT_EPS = 1e-15
        DIM = 32

        def _norm(x):
            return jnp.clip(jnp.linalg.norm(x, axis=-1, keepdims=True), MIN_NORM)

        def proj(x, c):
            maxnorm = (1.0 - BALL_EPS) / jnp.sqrt(c)
            n = _norm(x)
            return jnp.where(n > maxnorm, x / n * maxnorm, x)

        def expmap0(u, c):
            sc = jnp.sqrt(c)
            n = _norm(u)
            return jnp.tanh(sc * n) * u / (sc * n)

        def logmap0(p, c):
            sc = jnp.sqrt(c)
            n = _norm(p)
            return jnp.arctanh(jnp.clip(sc * n, -1.0 + 1e-07, 1.0 - 1e-07)) * p / (sc * n)

        def mobius_add(x, y, c):
            x2 = jnp.sum(x * x, -1, keepdims=True)
            y2 = jnp.sum(y * y, -1, keepdims=True)
            xy = jnp.sum(x * y, -1, keepdims=True)
            num = (1 + 2 * c * xy + c * y2) * x + (1 - c * x2) * y
            den = 1 + 2 * c * xy + c * c * x2 * y2
            return num / jnp.clip(den, MIN_NORM)

        def conv1d(x, w, pad, groups=1):
            return jax.lax.conv_general_dilated(x, w, (1,), [(pad, pad)], dimension_numbers=('NCH', 'OIH', 'NCH'), feature_group_count=groups)

        def batchnorm(x, gamma, beta):
            mean = jnp.mean(x, axis=(0, 2), keepdims=True)
            var = jnp.var(x, axis=(0, 2), keepdims=True)
            xn = (x - mean) * jax.lax.rsqrt(var + 1e-05)
            return gamma[None, :, None] * xn + beta[None, :, None]

        def _reference_tuple_inner(x, w_qkv, bn_gamma, bn_beta, w_dw, w_pw, w_res, b_res):
            c = C_CURV
            h = logmap0(proj(x, c), c)
            h = jnp.transpose(h, (1, 2, 0))
            h = conv1d(h, w_qkv, pad=2)
            h = batchnorm(h, bn_gamma, bn_beta)
            h = jax.nn.relu(jnp.transpose(h, (2, 0, 1)))
            qkv = proj(expmap0(h, c), c)
            t = jnp.transpose(logmap0(proj(qkv, c), c), (1, 2, 0))
            s = conv1d(t, w_dw, pad=2, groups=t.shape[1])
            s = conv1d(s, w_pw, pad=0, groups=t.shape[1] // DIM)
            cat = jnp.concatenate([t, s], axis=1)
            ai = proj(expmap0(jnp.transpose(cat, (2, 0, 1)), c), c)
            t2 = logmap0(proj(ai, c), c)
            L, N, C2 = t2.shape
            g = C2 // (3 * DIM)
            qkv3 = jnp.transpose(t2, (1, 2, 0)).reshape(N, g, 3 * DIM, L)
            q, k, v = jnp.split(qkv3, 3, axis=2)
            q = jax.nn.relu(q)
            k = jax.nn.relu(k)
            vk = jnp.einsum('ngdl,ngel->ngde', v, k)
            out = jnp.einsum('ngde,ngdl->ngdl', vk, q)
            out = out / (jnp.sum(v, -1, keepdims=True) + ATT_EPS)
            out = jnp.transpose(out.reshape(N, g * DIM, L), (2, 0, 1))
            fx_h = proj(expmap0(out, c), c)
            ft = jnp.transpose(logmap0(proj(fx_h, c), c), (1, 2, 0))
            ft = conv1d(ft, w_res, pad=0) + b_res[None, :, None]
            fx = proj(expmap0(jnp.transpose(ft, (2, 0, 1)), c), c)
            residual = mobius_add(fx, x, c)
            return (fx, residual)
        key = jax.random.key(seed)
        ks = jax.random.split(key, 6)
        L, N, C, TD = (128, 16, 256, 256)
        x = jax.random.normal(ks[0], (L, N, C), jnp.float32) * 0.05
        w_qkv = jax.random.normal(ks[1], (3 * TD, C, 5), jnp.float32) / np.sqrt(C * 5)
        bn_gamma = jnp.ones((3 * TD,), jnp.float32)
        bn_beta = jnp.zeros((3 * TD,), jnp.float32)
        w_dw = jax.random.normal(ks[2], (3 * TD, 1, 5), jnp.float32) / np.sqrt(5.0)
        w_pw = jax.random.normal(ks[3], (3 * TD, DIM, 1), jnp.float32) / np.sqrt(DIM)
        w_res = jax.random.normal(ks[4], (C, 2 * TD, 1), jnp.float32) / np.sqrt(2 * TD)
        b_res = jnp.zeros((C,), jnp.float32)
        return {'x': x, 'w_qkv': w_qkv, 'bn_gamma': bn_gamma, 'bn_beta': bn_beta, 'w_dw': w_dw, 'w_pw': w_pw, 'w_res': w_res, 'b_res': b_res}
    _L1_mix_all = _L1_mix_setup()
    _L1_mix_in = {k: v for k, v in _L1_mix_all.items() if k in ('w_qkv', 'bn_gamma', 'bn_beta', 'w_dw', 'w_pw', 'w_res', 'b_res')}
    del _L1_mix_all

    def _L1_ffn_setup():
        import jax, jax.numpy as jnp
        import numpy as np
        C = 256
        HID = 1024
        E = 8
        TEMP = 1.0
        key = jax.random.key(seed)
        ks = jax.random.split(key, 7)
        x = jax.random.normal(ks[0], (8, 1024, C), dtype=jnp.float32)
        W1 = jax.random.normal(ks[1], (C, HID), dtype=jnp.float32) * 0.02
        b1 = jnp.zeros((HID,), dtype=jnp.float32)
        Wg = jax.random.normal(ks[2], (HID, E), dtype=jnp.float32) * 0.02
        bg = jnp.zeros((E,), dtype=jnp.float32)
        Wd = jax.random.normal(ks[3], (E, HID, C), dtype=jnp.float32) * 0.02
        bd = jnp.zeros((E, C), dtype=jnp.float32)
        return {'x': x, 'W1': W1, 'b1': b1, 'Wg': Wg, 'bg': bg, 'Wd': Wd, 'bd': bd}
    _L1_ffn_all = _L1_ffn_setup()
    _L1_ffn_in = {k: v for k, v in _L1_ffn_all.items() if k in ('W1', 'b1', 'Wg', 'bg', 'Wd', 'bd')}
    del _L1_ffn_all
    return {'x': x, 'src': src, 'dst': dst, 'edge_attr_384': edge_attr_384, 'L0_gnn_Wq': _L0_gnn_in['Wq'], 'L0_gnn_bq': _L0_gnn_in['bq'], 'L0_gnn_Wk': _L0_gnn_in['Wk'], 'L0_gnn_bk': _L0_gnn_in['bk'], 'L0_gnn_Wv': _L0_gnn_in['Wv'], 'L0_gnn_bv': _L0_gnn_in['bv'], 'L0_gnn_Wskip': _L0_gnn_in['Wskip'], 'L0_gnn_bskip': _L0_gnn_in['bskip'], 'L0_gnn_Wgate': _L0_gnn_in['Wgate'], 'L0_gnn_bgate': _L0_gnn_in['bgate'], 'L0_gnn_ln_w': _L0_gnn_in['ln_w'], 'L0_gnn_ln_b': _L0_gnn_in['ln_b'], 'L0_gnn_prelu_a': _L0_gnn_in['prelu_a'], 'L0_mix_Wqkv': _L0_mix_in['Wqkv'], 'L0_mix_Wproj': _L0_mix_in['Wproj'], 'L0_mix_bproj': _L0_mix_in['bproj'], 'L0_mix_ln_g': _L0_mix_in['ln_g'], 'L0_mix_ln_b': _L0_mix_in['ln_b'], 'L0_mix_Wg1': _L0_mix_in['Wg1'], 'L0_mix_bg1': _L0_mix_in['bg1'], 'L0_mix_Wg2': _L0_mix_in['Wg2'], 'L0_mix_bg2': _L0_mix_in['bg2'], 'L0_ffn_Wr': _L0_ffn_in['Wr'], 'L0_ffn_br': _L0_ffn_in['br'], 'L0_ffn_W1': _L0_ffn_in['W1'], 'L0_ffn_b1': _L0_ffn_in['b1'], 'L0_ffn_g1': _L0_ffn_in['g1'], 'L0_ffn_be1': _L0_ffn_in['be1'], 'L0_ffn_m1': _L0_ffn_in['m1'], 'L0_ffn_v1': _L0_ffn_in['v1'], 'L0_ffn_W2': _L0_ffn_in['W2'], 'L0_ffn_b2': _L0_ffn_in['b2'], 'L0_ffn_g2': _L0_ffn_in['g2'], 'L0_ffn_be2': _L0_ffn_in['be2'], 'L0_ffn_m2': _L0_ffn_in['m2'], 'L0_ffn_v2': _L0_ffn_in['v2'], 'L0_ffn_Wo': _L0_ffn_in['Wo'], 'L0_ffn_bo': _L0_ffn_in['bo'], 'L1_gnn_W_edge': _L1_gnn_in['W_edge'], 'L1_gnn_b_edge': _L1_gnn_in['b_edge'], 'L1_gnn_W_node': _L1_gnn_in['W_node'], 'L1_gnn_b_node': _L1_gnn_in['b_node'], 'L1_gnn_base_weight': _L1_gnn_in['base_weight'], 'L1_gnn_spline_weight': _L1_gnn_in['spline_weight'], 'L1_gnn_spline_scaler': _L1_gnn_in['spline_scaler'], 'L1_mix_w_qkv': _L1_mix_in['w_qkv'], 'L1_mix_bn_gamma': _L1_mix_in['bn_gamma'], 'L1_mix_bn_beta': _L1_mix_in['bn_beta'], 'L1_mix_w_dw': _L1_mix_in['w_dw'], 'L1_mix_w_pw': _L1_mix_in['w_pw'], 'L1_mix_w_res': _L1_mix_in['w_res'], 'L1_mix_b_res': _L1_mix_in['b_res'], 'L1_ffn_W1': _L1_ffn_in['W1'], 'L1_ffn_b1': _L1_ffn_in['b1'], 'L1_ffn_Wg': _L1_ffn_in['Wg'], 'L1_ffn_bg': _L1_ffn_in['bg'], 'L1_ffn_Wd': _L1_ffn_in['Wd'], 'L1_ffn_bd': _L1_ffn_in['bd']}

def reference(x, src, dst, edge_attr_384, L0_gnn_Wq, L0_gnn_bq, L0_gnn_Wk, L0_gnn_bk, L0_gnn_Wv, L0_gnn_bv, L0_gnn_Wskip, L0_gnn_bskip, L0_gnn_Wgate, L0_gnn_bgate, L0_gnn_ln_w, L0_gnn_ln_b, L0_gnn_prelu_a, L0_mix_Wqkv, L0_mix_Wproj, L0_mix_bproj, L0_mix_ln_g, L0_mix_ln_b, L0_mix_Wg1, L0_mix_bg1, L0_mix_Wg2, L0_mix_bg2, L0_ffn_Wr, L0_ffn_br, L0_ffn_W1, L0_ffn_b1, L0_ffn_g1, L0_ffn_be1, L0_ffn_m1, L0_ffn_v1, L0_ffn_W2, L0_ffn_b2, L0_ffn_g2, L0_ffn_be2, L0_ffn_m2, L0_ffn_v2, L0_ffn_Wo, L0_ffn_bo, L1_gnn_W_edge, L1_gnn_b_edge, L1_gnn_W_node, L1_gnn_b_node, L1_gnn_base_weight, L1_gnn_spline_weight, L1_gnn_spline_scaler, L1_mix_w_qkv, L1_mix_bn_gamma, L1_mix_bn_beta, L1_mix_w_dw, L1_mix_w_pw, L1_mix_w_res, L1_mix_b_res, L1_ffn_W1, L1_ffn_b1, L1_ffn_Wg, L1_ffn_bg, L1_ffn_Wd, L1_ffn_bd):
    import jax
    import jax.numpy as jnp

    def _L0_gnn_ref(feat, src, dst, Wq, bq, Wk, bk, Wv, bv, Wskip, bskip, Wgate, bgate, ln_w, ln_b, prelu_a):
        import jax, jax.numpy as jnp
        import numpy as np
        N = 3125
        E = 50000
        F = 256
        H = 4
        D = 64
        n = feat.shape[0]
        scale = 1.0 / np.sqrt(D).astype(np.float32)
        q = (feat @ Wq.T + bq).reshape(n, H, D)
        k = (feat @ Wk.T + bk).reshape(n, H, D)
        v = (feat @ Wv.T + bv).reshape(n, H, D)
        e = jnp.einsum('ehd,ehd->eh', q[src], k[dst]) * scale
        m = jax.ops.segment_max(e, dst, num_segments=n)
        ex = jnp.exp(e - m[dst])
        denom = jax.ops.segment_sum(ex, dst, num_segments=n)
        sa = ex / denom[dst]
        agg = jax.ops.segment_sum(sa[:, :, None] * v[src], dst, num_segments=n)
        rst = agg.reshape(n, H * D)
        skip = feat @ Wskip.T + bskip
        g = jax.nn.sigmoid(jnp.concatenate([skip, rst, skip - rst], axis=-1) @ Wgate.T + bgate)
        rst = g * skip + (1.0 - g) * rst
        mu = rst.mean(-1, keepdims=True)
        var = rst.var(-1, keepdims=True)
        rst = (rst - mu) * jax.lax.rsqrt(var + 1e-05) * ln_w + ln_b
        return jnp.where(rst >= 0, rst, prelu_a * rst)

    def _L0_mix_ref(x, Wqkv, Wproj, bproj, ln_g, ln_b, Wg1, bg1, Wg2, bg2):
        import jax, jax.numpy as jnp
        import numpy as np
        B, N, C, H = (8, 1024, 256, 8)
        D = C // H
        GH = C // 4
        b, n, c = x.shape
        h, d = (H, D)
        qkv = (x @ Wqkv).reshape(b, n, 3, h, d)
        q, k, v = (qkv[:, :, 0], qkv[:, :, 1], qkv[:, :, 2])
        k = jax.nn.softmax(k, axis=1)
        context = jnp.einsum('bnhd,bnhv->bhdv', k, v)
        out = jnp.einsum('bnhd,bhdv->bnhv', q, context).reshape(b, n, c)
        mu = jnp.mean(x, axis=-1, keepdims=True)
        var = jnp.var(x, axis=-1, keepdims=True)
        xn = (x - mu) * jax.lax.rsqrt(var + 1e-05) * ln_g + ln_b
        hgate = jax.nn.gelu(xn @ Wg1 + bg1, approximate=False)
        gate = jax.nn.sigmoid(hgate @ Wg2 + bg2)
        return out * gate @ Wproj + bproj

    def _L0_ffn_ref(x, Wr, br, W1, b1, g1, be1, m1, v1, W2, b2, g2, be2, m2, v2, Wo, bo):
        import jax, jax.numpy as jnp
        import numpy as np
        BN_EPS = 0.001

        def _bn(h, g, b, m, v):
            return g * (h - m) * jax.lax.rsqrt(v + BN_EPS) + b
        feat = jnp.mean(x, axis=0)
        w = jax.nn.softmax(feat @ Wr + br, axis=-1)
        h = jnp.einsum('bfd,edh->bfeh', x, W1) + b1
        h = jax.nn.relu(_bn(h, g1, be1, m1, v1))
        h = jnp.einsum('bfeh,ehk->bfek', h, W2) + b2
        h = jax.nn.relu(_bn(h, g2, be2, m2, v2))
        y = jnp.einsum('bfeh,ehd->bfed', h, Wo) + bo
        return jnp.einsum('bfed,fe->bfd', y, w)

    def _L1_gnn_ref(x, edge_attr, edge_index, W_edge, b_edge, W_node, b_node, base_weight, spline_weight, spline_scaler):
        import jax, jax.numpy as jnp
        import numpy as np
        N_NODES = 625
        N_EDGES = 18750
        IN_FEAT = 256
        OUT_FEAT = 256
        EDGE_DIM = 384
        GRID_SIZE = 4
        SPLINE_ORDER = 3

        def _make_grid(in_features, grid_size=GRID_SIZE, k=SPLINE_ORDER, lo=-1.0, hi=1.0):
            h = (hi - lo) / grid_size
            g = jnp.arange(-k, grid_size + k + 1, dtype=jnp.float32) * h + lo
            return jnp.broadcast_to(g, (in_features, g.shape[0]))

        def _b_splines(x, grid, k=SPLINE_ORDER):
            xe = x[..., None]
            bases = ((xe >= grid[:, :-1]) & (xe < grid[:, 1:])).astype(x.dtype)
            for j in range(1, k + 1):
                left = (xe - grid[:, :-(j + 1)]) / (grid[:, j:-1] - grid[:, :-(j + 1)])
                right = (grid[:, j + 1:] - xe) / (grid[:, j + 1:] - grid[:, 1:-j])
                bases = left * bases[..., :-1] + right * bases[..., 1:]
            return bases
        e = edge_attr @ W_edge.T + b_edge
        h = x @ W_node.T + b_node
        row, col = (edge_index[0], edge_index[1])
        msg = e * h[row]
        agg = jax.ops.segment_sum(msg, col, num_segments=x.shape[0])
        grid = _make_grid(OUT_FEAT)
        base = jax.nn.silu(agg) @ base_weight.T
        sp = _b_splines(agg, grid)
        scaled_w = spline_weight * spline_scaler[..., None]
        spline_out = jnp.einsum('nik,oik->no', sp, scaled_w)
        return base + spline_out

    def _L1_mix_ref(x, w_qkv, bn_gamma, bn_beta, w_dw, w_pw, w_res, b_res):
        import jax, jax.numpy as jnp
        import numpy as np
        C_CURV = 1.0
        MIN_NORM = 1e-15
        BALL_EPS = 1e-05
        ATT_EPS = 1e-15
        DIM = 32

        def _norm(x):
            return jnp.clip(jnp.linalg.norm(x, axis=-1, keepdims=True), MIN_NORM)

        def proj(x, c):
            maxnorm = (1.0 - BALL_EPS) / jnp.sqrt(c)
            n = _norm(x)
            return jnp.where(n > maxnorm, x / n * maxnorm, x)

        def expmap0(u, c):
            sc = jnp.sqrt(c)
            n = _norm(u)
            return jnp.tanh(sc * n) * u / (sc * n)

        def logmap0(p, c):
            sc = jnp.sqrt(c)
            n = _norm(p)
            return jnp.arctanh(jnp.clip(sc * n, -1.0 + 1e-07, 1.0 - 1e-07)) * p / (sc * n)

        def mobius_add(x, y, c):
            x2 = jnp.sum(x * x, -1, keepdims=True)
            y2 = jnp.sum(y * y, -1, keepdims=True)
            xy = jnp.sum(x * y, -1, keepdims=True)
            num = (1 + 2 * c * xy + c * y2) * x + (1 - c * x2) * y
            den = 1 + 2 * c * xy + c * c * x2 * y2
            return num / jnp.clip(den, MIN_NORM)

        def conv1d(x, w, pad, groups=1):
            return jax.lax.conv_general_dilated(x, w, (1,), [(pad, pad)], dimension_numbers=('NCH', 'OIH', 'NCH'), feature_group_count=groups)

        def batchnorm(x, gamma, beta):
            mean = jnp.mean(x, axis=(0, 2), keepdims=True)
            var = jnp.var(x, axis=(0, 2), keepdims=True)
            xn = (x - mean) * jax.lax.rsqrt(var + 1e-05)
            return gamma[None, :, None] * xn + beta[None, :, None]

        def _reference_tuple_inner(x, w_qkv, bn_gamma, bn_beta, w_dw, w_pw, w_res, b_res):
            c = C_CURV
            h = logmap0(proj(x, c), c)
            h = jnp.transpose(h, (1, 2, 0))
            h = conv1d(h, w_qkv, pad=2)
            h = batchnorm(h, bn_gamma, bn_beta)
            h = jax.nn.relu(jnp.transpose(h, (2, 0, 1)))
            qkv = proj(expmap0(h, c), c)
            t = jnp.transpose(logmap0(proj(qkv, c), c), (1, 2, 0))
            s = conv1d(t, w_dw, pad=2, groups=t.shape[1])
            s = conv1d(s, w_pw, pad=0, groups=t.shape[1] // DIM)
            cat = jnp.concatenate([t, s], axis=1)
            ai = proj(expmap0(jnp.transpose(cat, (2, 0, 1)), c), c)
            t2 = logmap0(proj(ai, c), c)
            L, N, C2 = t2.shape
            g = C2 // (3 * DIM)
            qkv3 = jnp.transpose(t2, (1, 2, 0)).reshape(N, g, 3 * DIM, L)
            q, k, v = jnp.split(qkv3, 3, axis=2)
            q = jax.nn.relu(q)
            k = jax.nn.relu(k)
            vk = jnp.einsum('ngdl,ngel->ngde', v, k)
            out = jnp.einsum('ngde,ngdl->ngdl', vk, q)
            out = out / (jnp.sum(v, -1, keepdims=True) + ATT_EPS)
            out = jnp.transpose(out.reshape(N, g * DIM, L), (2, 0, 1))
            fx_h = proj(expmap0(out, c), c)
            ft = jnp.transpose(logmap0(proj(fx_h, c), c), (1, 2, 0))
            ft = conv1d(ft, w_res, pad=0) + b_res[None, :, None]
            fx = proj(expmap0(jnp.transpose(ft, (2, 0, 1)), c), c)
            residual = mobius_add(fx, x, c)
            return (fx, residual)
        return _reference_tuple_inner(x, w_qkv, bn_gamma, bn_beta, w_dw, w_pw, w_res, b_res)[0]

    def _L1_ffn_ref(x, W1, b1, Wg, bg, Wd, bd):
        import jax, jax.numpy as jnp
        import numpy as np
        C = 256
        HID = 1024
        E = 8
        TEMP = 1.0
        orig_shape = x.shape
        xf = x.reshape(-1, orig_shape[-1])
        H = jax.nn.gelu(xf @ W1 + b1, approximate=False)
        probs = jax.nn.softmax((H @ Wg + bg) / TEMP, axis=-1)
        assign = jnp.argmax(probs, axis=-1)
        out = jnp.zeros_like(xf)
        for e in range(Wd.shape[0]):
            y = H @ Wd[e] + bd[e]
            sel = (assign == e)[:, None]
            out = out + jnp.where(sel, probs[:, e:e + 1] * y, 0.0)
        return out.reshape(orig_shape)
    edge_index = jnp.stack([src, dst])
    xn = _layernorm(x, axis=-1)
    x = x + _L0_gnn_ref(xn, src, dst, L0_gnn_Wq, L0_gnn_bq, L0_gnn_Wk, L0_gnn_bk, L0_gnn_Wv, L0_gnn_bv, L0_gnn_Wskip, L0_gnn_bskip, L0_gnn_Wgate, L0_gnn_bgate, L0_gnn_ln_w, L0_gnn_ln_b, L0_gnn_prelu_a) + _L0_mix_ref(xn[None], L0_mix_Wqkv, L0_mix_Wproj, L0_mix_bproj, L0_mix_ln_g, L0_mix_ln_b, L0_mix_Wg1, L0_mix_bg1, L0_mix_Wg2, L0_mix_bg2)[0]
    x = x + _L0_ffn_ref(_layernorm(x, axis=-1)[None], L0_ffn_Wr, L0_ffn_br, L0_ffn_W1, L0_ffn_b1, L0_ffn_g1, L0_ffn_be1, L0_ffn_m1, L0_ffn_v1, L0_ffn_W2, L0_ffn_b2, L0_ffn_g2, L0_ffn_be2, L0_ffn_m2, L0_ffn_v2, L0_ffn_Wo, L0_ffn_bo)[0]
    xn = _layernorm(x, axis=-1)
    x = x + _L1_gnn_ref(xn, edge_attr_384, edge_index, L1_gnn_W_edge, L1_gnn_b_edge, L1_gnn_W_node, L1_gnn_b_node, L1_gnn_base_weight, L1_gnn_spline_weight, L1_gnn_spline_scaler) + _L1_mix_ref(xn[None], L1_mix_w_qkv, L1_mix_bn_gamma, L1_mix_bn_beta, L1_mix_w_dw, L1_mix_w_pw, L1_mix_w_res, L1_mix_b_res)[0]
    x = x + _L1_ffn_ref(_layernorm(x, axis=-1)[None], L1_ffn_W1, L1_ffn_b1, L1_ffn_Wg, L1_ffn_bg, L1_ffn_Wd, L1_ffn_bd)[0]
    return x

_drawn_inputs = setup_inputs


def setup_inputs(seed=0):
    import zlib

    import numpy as np

    out = dict(_drawn_inputs(seed))
    spreads = {'L0_gnn_bq': (0.0, 2.0),
     'L0_gnn_bk': (0.0, 2.0),
     'L0_gnn_bv': (0.0, 0.525),
     'L0_gnn_bskip': (0.0, 0.473),
     'L0_gnn_ln_w': (1.0, 0.6),
     'L0_gnn_ln_b': (0.0, 0.8),
     'L0_mix_bproj': (0.0, 0.8),
     'L0_mix_ln_g': (1.0, 0.6),
     'L0_mix_ln_b': (0.0, 0.8),
     'L0_mix_bg1': (0.0, 0.8),
     'L0_mix_bg2': (0.0, 0.8),
     'L0_ffn_br': (0.0, 0.8),
     'L0_ffn_b1': (0.0, 2.0),
     'L0_ffn_g1': (1.0, 0.6),
     'L0_ffn_be1': (0.0, 2.0),
     'L0_ffn_m1': (0.0, 2.0),
     'L0_ffn_v1': (1.0, 0.6),
     'L0_ffn_b2': (0.0, 0.8),
     'L0_ffn_g2': (1.0, 0.6),
     'L0_ffn_be2': (0.0, 2.0),
     'L0_ffn_m2': (0.0, 0.8),
     'L0_ffn_v2': (1.0, 0.6),
     'L0_ffn_bo': (0.0, 0.8),
     'L1_gnn_b_edge': (0.0, 0.368),
     'L1_gnn_b_node': (0.0, 0.355),
     'L1_mix_bn_gamma': (1.0, 0.6),
     'L1_mix_bn_beta': (0.0, 2.0),
     'L1_mix_b_res': (0.0, 2.0),
     'L1_ffn_b1': (0.0, 0.8),
     'L1_ffn_bg': (0.0, 0.507),
     'L1_ffn_bd': (0.0, 2.0)}
    factors = {'L0_gnn_Wq': 10.334,
     'L0_gnn_Wk': 13.339,
     'L0_mix_Wqkv': 8.0,
     'L0_mix_Wproj': 8.0,
     'L0_mix_Wg1': 8.0,
     'L0_mix_Wg2': 8.0,
     'L1_mix_w_dw': 200.0,
     'L1_mix_w_pw': 200.0,
     'L1_ffn_W1': 3.977,
     'L1_ffn_Wg': 4.087,
     'L1_ffn_Wd': 4.957,
     'L0_gnn_Wv': 2.889,
     'L0_gnn_Wgate': 8.0,
     'L0_ffn_Wr': 3.326,
     'L0_ffn_W1': 3.484,
     'L0_ffn_W2': 2.918,
     'L1_gnn_spline_scaler': 24.316,
     'L1_mix_w_qkv': 64.0,
     'L1_mix_w_res': 64.0}
    for name, (base, spread) in spreads.items():
        noise = np.random.default_rng([zlib.crc32(name.encode()), seed]).standard_normal(out[name].shape)
        drawn = base * np.exp(spread * noise) if base else spread * noise
        out[name] = jnp.asarray(drawn.astype(out[name].dtype))
    for name, factor in factors.items():
        out[name] = (out[name] * factor).astype(out[name].dtype)
    return out
```

```python
from contextlib import ExitStack

import numpy as np

import concourse.bass as bass
from concourse import mybir
from concourse.alu_op_type import AluOpType as ALU

F32 = mybir.dt.float32
I32 = mybir.dt.int32
ACT = mybir.ActivationFunctionType
AX = mybir.AxisListType

P = 128
N = 3125
NT = -(-N // P)
NP = NT * P
F = 256
FT = F // P
U = 5
TU = NT // U
CW = NP // 10
NC = NP // CW
E = 50000
G = 4
EG = -(-E // (P * G))
ET = EG * G
EP = ET * P
HEADS = 4
HD = F // HEADS
ED = 384
EC = ED // P
BIG = 1.0e30
LN_EPS = 1e-5
BN_EPS = 1e-3
MIN_NORM = 1e-15
MAX_NORM = 1.0 - 1e-5
REACH = float(np.arctanh(MAX_NORM))
XQ = 8
HID = 1024
HT = HID // P
MC = 768
MT = MC // P
MG = 2 * MC // 96


class Chain:

    def __init__(self, eng, sem):
        self.eng, self.sem, self.n, self.base = eng, sem, 0, 0

    def __call__(self, ins):
        self.n += 1
        ins.then_inc(self.sem, 1)
        self.eng.wait_ge(self.sem, self.base + self.n)

    def enter(self, i, per):
        self.start, self.base, self.per = self.n, i * per, per

    def leave(self, passes):
        assert self.n - self.start == self.per, (self.n - self.start, self.per)
        self.n, self.base = self.start + self.per * passes, 0


class Stage:

    def __init__(self, nc, name):
        self.nc, self.name, self.ctx = nc, name, ExitStack()

    def __enter__(self):
        return self

    def __exit__(self, *a):
        self.ctx.close()

    def sb(self, name, shape, dt=F32):
        return self.ctx.enter_context(self.nc.sbuf_tensor(f"{self.name}_{name}", shape, dt))

    def gather_sem(self, name):
        return self.nc.alloc_semaphore(f"{self.name}_{name}")

    def sem(self, name):
        return self.ctx.enter_context(self.nc.semaphore(f"{self.name}_{name}"))


def recycle_semaphores(nc):
    used = sorted(nc.released_uncleared_semaphores)
    with nc.Block() as block:
        @block.sync
        def _(sp):
            start = used[0]
            for i, n in enumerate(used):
                if i + 1 == len(used) or used[i + 1] != n + 1:
                    sp.sem_clear(range(start, n + 1))
                    start = used[i + 1] if i + 1 < len(used) else None


def mean_and_variance(nc, c, stats, mv, work):
    even, odd = stats[:, :, 1], stats[:, :, 4]
    c(nc.vector.tensor_tensor(mv[:, :, 0], even, odd, ALU.add))
    c(nc.vector.tensor_tensor(work[:], even, odd, ALU.subtract))
    c(nc.vector.tensor_scalar(mv[:, :, 0], mv[:, :, 0], 0.5, None, ALU.mult))
    c(nc.vector.scalar_tensor_tensor(work[:], work[:], 0.25, work[:], ALU.mult, ALU.mult))
    c(nc.vector.tensor_tensor(mv[:, :, 1], stats[:, :, 2], stats[:, :, 5], ALU.add))
    c(nc.vector.scalar_tensor_tensor(mv[:, :, 1], mv[:, :, 1], 1.0 / F, work[:], ALU.mult, ALU.add))
    c(nc.vector.tensor_scalar(mv[:, :, 1], mv[:, :, 1], LN_EPS, None, ALU.add))


def layer_norm(nc, name, src, rows, cols, ident, banks, gain=None, shift=None):
    with Stage(nc, name) as st:
        stats = st.sb("stats", [P, NT, 6])
        mv = st.sb("mean_var", [P, NT, 2])
        rstd = st.sb("rstd", [P, NT])
        var_ready, std_ready, rows_ready = st.sem("var"), st.sem("std"), st.sem("rows")
        transposed, copied, own = st.sem("transposed"), st.sem("copied"), st.sem("own")
        with nc.Block() as block:
            @block.vector
            def _(dve):
                c = Chain(dve, own)
                with dve.Fori(0, NT) as t:
                    nc.vector.bn_stats(stats[:, bass.ds(t, 1), :], src[:, bass.ds(t, 1), :]).then_inc(own, 1)
                c.n = NT
                dve.wait_ge(own, NT)
                mean_and_variance(nc, c, stats, mv, rstd)
                dve.sem_inc(var_ready, 1)
                dve.wait_ge(std_ready, 1)
                c(nc.vector.reciprocal(rstd[:], rstd[:]))
                with dve.Fori(0, NT) as t:
                    nc.vector.tensor_scalar(rows[:, bass.ds(t, 1), :], src[:, bass.ds(t, 1), :],
                                            mv[:, bass.ds(t, 1), 0], rstd[:, bass.ds(t, 1)],
                                            ALU.subtract, ALU.mult).then_inc(rows_ready, 1)

            @block.tensor
            def _(pe):
                for tt in range(TU):
                    for u in range(U):
                        pe.wait_ge(rows_ready, tt * U + u + 1)
                        pe.wait_ge(copied, (tt * U + u) * FT + FT)
                        for f in range(FT):
                            nc.tensor.transpose(banks[u][:, f * P:(f + 1) * P],
                                                rows[:, bass.ds(tt * U + u, 1), f * P:(f + 1) * P],
                                                ident[:]).then_inc(transposed, 1)

            @block.scalar
            def _(act):
                act.sem_inc(copied, U * FT)
                act.wait_ge(var_ready, 1)
                nc.scalar.activation(rstd[:], mv[:, :, 1], ACT.Sqrt).then_inc(std_ready, 1)
                with act.Fori(0, TU) as tt:
                    for u in range(U):
                        act.wait_ge(transposed, (tt * U + u) * FT + FT)
                        for f in range(FT):
                            to = cols[:, f, bass.ds((tt * U + u) * P, P)]
                            if gain is None:
                                nc.scalar.activation(to, banks[u][:, f * P:(f + 1) * P], ACT.Copy).then_inc(copied, 1)
                            else:
                                nc.scalar.activation(to, banks[u][:, f * P:(f + 1) * P], ACT.Identity,
                                                     scale=gain[:, f:f + 1], bias=shift[:, f:f + 1]).then_inc(copied, 1)


def node_tables(nc, name, cols, weights, biases, tables, banks):
    n = len(tables)
    with Stage(nc, name) as st:
        w = st.sb("w", [P, n, FT, F])
        b = st.sb("b", [P, n, F])
        rows = st.sb("rows", [P, U, n, F])
        loaded, product, added = st.sem("loaded"), st.sem("product"), st.sem("added")
        stored = [st.sem(f"stored{u}") for u in range(U)]

        def bank(k):
            return banks[k % U][:, 0:F]
        with nc.Block() as block:
            @block.sync
            def _(sp):
                for j in range(n):
                    sp.dma_start(w[:, j], weights[j]).then_inc(loaded, 16)
                    sp.dma_start(b[:, j], biases[j]).then_inc(loaded, 16)
                for u in range(U):
                    sp.sem_inc(stored[u], 16 * n)
                with sp.Fori(0, TU) as tt:
                    for u in range(U):
                        sp.wait_ge(added, (tt * U + u) * n + n + U)
                        for j in range(n):
                            sp.dma_start(tables[j][bass.ds((tt * U + u) * P, P), :],
                                         rows[:, u, j]).then_inc(stored[u], 16)
                for u in range(U):
                    sp.wait_ge(stored[u], 16 * n * (TU + 1))

            @block.tensor
            def _(pe):
                pe.wait_ge(loaded, 32 * n)
                for tt in range(TU):
                    for u in range(U):
                        for j in range(n):
                            pe.wait_ge(added, (tt * U + u) * n + j + 1)
                            for f in range(FT):
                                mm = nc.tensor.matmul(bank(u * n + j), cols[:, f, bass.ds((tt * U + u) * P, P)],
                                                      w[:, j, f], start=f == 0, stop=f == FT - 1)
                            mm.then_inc(product, 1)

            @block.vector
            def _(dve):
                dve.sem_inc(added, U)
                with dve.Fori(0, TU) as tt:
                    for u in range(U):
                        dve.wait_ge(stored[u], (tt + 1) * (16 * n))
                        for j in range(n):
                            dve.wait_ge(product, (tt * U + u) * n + j + 1)
                            nc.vector.tensor_tensor(rows[:, u, j], bank(u * n + j), b[:, j], ALU.add).then_inc(added, 1)


def constants(nc, a, m, banks):
    with Stage(nc, "const") as st:
        dst_i = st.sb("dst_i", [P, ET], I32)
        tile_of = st.sb("tile_of", [P, ET])
        from_start = st.sb("from_start", [P, ET])
        from_end = st.sb("from_end", [P, ET])
        hits = st.sb("hits", [P, 2, ET])
        tile_no = st.sb("tile_no", [P, NT])
        most = st.sb("most", [P, 2 * NT])
        most_of_all = st.sb("most_of_all", [2 * NT, 1])
        row = st.sb("row", [1, 2 * NT])
        work = st.sb("work", [1, 4, NT])
        rng_f = st.sb("rng_f", [1, NT, 3])
        edges, nodes, filled, made = st.sem("edges"), st.sem("nodes"), st.sem("filled"), st.sem("made")
        own, tables, turned = st.sem("own"), st.sem("tables"), st.sem("turned")
        with nc.Block() as block:
            @block.sync
            def _(sp):
                sp.dma_start(dst_i[:], a["dst_tiles"]).then_inc(edges, 16)
                sp.dma_start(m.src[:], a["src_tiles"]).then_inc(nodes, 16)
                sp.dma_start(m.x[:], a["x"].rearrange("(t p) f -> p t f", p=P)).then_inc(nodes, 16)
                sp.wait_ge(nodes, 32)

            @block.gpsimd
            def _(pool):
                nc.gpsimd.memset(m.ident[:], 0.0).then_inc(filled, 1)
                pool.wait_ge(filled, 1)
                nc.gpsimd.affine_select(out=m.ident[:], in_=m.ident[:], compare_op=ALU.not_equal, fill=1.0,
                                        base=0, pattern=[[-1, P]], channel_multiplier=1).then_inc(made, 1)
                nc.gpsimd.iota(from_start[:], [[1, EG], [0, G]], base=1, channel_multiplier=0,
                               allow_small_or_imprecise_dtypes=True).then_inc(made, 1)
                nc.gpsimd.iota(from_end[:], [[-1, EG], [0, G]], base=EG, channel_multiplier=0,
                               allow_small_or_imprecise_dtypes=True).then_inc(made, 1)
                nc.gpsimd.iota(tile_no[:], [[1, NT]], base=0, channel_multiplier=0,
                               allow_small_or_imprecise_dtypes=True).then_inc(made, 1)
                nc.gpsimd.iota(m.node_no[:], [[1, NP]], base=0, channel_multiplier=0,
                               allow_small_or_imprecise_dtypes=True).then_inc(made, 1)

            @block.vector
            def _(dve):
                c = Chain(dve, own)
                c(nc.vector.memset(m.zeros[:], 0.0))
                dve.wait_ge(edges, 16)
                c(nc.vector.tensor_copy(m.dst[:], dst_i[:]))
                c(nc.vector.tensor_scalar(dst_i[:], dst_i[:], 7, None, ALU.arith_shift_right))
                c(nc.vector.tensor_copy(tile_of[:], dst_i[:]))
                dve.wait_ge(made, 5)
                with dve.Fori(0, NT) as t:
                    c.enter(t, 4)
                    c(nc.vector.scalar_tensor_tensor(hits[:, 0], tile_of[:], tile_no[:, bass.ds(t, 1)], from_start[:],
                                                     ALU.is_equal, ALU.mult))
                    c(nc.vector.scalar_tensor_tensor(hits[:, 1], tile_of[:], tile_no[:, bass.ds(t, 1)], from_end[:],
                                                     ALU.is_equal, ALU.mult))
                    c(nc.vector.tensor_reduce(most[:, bass.ds(t, 1)], hits[:, 0], AX.X, ALU.max))
                    c(nc.vector.tensor_reduce(most[:, bass.ds(t + NT, 1)], hits[:, 1], AX.X, ALU.max))
                c.leave(NT)
                dve.sem_inc(tables, 1)
                dve.wait_ge(turned, 1)
                c(nc.vector.tensor_reduce(most_of_all[:], banks[0][0:2 * NT, 0:P], AX.X, ALU.max))
                dve.sem_inc(tables, 1)
                dve.wait_ge(turned, 2)
                c(nc.vector.tensor_copy(row[:], banks[1][0:1, 0:2 * NT]))
                end, first, count, ones = (work[:, k] for k in range(4))
                c(nc.vector.memset(ones, 1.0))
                c(nc.vector.tensor_scalar(end, row[:, 0:NT], 1.0, None, ALU.max))
                c(nc.vector.tensor_scalar(first, row[:, NT:2 * NT], -1.0, float(EG), ALU.mult, ALU.add))
                c(nc.vector.scalar_tensor_tensor(first, end, -1.0, first, ALU.add, ALU.min))
                c(nc.vector.tensor_tensor(count, end, first, ALU.subtract))
                c(nc.vector.tensor_tensor_scan(rng_f[:, :, 1], ones, count, 0.0, ALU.mult, ALU.add))
                c(nc.vector.tensor_tensor(rng_f[:, :, 0], rng_f[:, :, 1], count, ALU.subtract))
                c(nc.vector.tensor_tensor(rng_f[:, :, 2], first, rng_f[:, :, 0], ALU.subtract))
                c(nc.vector.tensor_copy(m.ranges[:], rng_f[:].rearrange("p t k -> p (t k)")))

            @block.tensor
            def _(pe):
                pe.wait_ge(tables, 1)
                nc.tensor.transpose(banks[0][0:2 * NT, 0:P], most[:], m.ident[:]).then_inc(turned, 1)
                pe.wait_ge(tables, 2)
                nc.tensor.matmul(banks[1][0:1, 0:2 * NT], most_of_all[:], m.ident[0:2 * NT, 0:2 * NT],
                                 start=True, stop=True).then_inc(turned, 1)


def edge_scores(nc, a, m, banks):
    H = G
    PAIRS = ET // (2 * H)
    with Stage(nc, "scores") as st:
        src = st.sb("src", [P, ET], I32)
        dst = st.sb("dst", [P, 3, ET], I32)
        dst0 = st.sb("dst0", [P, ET], I32)
        ix = st.sb("ix", [P, 2, 2, H], I32)
        q = st.sb("q", [P, 2 * H, F])
        k = st.sb("k", [P, 2 * H, F])
        qk = st.sb("qk", [P, 2, H, F])
        S = st.sb("S", [P, HEADS, ET])
        R = st.sb("R", [P, HEADS, ET])
        W = st.sb("W", [P, HEADS, ET])
        bound = st.sb("bound", [P, 2, ET])
        tails = st.sb("tails", [P, 2, HEADS])
        low = st.sb("low", [P, 2, 1])
        scan_in = st.sb("scan_in", [HEADS, 2, P])
        carried = st.sb("carried", [HEADS, P + 1])
        carry = st.sb("carry", [P, HEADS])
        probs = st.sb("probs", [P, ET, HEADS])
        loaded, index, dotted, own = st.sem("loaded"), st.sem("index"), st.sem("dotted"), st.sem("own")
        gathers = st.sem("gathers")
        gathered = [st.gather_sem(f"gathered{u}") for u in range(2 * H)]
        dst_ready, scans, turned, diff, exps, stored = (st.sem(x) for x in
                                                        ("dst0", "scans", "turned", "diff", "exps", "stored"))
        with nc.Block() as block:
            @block.sync
            def _(sp):
                sp.dma_start(src[:], a["src_scan"]).then_inc(loaded, 16)
                for j, x in enumerate(("dst_scan", "before_scan", "after_scan")):
                    sp.dma_start(dst[:, j], a[x]).then_inc(loaded, 16)
                sp.wait_ge(exps, 1)
                sp.dma_start(m.d_probs.rearrange("(p j) h -> p j h", p=P), probs[:]).then_inc(stored, 16)
                sp.wait_ge(stored, 16)
                sp.dma_start(m.probs[:], m.d_probs.rearrange("(j p) h -> p j h", p=P)).then_inc(stored, 16)
                sp.wait_ge(stored, 32)

            @block.scalar
            def _(act):
                act.wait_ge(loaded, 64)
                act.wait_ge(dst_ready, 1)
                with act.Fori(0, PAIRS) as jj:
                    for h in range(2):
                        act.wait_ge(dotted, jj * 2 + h + 1)
                        nc.scalar.activation(ix[:, h, 0], src[:, bass.ds(jj * (2 * H) + h * H, H)], ACT.Copy).then_inc(index, 1)
                        nc.scalar.activation(ix[:, h, 1], dst0[:, bass.ds(jj * (2 * H) + h * H, H)], ACT.Copy).then_inc(index, 1)
                act.wait_ge(diff, 1)
                nc.scalar.activation(probs[:], S[:].rearrange("p h j -> p j h"), ACT.Exp, scale=float(HD) ** -0.5).then_inc(exps, 1)

            @block.gpsimd
            def _(pool):
                with pool.Fori(0, PAIRS) as jj:
                    for h in range(2):
                        pool.wait_ge(index, jj * 4 + h * 2 + 2)
                        pool.sem_inc(gathers, 1)
                        for u in range(H):
                            for j, (to, table) in enumerate(((q, m.d_q), (k, m.d_k))):
                                nc.gpsimd.indirect_dma_start(
                                    out=to[:, h * H + u, :], out_offset=None, in_=table,
                                    in_offset=bass.IndirectOffsetOnAxis(ap=ix[:, h, j, u:u + 1], axis=0)
                                ).then_inc(gathered[h * H + u], 16)

            @block.vector
            def _(dve):
                c = Chain(dve, own)
                dve.sem_inc(dotted, 2)
                dve.wait_ge(loaded, 64)
                nc.vector.tensor_scalar(dst0[:], dst[:, 0], 0.0, None, ALU.max).then_inc(dst_ready, 1)
                for j in range(2):
                    c(nc.vector.tensor_tensor(bound[:, j], dst[:, 0], dst[:, j + 1], ALU.not_equal))
                    c(nc.vector.tensor_scalar(bound[:, j], bound[:, j], -BIG, None, ALU.mult))
                    c(nc.vector.tensor_reduce(low[:, j], bound[:, j], AX.X, ALU.min))
                with dve.Fori(0, PAIRS) as jj:
                    c.enter(jj, 2)
                    for h in range(2):
                        for u in range(H):
                            dve.wait_ge(gathered[h * H + u], jj * 32 + 32)
                        dve.wait_ge(dotted, jj * 2 + h + 1)
                        c(nc.vector.tensor_tensor(qk[:, h], q[:, h * H:(h + 1) * H], k[:, h * H:(h + 1) * H], ALU.mult))
                        nc.vector.tensor_reduce(
                            S[:, :, bass.ds(jj * (2 * H) + h * H, H)].rearrange("p h j -> p j h"),
                            qk[:, h].rearrange("p j (h d) -> p j h d", h=HEADS), AX.X, ALU.add).then_inc(dotted, 1)
                c.leave(PAIRS)
                dve.wait_ge(dotted, 2 * PAIRS + 2)

                def scan(out, by, seen, first, back):
                    step = slice(None, None, -1) if back else slice(None)
                    for h in range(HEADS):
                        ins = nc.vector.tensor_tensor_scan(out[:, h, step], by[:, step], seen[:, h, step],
                                                           -BIG if first is None else first[:, h:h + 1], ALU.add, ALU.max)
                        c(ins)

                for j, (seen, out) in enumerate(((S, R), (R, W))):
                    back = j == 1
                    edge = 0 if back else ET - 1
                    scan(W, bound[:, j], seen, None, back)
                    c(nc.vector.tensor_copy(tails[:, 0], W[:, :, edge]))
                    nc.vector.tensor_copy(tails[:, 1], low[:, j].to_broadcast([P, HEADS])).then_inc(scans, 1)
                    dve.wait_ge(turned, 3 * j + 2)
                    c(nc.vector.tensor_copy(scan_in[:, 0], banks[0][0:HEADS, 0:P]))
                    c(nc.vector.tensor_copy(scan_in[:, 1], banks[1][0:HEADS, 0:P]))
                    c(nc.vector.memset(carried[:], -BIG))
                    step = slice(P - 1, None, -1) if back else slice(None)
                    out_c = carried[:, P - 1::-1] if back else carried[:, 1:P + 1]
                    c(nc.vector.tensor_tensor_scan(out_c, scan_in[:, 1, step], scan_in[:, 0, step], -BIG, ALU.add, ALU.max))
                    dve.sem_inc(scans, 1)
                    dve.wait_ge(turned, 3 * j + 3)
                    c(nc.vector.tensor_copy(carry[:], banks[2][:, 0:HEADS]))
                    scan(out, bound[:, j], seen, carry, back)
                nc.vector.tensor_tensor(S[:], S[:], W[:], ALU.subtract).then_inc(diff, 1)

            @block.tensor
            def _(pe):
                for j in range(2):
                    pe.wait_ge(scans, 2 * j + 1)
                    for i in range(2):
                        nc.tensor.transpose(banks[i][0:HEADS, 0:P], tails[:, i], m.ident[:]).then_inc(turned, 1)
                    pe.wait_ge(scans, 2 * j + 2)
                    part = carried[:, 1:P + 1] if j else carried[:, 0:P]
                    nc.tensor.transpose(banks[2][:, 0:HEADS], part, m.ident[0:HEADS, 0:HEADS]).then_inc(turned, 1)


def steps_of(eng, m, t):
    first = eng.value_load(m.ranges[0:1, bass.ds(t * 3, 1)], min_val=0, max_val=NT * EG)
    end = eng.value_load(m.ranges[0:1, bass.ds(t * 3 + 1, 1)], min_val=1, max_val=NT * EG)
    shift = eng.value_load(m.ranges[0:1, bass.ds(t * 3 + 2, 1)])
    return first, end, shift


def group_of(eng, s, shift):
    return eng.bass.s_assert_within(s + shift, 0, EG - 1,
                                    skip_runtime_bounds_check_because="the ranges are made of groups that exist")


def attention_sums(nc, a, m, banks):
    WIDE = F + HEADS
    with Stage(nc, "attend") as st:
        ix = st.sb("ix", [P, G], I32)
        v = st.sb("v", [P, G, F])
        pv = st.sb("pv", [P, G, WIDE])
        hot = st.sb("hot", [P, G, P])
        index, weighted, multiplied, summed, kept = (st.sem(x) for x in ("index", "weighted", "multiplied", "summed", "kept"))
        gathers = st.sem("gathers")
        gathered = [st.gather_sem(f"gathered{g}") for g in range(G)]
        acc = banks[0][:, 0:WIDE]
        with nc.Block() as block:
            @block.scalar
            def _(act):
                with act.Fori(0, NT) as t:
                    first, end, shift = steps_of(act, m, t)
                    with act.Fori(first, end) as s:
                        i = group_of(act, s, shift)
                        for g in range(G):
                            act.wait_ge(weighted, s * G + g + 1)
                            nc.scalar.activation(ix[:, g:g + 1], m.src[:, bass.ds(i * G + g, 1)], ACT.Copy).then_inc(index, 1)

            @block.gpsimd
            def _(pool):
                with pool.Fori(0, NT) as t:
                    first, end, shift = steps_of(pool, m, t)
                    with pool.Fori(first, end) as s:
                        for g in range(G):
                            pool.wait_ge(index, s * G + g + 1)
                            pool.wait_ge(weighted, s * G + g + 1)
                            pool.sem_inc(gathers, 1)
                            nc.gpsimd.indirect_dma_start(
                                out=v[:, g, :], out_offset=None, in_=m.d_v,
                                in_offset=bass.IndirectOffsetOnAxis(ap=ix[:, g:g + 1], axis=0)
                            ).then_inc(gathered[g], 16)

            @block.vector
            def _(dve):
                dve.sem_inc(weighted, G)
                with dve.Fori(0, NT) as t:
                    first, end, shift = steps_of(dve, m, t)
                    with dve.Fori(first, end) as s:
                        i = group_of(dve, s, shift)
                        for g in range(G):
                            dve.wait_ge(multiplied, s * G + g + 1)
                            nc.vector.tensor_scalar(hot[:, g], m.node_no[:, bass.ds(t * P, P)],
                                                    m.dst[:, bass.ds(i * G + g, 1)], None, ALU.is_equal)
                            prob = m.probs[:, bass.ds(i * G + g, 1), :].rearrange("p j h -> p (j h)")
                            nc.vector.tensor_copy(pv[:, g, F:WIDE], prob)
                            dve.wait_ge(gathered[g], (s + 1) * 16)
                            nc.vector.tensor_tensor(pv[:, g, 0:F].rearrange("p (h d) -> p h d", h=HEADS),
                                                    v[:, g].rearrange("p (h d) -> p h d", h=HEADS),
                                                    prob.unsqueeze(2).to_broadcast([P, HEADS, HD]),
                                                    ALU.mult).then_inc(weighted, 1)
                    dve.wait_ge(summed, t + 1)
                    nc.vector.tensor_copy(m.sums[:, bass.ds(t, 1), :], acc.unsqueeze(1)).then_inc(kept, 1)

            @block.tensor
            def _(pe):
                pe.sem_inc(multiplied, G)
                with pe.Fori(0, NT) as t:
                    first, end, shift = steps_of(pe, m, t)
                    pe.wait_ge(kept, t + 1)
                    nc.tensor.matmul(acc, m.zeros[:, 0:P], m.zeros[:, 0:WIDE], start=True, stop=False)
                    with pe.Fori(first, end) as s:
                        for g in range(G):
                            pe.wait_ge(weighted, s * G + g + 1 + G)
                            nc.tensor.matmul(acc, hot[:, g], pv[:, g], start=False, stop=False).then_inc(multiplied, 1)
                    nc.tensor.matmul(acc, m.zeros[:, 0:P], m.zeros[:, 0:WIDE], start=False, stop=True).then_inc(summed, 1)

            @block.sync
            def _(sp):
                sp.sem_inc(kept, 1)


def linear_attention(nc, a, m, banks):
    B = 32
    with Stage(nc, "context") as st:
        wk = st.sb("wk", [P, FT, F])
        wv = st.sb("wv", [P, FT, F])
        ek = st.sb("ek", [P, 2, F])
        v = st.sb("v", [P, 2, F])
        top = st.sb("top", [P, FT])
        total = st.sb("total", [P, FT])
        kT = m.big
        loaded, product, copied, shift, exps, own = (st.sem(x) for x in ("loaded", "product", "copied", "shift", "exps", "own"))
        turned, v_made, ek_copied, v_copied, done = (st.sem(x) for x in ("turned", "v_made", "ek_copied", "v_copied", "done"))
        with nc.Block() as block:
            @block.sync
            def _(sp):
                sp.dma_start(wk[:], a["mix_wk"]).then_inc(loaded, 16)
                sp.dma_start(wv[:], a["mix_wv"]).then_inc(loaded, 16)
                sp.wait_ge(loaded, 32)

            @block.tensor
            def _(pe):
                pe.wait_ge(loaded, 32)
                with pe.Fori(0, NC) as i:
                    for c in range(FT):
                        pe.wait_ge(copied, i * FT + c + 1)
                        for f in range(FT):
                            mm = nc.tensor.matmul(banks[c][:, 0:CW], wk[:, f, c * P:(c + 1) * P],
                                                  m.xT[:, f, bass.ds(i * CW, CW)], start=f == 0, stop=f == FT - 1)
                        mm.then_inc(product, 1)
                pe.wait_ge(exps, FT)
                for c in range(FT):
                    nc.tensor.matmul(banks[6 + c][:, 0:P], m.zeros[:, 0:P], m.zeros[:, 0:P], start=True, stop=False)

                def front(t, u):
                    pe.wait_ge(ek_copied, t + 1)
                    for c in range(FT):
                        tr = nc.tensor.transpose(banks[u][:, c * P:(c + 1) * P], kT[:, c, bass.ds(t * P, P)], m.ident[:])
                    tr.then_inc(turned, 1)
                    pe.wait_ge(v_copied, t + 1)
                    for f in range(FT):
                        mm = nc.tensor.matmul(banks[2 + u][:, 0:F], m.xT[:, f, bass.ds(t * P, P)], wv[:, f],
                                              start=f == 0, stop=f == FT - 1)
                    mm.then_inc(v_made, 1)

                def back(t, u):
                    pe.wait_ge(ek_copied, t + 3)
                    pe.wait_ge(v_copied, t + 3)
                    for c in range(FT):
                        mm = nc.tensor.matmul(banks[6 + c][:, 0:P], ek[:, u, c * P:(c + 1) * P], v[:, u, c * P:(c + 1) * P],
                                              start=False, stop=False)
                    mm.then_inc(done, 1)
                front(0, 0)
                for tt in range(NT // 2):
                    front(tt * 2 + 1, 1)
                    back(tt * 2, 0)
                    front(tt * 2 + 2, 0)
                    back(tt * 2 + 1, 1)
                back(NT - 1, 0)
                for c in range(FT):
                    nc.tensor.matmul(banks[6 + c][:, 0:P], m.zeros[:, 0:P], m.zeros[:, 0:P], start=False, stop=True).then_inc(done, 1)

            @block.scalar
            def _(act):
                act.sem_inc(copied, FT)
                with act.Fori(0, NC) as i:
                    for c in range(FT):
                        act.wait_ge(product, i * FT + c + 1)
                        nc.scalar.activation(kT[:, c, bass.ds(i * CW, CW)], banks[c][:, 0:CW], ACT.Copy).then_inc(copied, 1)
                act.wait_ge(shift, FT)
                for c in range(FT):
                    nc.scalar.activation(kT[:, c, 0:N], kT[:, c, 0:N], ACT.Exp, bias=top[:, c:c + 1],
                                         accum_out=total[:, c:c + 1]).then_inc(exps, 1)
                act.sem_inc(ek_copied, 2)
                with act.Fori(0, NT // 2) as half:
                    t = half * 2
                    for u in range(2):
                        act.wait_ge(turned, t + u + 1)
                        act.wait_ge(done, t + u + 1)
                        nc.scalar.activation(ek[:, u], banks[u][:, 0:F], ACT.Copy).then_inc(ek_copied, 1)
                act.wait_ge(turned, NT)
                act.wait_ge(done, NT)
                nc.scalar.activation(ek[:, 0], banks[0][:, 0:F], ACT.Copy).then_inc(ek_copied, 1)

            @block.vector
            def _(dve):
                c_ = Chain(dve, own)
                dve.sem_inc(v_copied, 2)
                dve.sem_inc(done, 2)
                c_(nc.vector.memset(m.context[:], 0.0))
                dve.wait_ge(copied, FT * NC + FT)
                for c in range(FT):
                    nc.vector.tensor_reduce(top[:, c:c + 1], kT[:, c, 0:N], AX.X, ALU.max, negate=True).then_inc(shift, 1)
                with dve.Fori(0, NT // 2) as half:
                    t = half * 2
                    for u in range(2):
                        dve.wait_ge(v_made, t + u + 1)
                        dve.wait_ge(done, t + u + 1)
                        nc.vector.tensor_copy(v[:, u], banks[2 + u][:, 0:F]).then_inc(v_copied, 1)
                dve.wait_ge(v_made, NT)
                dve.wait_ge(done, NT)
                nc.vector.tensor_copy(v[:, 0], banks[2][:, 0:F]).then_inc(v_copied, 1)
                dve.wait_ge(exps, FT)
                c_(nc.vector.reciprocal(total[:], total[:]))
                dve.wait_ge(done, 2 + NT + FT)
                for c in range(FT):
                    for b in range(P // B):
                        at = slice(b * B, (b + 1) * B)
                        nc.vector.tensor_scalar(m.context[at, c, at], banks[6 + c][at, at], total[at, c:c + 1], None, ALU.mult)


def gated_mix(nc, a, m, banks):
    GH = F // 4
    with Stage(nc, "mix") as st:
        wq = st.sb("wq", [P, FT, F])
        wg1 = st.sb("wg1", [P, FT, GH])
        wg2 = st.sb("wg2", [GH, F])
        bg1 = st.sb("bg1", [GH, 1])
        bg2 = st.sb("bg2", [P, FT])
        hT = st.sb("hT", [GH, NP])
        qT = st.sb("qT", [P, FT, CW])
        gate = st.sb("gate", [P, FT, CW])
        loaded, hid, gelu, product, sig, qc, mixed = (st.sem(x) for x in ("loaded", "hid", "gelu", "product", "sig", "qc", "mixed"))
        with nc.Block() as block:
            @block.sync
            def _(sp):
                for to, x in ((wq, "mix_wq"), (wg1, "mix_wg1"), (wg2, "mix_wg2"), (bg1, "mix_bg1"), (bg2, "mix_bg2")):
                    sp.dma_start(to[:], a[x]).then_inc(loaded, 16)
                sp.wait_ge(loaded, 80)

            @block.tensor
            def _(pe):
                pe.wait_ge(loaded, 80)
                with pe.Fori(0, NC // 2) as ii:
                    for u in range(2):
                        pe.wait_ge(gelu, ii * 2 + u + 1)
                        for f in range(FT):
                            mm = nc.tensor.matmul(banks[u][0:GH, 0:CW], wg1[:, f], m.big[:, f, bass.ds((ii * 2 + u) * CW, CW)],
                                                  start=f == 0, stop=f == FT - 1)
                        mm.then_inc(hid, 1)
                with pe.Fori(0, NC) as i:
                    for c in range(FT):
                        pe.wait_ge(qc, i * FT + c + 1)
                        for f in range(FT):
                            mm = nc.tensor.matmul(banks[2 + c][:, 0:CW], wq[:, f, c * P:(c + 1) * P],
                                                  m.xT[:, f, bass.ds(i * CW, CW)], start=f == 0, stop=f == FT - 1)
                        mm.then_inc(product, 1)
                    for c in range(FT):
                        pe.wait_ge(gelu, NC + 2)
                        pe.wait_ge(sig, i * FT + c + 1)
                        nc.tensor.matmul(banks[4 + c][:, 0:CW], wg2[:, c * P:(c + 1) * P], hT[:, bass.ds(i * CW, CW)],
                                         start=True, stop=True).then_inc(product, 1)
                    for c in range(FT):
                        pe.wait_ge(qc, i * FT + c + 1 + FT)
                        pe.wait_ge(mixed, i * FT + c + 1)
                        nc.tensor.matmul(banks[6 + c][:, 0:CW], m.context[:, c], qT[:, c], start=True, stop=True).then_inc(product, 1)

            @block.scalar
            def _(act):
                act.wait_ge(loaded, 80)
                act.sem_inc(gelu, 2)
                act.sem_inc(sig, FT)
                with act.Fori(0, NC // 2) as ii:
                    for u in range(2):
                        act.wait_ge(hid, ii * 2 + u + 1)
                        nc.scalar.activation(hT[:, bass.ds((ii * 2 + u) * CW, CW)], banks[u][0:GH, 0:CW], ACT.Gelu,
                                             bias=bg1[:]).then_inc(gelu, 1)
                with act.Fori(0, NC) as i:
                    for c in range(FT):
                        act.wait_ge(product, i * 6 + 3 + c)
                        act.wait_ge(mixed, i * FT + c + 1)
                        nc.scalar.activation(gate[:, c], banks[4 + c][:, 0:CW], ACT.Sigmoid, bias=bg2[:, c:c + 1]).then_inc(sig, 1)

            @block.vector
            def _(dve):
                dve.sem_inc(qc, FT)
                dve.sem_inc(mixed, FT)
                with dve.Fori(0, NC) as i:
                    for c in range(FT):
                        dve.wait_ge(product, i * 6 + 1 + c)
                        dve.wait_ge(mixed, i * FT + c + 1)
                        nc.vector.tensor_copy(qT[:, c], banks[2 + c][:, 0:CW]).then_inc(qc, 1)
                    for c in range(FT):
                        dve.wait_ge(product, i * 6 + 5 + c)
                        dve.wait_ge(sig, i * FT + c + 1 + FT)
                        nc.vector.tensor_tensor(m.big[:, c, bass.ds(i * CW, CW)], banks[6 + c][:, 0:CW], gate[:, c],
                                                ALU.mult).then_inc(mixed, 1)


def first_update(nc, a, m, banks):
    with Stage(nc, "update") as st:
        names = ("gnn_wskip", "mix_wproj")
        w = st.sb("w", [P, 2, FT, F])
        rows = st.sb("rows", [P, 6, F])
        wgate = st.sb("wgate", [P, 3, F])
        bgate = st.sb("bgate", [P, 1])
        slope = st.sb("slope", [P, 1])
        skip = m.rows
        inv = st.sb("inv", [P, NT, HEADS])
        dots = st.sb("dots", [P, 2, NT])
        g = st.sb("g", [P, NT])
        junk = st.sb("junk", [P, F])
        res = st.sb("res", [P, NT, F])
        neg = m.rows
        stats = st.sb("stats", [P, NT, 6])
        mv = st.sb("mv", [P, NT, 2])
        rstd = st.sb("rstd", [P, NT])
        loaded, skipped, kept, own, z_ready, gate_ready, var_ready, std_ready, projected, added = (
            st.sem(x) for x in ("loaded", "skipped", "kept", "own", "z", "gate", "var", "std", "projected", "added"))
        LOADS = 9

        def row(k):
            return rows[:, k].unsqueeze(1).to_broadcast([P, NT, F])
        with nc.Block() as block:
            @block.sync
            def _(sp):
                for j, x in enumerate(names):
                    sp.dma_start(w[:, j], a[x]).then_inc(loaded, 16)
                for j, x in enumerate(("gnn_bskip", "gnn_ln_w", "gnn_ln_b", "mix_bproj")):
                    sp.dma_start(rows[:, j], a[x]).then_inc(loaded, 16)
                sp.dma_start(wgate[:], a["gnn_wgate"]).then_inc(loaded, 16)
                sp.dma_start(bgate[:], a["gnn_bgate"]).then_inc(loaded, 16)
                sp.dma_start(slope[:], a["gnn_slope"]).then_inc(loaded, 16)
                sp.wait_ge(loaded, 16 * LOADS)

            @block.tensor
            def _(pe):
                pe.wait_ge(loaded, 16 * LOADS)
                for j, (src, sem, free) in enumerate(((m.xT, skipped, kept), (m.big, projected, added))):
                    if j:
                        pe.wait_ge(kept, NT + U)
                    for tt in range(TU):
                        for u in range(U):
                            pe.wait_ge(free, tt * U + u + 1)
                            for f in range(FT):
                                mm = nc.tensor.matmul(banks[u][:, 0:F], src[:, f, bass.ds((tt * U + u) * P, P)], w[:, j, f],
                                                      start=f == 0, stop=f == FT - 1)
                            mm.then_inc(sem, 1)

            @block.scalar
            def _(act):
                act.wait_ge(loaded, 16 * LOADS)
                act.wait_ge(z_ready, 1)
                nc.scalar.activation(g[:], dots[:, 0], ACT.Sigmoid, bias=bgate[:]).then_inc(gate_ready, 1)
                act.wait_ge(var_ready, 1)
                nc.scalar.activation(rstd[:], mv[:, :, 1], ACT.Sqrt).then_inc(std_ready, 1)

            @block.vector
            def _(dve):
                c = Chain(dve, own)
                dve.sem_inc(kept, U)
                dve.sem_inc(added, U)
                dve.wait_ge(loaded, 16 * LOADS)
                c(nc.vector.tensor_tensor(rows[:, 4], wgate[:, 0], wgate[:, 2], ALU.add))
                c(nc.vector.tensor_tensor(rows[:, 5], wgate[:, 1], wgate[:, 2], ALU.subtract))
                with dve.Fori(0, TU) as tt:
                    for u in range(U):
                        dve.wait_ge(skipped, tt * U + u + 1)
                        nc.vector.tensor_tensor(skip[:, bass.ds(tt * U + u, 1), :], banks[u][:, 0:F].unsqueeze(1),
                                                rows[:, 0:1], ALU.add).then_inc(kept, 1)
                c(nc.vector.tensor_scalar(inv[:], m.sums[:, :, F:F + HEADS], 1.0 / BIG, None, ALU.max))
                c(nc.vector.reciprocal(inv[:], inv[:]))
                with dve.Fori(0, NT) as t:
                    r = res[:, bass.ds(t, 1), :].rearrange("p t (h d) -> p (t h) d", h=HEADS)
                    nc.vector.tensor_tensor(r, m.sums[:, bass.ds(t, 1), 0:F].rearrange("p t (h d) -> p (t h) d", h=HEADS),
                                            inv[:, bass.ds(t, 1), :].rearrange("p t h -> p (t h)").unsqueeze(2).to_broadcast([P, HEADS, HD]),
                                            ALU.mult).then_inc(own, 1)
                c.n += NT
                dve.wait_ge(own, c.n)
                dve.wait_ge(kept, NT + U)
                for t in range(NT):
                    for j, part in enumerate((skip, res)):
                        c(nc.vector.tensor_tensor_reduce(out=junk[:], in0=part[:, t], in1=rows[:, 4 + j], scale=1.0, scalar=0.0,
                                                         op0=ALU.mult, op1=ALU.add, accum_out=dots[:, j, t:t + 1]))
                nc.vector.tensor_tensor(dots[:, 0], dots[:, 0], dots[:, 1], ALU.add).then_inc(z_ready, 1)
                c(nc.vector.tensor_tensor(skip[:], skip[:], res[:], ALU.subtract))
                dve.wait_ge(gate_ready, 1)
                with dve.Fori(0, NT) as t:
                    nc.vector.scalar_tensor_tensor(res[:, bass.ds(t, 1), :], skip[:, bass.ds(t, 1), :], g[:, bass.ds(t, 1)],
                                                   res[:, bass.ds(t, 1), :], ALU.mult, ALU.add).then_inc(own, 1)
                c.n += NT
                dve.wait_ge(own, c.n)
                with dve.Fori(0, NT) as t:
                    nc.vector.bn_stats(stats[:, bass.ds(t, 1), :], res[:, bass.ds(t, 1), :]).then_inc(own, 1)
                c.n += NT
                dve.wait_ge(own, c.n)
                mean_and_variance(nc, c, stats, mv, rstd)
                dve.sem_inc(var_ready, 1)
                dve.wait_ge(std_ready, 1)
                c(nc.vector.reciprocal(rstd[:], rstd[:]))
                with dve.Fori(0, NT) as t:
                    nc.vector.tensor_scalar(res[:, bass.ds(t, 1), :], res[:, bass.ds(t, 1), :], mv[:, bass.ds(t, 1), 0],
                                            rstd[:, bass.ds(t, 1)], ALU.subtract, ALU.mult).then_inc(own, 1)
                c.n += NT
                dve.wait_ge(own, c.n)
                c(nc.vector.tensor_tensor(res[:], res[:], row(1), ALU.mult))
                c(nc.vector.tensor_tensor(res[:], res[:], row(2), ALU.add))
                c(nc.vector.tensor_scalar(neg[:], res[:], 0.0, slope[:], ALU.min, ALU.mult))
                c(nc.vector.scalar_tensor_tensor(res[:], res[:], 0.0, neg[:], ALU.max, ALU.add))
                c(nc.vector.tensor_tensor(m.x[:], m.x[:], row(3), ALU.add))
                c(nc.vector.tensor_tensor(m.x[:], m.x[:], res[:], ALU.add))
                with dve.Fori(0, TU) as tt:
                    for u in range(U):
                        dve.wait_ge(projected, tt * U + u + 1)
                        x = m.x[:, bass.ds(tt * U + u, 1), :]
                        nc.vector.tensor_tensor(x, x, banks[u][:, 0:F].unsqueeze(1), ALU.add).then_inc(added, 1)


def softmax_rows(nc, c, act_exp, z, w, top, total):
    c(nc.vector.tensor_reduce(top[:], z[:], AX.X, ALU.max))
    c(nc.vector.tensor_tensor(z[:], z[:], top[:].unsqueeze(2).to_broadcast(list(z.shape)), ALU.subtract))
    act_exp()
    c(nc.vector.tensor_reduce(total[:], w[:], AX.X, ALU.add))
    c(nc.vector.reciprocal(total[:], total[:]))
    c(nc.vector.tensor_tensor(w[:], w[:], total[:].unsqueeze(2).to_broadcast(list(w.shape)), ALU.mult))


def soft_experts(nc, a, m, banks):
    CH = 2 * CW
    with Stage(nc, "soft") as st:
        wr = st.sb("wr", [P, FT, XQ])
        br = st.sb("br", [P, XQ])
        bo = st.sb("bo", [XQ, F])
        z = st.sb("z", [P, NT, XQ])
        w = st.sb("w", [P, NT, XQ])
        top = st.sb("top", [P, NT])
        total = st.sb("total", [P, NT])
        wT = st.sb("wT", [XQ, NP])
        raw = st.sb("raw", [P, 2, 5, XQ * FT])
        sc = st.sb("sc", [P, 2, XQ, FT])
        bi = st.sb("bi", [P, 2, XQ, FT])
        W = st.sb("W", [P, 2, 3, FT, F])
        h1 = st.sb("h1", [P, FT, CH])
        h2 = st.sb("h2", [P, FT, CH])
        loaded, own, logits, zs, exps, std, scales, wts, turned, wcopy = (
            st.sem(x) for x in ("loaded", "own", "logits", "zs", "exps", "std", "scales", "wts", "turned", "wcopy"))
        hid, relu, outs, summed, biased, w_used = (st.sem(x) for x in ("hid", "relu", "outs", "summed", "biased", "w_used"))
        begun, begun_act = st.sem("begun"), st.sem("begun_act")
        wload = [st.sem(f"wload{j}") for j in range(2)]
        HSLOTS = 2
        with nc.Block() as block:
            @block.sync
            def _(sp):
                sp.dma_start(wr[:], a["ffn_wr"]).then_inc(loaded, 16)
                sp.dma_start(br[:], a["ffn_br"]).then_inc(loaded, 16)
                sp.dma_start(bo[:], a["ffn_bo"]).then_inc(loaded, 16)
                for j in range(2):
                    sp.dma_start(raw[:, j], a[f"ffn_bn{j + 1}"]).then_inc(loaded, 16)
                sp.wait_ge(loaded, 80)
                with sp.Fori(0, XQ // 2) as ee:
                    for j in range(2):
                        sp.wait_ge(w_used, ee * 2 + j + 1)
                        for k, x in enumerate(("ffn_w1", "ffn_w2", "ffn_wo")):
                            sp.dma_start(W[:, j, k], a[x][bass.ds(ee * 2 + j, 1)].rearrange("e p f n -> p (e f) n")).then_inc(wload[j], 16)

            @block.gpsimd
            def _(pool):
                pool.sem_inc(w_used, 2)

            @block.tensor
            def _(pe):
                pe.wait_ge(loaded, 80)
                for t in range(NT):
                    for f in range(FT):
                        mm = nc.tensor.matmul(banks[0][:, t * XQ:(t + 1) * XQ], m.xT[:, f, t * P:(t + 1) * P], wr[:, f],
                                              start=f == 0, stop=f == FT - 1)
                mm.then_inc(logits, 1)
                pe.wait_ge(wts, 1)
                for tt in range(TU):
                    for u in range(U):
                        pe.wait_ge(wcopy, tt * U + u + 1)
                        nc.tensor.matmul(banks[4 + u % 2][0:XQ, 0:P], w[:, bass.ds(tt * U + u, 1), :].rearrange("p t e -> p (t e)"),
                                         m.ident[:], start=True, stop=True).then_inc(turned, 1)
                        pe.wait_ge(wcopy, tt * U + u + 3)
                        pe.wait_ge(biased, tt * U + u + 2)
                        nc.tensor.matmul(banks[6 + u % 2][:, 0:F], wT[:, bass.ds((tt * U + u) * P, P)], bo[:],
                                         start=True, stop=True).then_inc(turned, 1)
                pe.wait_ge(biased, NT + 2)
                with pe.Fori(0, XQ // 2) as ee:
                    for j in range(2):
                        pe.wait_ge(wload[j], ee * 48 + 48)
                        pe.sem_inc(begun, 1)
                        with pe.Fori(0, TU) as ch:
                            n = (ee * 2 + j) * TU + ch
                            for layer, (src, dst) in enumerate(((m.xT, h1), (h1, h2))):
                                for hf in range(2):
                                    for c in range(FT):
                                        k = layer * 4 + hf * 2 + c
                                        pe.wait_ge(relu, n * 8 + k + 1)
                                        if layer:
                                            pe.wait_ge(relu, n * 8 + HSLOTS + hf * 2 + 2)
                                        for f in range(FT):
                                            cols = m.xT[:, f, bass.ds(ch * CH + hf * CW, CW)] if layer == 0 else h1[:, f, hf * CW:(hf + 1) * CW]
                                            mm = nc.tensor.matmul(banks[k % HSLOTS][:, 0:CW], W[:, j, layer, f, c * P:(c + 1) * P], cols,
                                                                  start=f == 0, stop=f == FT - 1)
                                        mm.then_inc(hid, 1)
                            for u in range(U):
                                pe.wait_ge(relu, n * 8 + HSLOTS + (6 if u < 2 else 8))
                                pe.wait_ge(summed, n * U + u + 1)
                                for f in range(FT):
                                    mm = nc.tensor.matmul(banks[HSLOTS + u][:, 0:F], h2[:, f, u * P:(u + 1) * P], W[:, j, 2, f],
                                                          start=f == 0, stop=f == FT - 1)
                                mm.then_inc(outs, 1)
                        pe.wait_ge(outs, (ee * 2 + j) * (TU * U) + TU * U)
                        pe.sem_inc(w_used, 1)

            @block.scalar
            def _(act):
                act.sem_inc(relu, HSLOTS)
                act.wait_ge(std, 1)
                nc.scalar.activation(sc[:], sc[:], ACT.Sqrt).then_inc(std, 1)
                act.wait_ge(zs, 1)
                nc.scalar.activation(w[:], z[:], ACT.Exp).then_inc(exps, 1)
                act.sem_inc(wcopy, 2)
                with act.Fori(0, TU) as tt:
                    for u in range(U):
                        act.wait_ge(turned, tt * (2 * U) + 2 * u + 1)
                        nc.scalar.activation(wT[:, bass.ds((tt * U + u) * P, P)], banks[4 + u % 2][0:XQ, 0:P], ACT.Copy).then_inc(wcopy, 1)
                act.wait_ge(scales, 1)
                with act.Fori(0, XQ) as e:
                    with act.Fori(0, TU) as ch:
                        n = e * TU + ch
                        for layer, dst in enumerate((h1, h2)):
                            for hf in range(2):
                                for c in range(FT):
                                    k = layer * 4 + hf * 2 + c
                                    act.wait_ge(hid, n * 8 + k + 1)
                                    act.sem_inc(begun_act, 1)
                                    nc.scalar.activation(dst[:, c, hf * CW:(hf + 1) * CW], banks[k % HSLOTS][:, 0:CW], ACT.Relu,
                                                         scale=sc[:, layer, bass.ds(e, 1), c], bias=bi[:, layer, bass.ds(e, 1), c]).then_inc(relu, 1)

            @block.vector
            def _(dve):
                c = Chain(dve, own)
                dve.sem_inc(summed, U)
                dve.sem_inc(biased, 2)
                dve.wait_ge(loaded, 80)
                scv, biv = (x[:].rearrange("p l e c -> p l (e c)") for x in (sc, bi))
                nc.vector.tensor_scalar(scv, raw[:, :, 4], BN_EPS, None, ALU.add).then_inc(std, 1)
                dve.wait_ge(std, 2)
                c(nc.vector.reciprocal(scv, scv))
                c(nc.vector.tensor_tensor(scv, scv, raw[:, :, 1], ALU.mult))
                c(nc.vector.tensor_tensor(biv, raw[:, :, 0], raw[:, :, 3], ALU.subtract))
                c(nc.vector.tensor_tensor(biv, biv, scv, ALU.mult))
                nc.vector.tensor_tensor(biv, biv, raw[:, :, 2], ALU.add).then_inc(scales, 1)
                dve.wait_ge(logits, 1)
                c(nc.vector.tensor_tensor(z[:], banks[0][:, 0:NT * XQ].rearrange("p (t e) -> p t e", e=XQ),
                                          br[:].unsqueeze(1).to_broadcast([P, NT, XQ]), ALU.add))

                def act_exp():
                    dve.sem_inc(zs, 1)
                    dve.wait_ge(exps, 1)
                softmax_rows(nc, c, act_exp, z, w, top, total)
                dve.sem_inc(wts, 1)
                with dve.Fori(0, TU) as tt:
                    for u in range(U):
                        dve.wait_ge(turned, tt * (2 * U) + 2 * u + 2)
                        x = m.x[:, bass.ds(tt * U + u, 1), :]
                        nc.vector.tensor_tensor(x, x, banks[6 + u % 2][:, 0:F].unsqueeze(1), ALU.add).then_inc(biased, 1)
                with dve.Fori(0, XQ) as e:
                    with dve.Fori(0, TU) as ch:
                        n = e * TU + ch
                        for u in range(U):
                            dve.wait_ge(outs, n * U + u + 1)
                            x = m.x[:, bass.ds(ch * U + u, 1), :]
                            nc.vector.scalar_tensor_tensor(x, banks[HSLOTS + u][:, 0:F].unsqueeze(1), w[:, bass.ds(ch * U + u, 1), bass.ds(e, 1)].rearrange("p t e -> p (t e)"),
                                                           x, ALU.mult, ALU.add).then_inc(summed, 1)


def edge_convolution(nc, a, m, banks):
    with Stage(nc, "conv") as st:
        w = st.sb("w", [P, EC, F])
        b = st.sb("b", [P, F])
        ix = st.sb("ix", [P, G], I32)
        eT = st.sb("eT", [P, G, EC, P])
        h = st.sb("h", [P, G, F])
        be = st.sb("be", [P, 2, F])
        msg = st.sb("msg", [P, G, F])
        hot = st.sb("hot", [P, G, P])
        loaded, index, made, ready, multiplied, summed, kept, own = (
            st.sem(x) for x in ("w", "index", "made", "ready", "multiplied", "summed", "kept", "own"))
        gathers = st.sem("gathers")
        gathered = [st.gather_sem(f"gathered{g}") for g in range(G)]
        arrived = [st.sem(f"arrived{g}") for g in range(G)]
        acc = banks[0][:, 0:F]

        def edge_bank(g):
            return banks[1 + g][:, 0:F]
        with nc.Block() as block:
            @block.sync
            def _(sp):
                sp.dma_start(w[:], a["gnn1_wedge"]).then_inc(loaded, 16)
                sp.dma_start(b[:], a["gnn1_bedge"]).then_inc(loaded, 16)
                sp.wait_ge(loaded, 32)
                with sp.Fori(0, NT) as t:
                    first, end, shift = steps_of(sp, m, t)
                    with sp.Fori(first, end) as s:
                        i = group_of(sp, s, shift)
                        for g in range(G):
                            sp.wait_ge(made, s * G + g + 1)
                            sp.dma_start(eT[:, g], a["edges"][bass.ds(i * G + g, 1)].rearrange("t p c e -> p (t c) e")).then_inc(arrived[g], 16)

            @block.scalar
            def _(act):
                act.sem_inc(kept, 1)
                with act.Fori(0, NT) as t:
                    first, end, shift = steps_of(act, m, t)
                    with act.Fori(first, end) as s:
                        i = group_of(act, s, shift)
                        for g in range(G):
                            act.wait_ge(ready, s * G + g + 1)
                            nc.scalar.activation(ix[:, g:g + 1], m.src[:, bass.ds(i * G + g, 1)], ACT.Copy).then_inc(index, 1)

            @block.gpsimd
            def _(pool):
                with pool.Fori(0, NT) as t:
                    first, end, shift = steps_of(pool, m, t)
                    with pool.Fori(first, end) as s:
                        for g in range(G):
                            pool.wait_ge(index, s * G + g + 1)
                            pool.wait_ge(ready, s * G + g + 1)
                            pool.sem_inc(gathers, 1)
                            nc.gpsimd.indirect_dma_start(
                                out=h[:, g, :], out_offset=None, in_=m.d_h,
                                in_offset=bass.IndirectOffsetOnAxis(ap=ix[:, g:g + 1], axis=0)
                            ).then_inc(gathered[g], 16)

            @block.vector
            def _(dve):
                dve.sem_inc(ready, G)
                dve.wait_ge(loaded, 32)
                with dve.Fori(0, NT) as t:
                    first, end, shift = steps_of(dve, m, t)
                    with dve.Fori(first, end) as s:
                        i = group_of(dve, s, shift)
                        for g in range(G):
                            dve.wait_ge(made, s * G + g + 1 + G)
                            nc.vector.tensor_tensor(be[:, g % 2], edge_bank(g), b[:], ALU.add).then_inc(own, 1)
                            dve.wait_ge(multiplied, s * G + g + 1)
                            nc.vector.tensor_scalar(hot[:, g], m.node_no[:, bass.ds(t * P, P)],
                                                    m.dst[:, bass.ds(i * G + g, 1)], None, ALU.is_equal)
                            dve.wait_ge(own, s * G + g + 1)
                            dve.wait_ge(gathered[g], (s + 1) * 16)
                            nc.vector.tensor_tensor(msg[:, g], be[:, g % 2], h[:, g], ALU.mult).then_inc(ready, 1)
                    dve.wait_ge(summed, t + 1)
                    nc.vector.tensor_copy(m.sums[:, bass.ds(t, 1), 0:F], acc.unsqueeze(1)).then_inc(kept, 1)

            @block.tensor
            def _(pe):
                pe.sem_inc(made, G)
                pe.sem_inc(multiplied, G)
                pe.wait_ge(loaded, 32)
                with pe.Fori(0, NT) as t:
                    first, end, shift = steps_of(pe, m, t)
                    pe.wait_ge(kept, t + 1)
                    nc.tensor.matmul(acc, m.zeros[:, 0:P], m.zeros[:, 0:F], start=True, stop=False)
                    with pe.Fori(first, end) as s:
                        def project(g):
                            pe.wait_ge(arrived[g], (s + 1) * 16)
                            pe.wait_ge(ready, s * G + g + 1)
                            for c in range(EC):
                                mm = nc.tensor.matmul(edge_bank(g), eT[:, g, c], w[:, c], start=c == 0, stop=c == EC - 1)
                            mm.then_inc(made, 1)

                        def add_up(g):
                            pe.wait_ge(ready, s * G + g + 1 + G)
                            nc.tensor.matmul(acc, hot[:, g], msg[:, g], start=False, stop=False).then_inc(multiplied, 1)
                        project(0)
                        for g in range(1, G):
                            project(g)
                            add_up(g - 1)
                        add_up(G - 1)
                    nc.tensor.matmul(acc, m.zeros[:, 0:P], m.zeros[:, 0:F], start=False, stop=True).then_inc(summed, 1)


KS = 7


def spline_layer(nc, a, m, banks):
    with Stage(nc, "spline") as st:
        wb = st.sb("wb", [P, FT, F])
        ws = st.sb("ws", [P, FT, KS, F])
        scaler = st.sb("scaler", [P, FT, F])
        knot = st.sb("knot", [P, KS + 2])
        sT = st.sb("sT", [P, 2, FT * P])
        base = st.sb("base", [P, 2, FT, P])
        near = st.sb("near", [P, 2, KS, FT * P])
        wide = st.sb("wide", [P, 2, KS, FT * P])
        spl = st.sb("spl", [P, 2, KS, FT * P])
        loaded, turned, copied, own, own_act, parts, bases, made, added, knots = (
            st.sem(x) for x in ("loaded", "turned", "copied", "own", "own_act", "parts", "bases", "made", "added", "knots"))

        def staggered(eng, front, back, unroll=False):
            def pair(t):
                front(t + 1, 1)
                back(t, 0)
                front(t + 2, 0)
                back(t + 1, 1)
            front(0, 0)
            if unroll:
                for t in range(0, NT - 1, 2):
                    pair(t)
            else:
                with eng.Fori(0, NT // 2) as half:
                    t = half * 2
                    pair(t)
            back(NT - 1, 0)
        with nc.Block() as block:
            @block.sync
            def _(sp):
                for to, x in ((wb, "base_w"), (ws, "spline_w"), (scaler, "spline_scaler")):
                    sp.dma_start(to[:], a[x]).then_inc(loaded, 16)
                sp.wait_ge(loaded, 48)

            @block.tensor
            def _(pe):
                pe.wait_ge(loaded, 48)
                pe.sem_inc(made, 2)

                def turn(t, u):
                    pe.wait_ge(copied, t + 1)
                    for f in range(FT):
                        tr = nc.tensor.transpose(banks[0][:, f * P:(f + 1) * P], m.sums[:, bass.ds(t, 1), f * P:(f + 1) * P], m.ident[:])
                    tr.then_inc(turned, 1)

                def products(t, u):
                    pe.wait_ge(bases, t + 3)
                    pe.wait_ge(added, t + 1)
                    for f in range(FT):
                        nc.tensor.matmul(banks[2 + u][:, 0:F], base[:, u, f], wb[:, f], start=f == 0, stop=False)
                    for f in range(FT):
                        for k in range(KS):
                            mm = nc.tensor.matmul(banks[2 + u][:, 0:F], spl[:, u, k, f * P:(f + 1) * P], ws[:, f, k],
                                                  start=False, stop=f == FT - 1 and k == KS - 1)
                    mm.then_inc(made, 1)
                staggered(pe, turn, products, unroll=True)

            @block.scalar
            def _(act):
                act.sem_inc(copied, 1)
                act.wait_ge(knots, 1)

                def body(t, u):
                    act.wait_ge(turned, t + 1)
                    act.wait_ge(made, t + 1)
                    nc.scalar.activation(sT[:, u], banks[0][:, 0:FT * P], ACT.Copy).then_inc(copied, 1)
                    act.wait_ge(copied, t + 2)
                    nc.scalar.activation(base[:, u].rearrange("p f n -> p (f n)"), sT[:, u], ACT.Silu)
                    for k in range(KS):
                        nc.scalar.activation(near[:, u, k], sT[:, u], ACT.Abs, scale=2.0, bias=knot[:, k:k + 1]).then_inc(own_act, 1)
                    act.wait_ge(own_act, t * 8 + 7)
                    nc.scalar.activation(wide[:, u], near[:, u], ACT.Relu, scale=-1.0, bias=knot[:, KS:KS + 1]).then_inc(own_act, 1)
                    act.wait_ge(own_act, t * 8 + 8)
                    nc.scalar.activation(spl[:, u], wide[:, u], ACT.Square)
                    nc.scalar.activation(near[:, u], near[:, u], ACT.Relu, scale=-1.0, bias=knot[:, KS + 1:KS + 2]).then_inc(parts, 1)
                with act.Fori(0, NT // 2) as half:
                    t = half * 2
                    body(t, 0)
                    body(t + 1, 1)
                body(NT - 1, 0)

            @block.vector
            def _(dve):
                c = Chain(dve, own)
                for k in range(KS):
                    c(nc.vector.memset(knot[:, k:k + 1], 3.0 - k))
                for k in range(2):
                    c(nc.vector.memset(knot[:, KS + k:KS + k + 1], 2.0 - k))
                dve.sem_inc(knots, 1)
                dve.sem_inc(added, 2)
                dve.sem_inc(bases, 2)
                dve.wait_ge(loaded, 48)
                c(nc.vector.tensor_scalar(scaler[:], scaler[:], 1.0 / 6.0, None, ALU.mult))
                for f in range(FT):
                    c(nc.vector.tensor_tensor(ws[:, f], ws[:, f], scaler[:, f].unsqueeze(1).to_broadcast([P, KS, F]), ALU.mult))
                done = c.n

                def compute(t, u):
                    dve.wait_ge(parts, t + 1)
                    nc.vector.tensor_tensor(spl[:, u], spl[:, u], wide[:, u], ALU.mult).then_inc(own, 1)
                    dve.wait_ge(own, t * 3 + done + 1)
                    nc.vector.tensor_tensor(wide[:, u], near[:, u], near[:, u], ALU.mult).then_inc(own, 1)
                    dve.wait_ge(own, t * 3 + done + 2)
                    nc.vector.scalar_tensor_tensor(wide[:, u], wide[:, u], -4.0, near[:, u], ALU.mult, ALU.mult).then_inc(own, 1)
                    dve.wait_ge(own, t * 3 + done + 3)
                    nc.vector.tensor_tensor(spl[:, u], spl[:, u], wide[:, u], ALU.add).then_inc(bases, 1)

                def add(t, u):
                    dve.wait_ge(made, t + 3)
                    x = m.x[:, bass.ds(t, 1), :]
                    nc.vector.tensor_tensor(x, x, banks[2 + u][:, 0:F].unsqueeze(1), ALU.add).then_inc(added, 1)
                staggered(dve, compute, add)


def ball_attention(nc, a, m, banks):
    WC = 2 * MC
    OC = MG * 32
    OT = OC // P
    TAIL = N - (NC - 1) * CW
    with Stage(nc, "ball") as st:
        w = st.sb("w", [P, FT, MC])
        gb = st.sb("gb", [P, 2, MT])
        wdw = st.sb("wdw", [P, MT])
        mix = st.sb("mix", [P, MT, 2, P])
        wres = st.sb("wres", [P, OT, F])
        bres = st.sb("bres", [P, F])
        norm = st.sb("norm", [P, NT])
        f1 = st.sb("f1", [P, NT])
        f2 = st.sb("f2", [P, NT])
        small = st.sb("small", [P, NT])
        junk = st.sb("junk", [P, 2, 3, 512])
        junk2 = st.sb("junk2", [P, 512])
        stats = st.sb("stats", [P, MT, NC, 6])
        mv = st.sb("mv", [P, MT, 2])
        sc = st.sb("sc", [P, MT])
        bi = st.sb("bi", [P, MT])
        rT = st.sb("rT", [P, 2, MT, P])
        sq = st.sb("sq", [P, 2, 4])
        z = st.sb("z", [P, 2, WC])
        zq = st.sb("zq", [P, OC])
        ksum = st.sb("ksum", [P, MG])
        out = st.sb("out", [P, NT, OC])
        oT = st.sb("oT", [P, 2, OC])
        loaded, own, own_act = st.sem("loaded"), st.sem("own"), st.sem("own_act")
        (sq_done, root_in, root, lns, ln, scaled, turned, tcopied, h_made, h_seen, var_in, var_out, tables,
         pre, relued, wide_made, wide_sq, fin, fout, wide_out, z_ready, o_ready) = (
            st.sem(x) for x in ("sq", "root_in", "root", "lns", "ln", "scaled", "turned", "tcopied", "h_made", "h_seen",
                                "var_in", "var_out", "tables", "pre", "relued", "wide_made", "wide_sq", "fin", "fout",
                                "wide_out", "z_ready", "o_ready"))
        nsq, nroot, orot, ocopy, resed, ftd, tanh = (st.sem(x) for x in ("nsq", "nroot", "orot", "ocopy", "resed", "ftd", "tanh"))
        with nc.Block() as block:
            @block.sync
            def _(sp):
                for to, x in ((w[:], "ball_w"), (gb[:], "ball_bn"), (wdw[:], "ball_wdw"), (mix[:, :, 1], "ball_wpw"),
                              (wres[:], "ball_wres"), (bres[:], "ball_bres")):
                    sp.dma_start(to, a[x]).then_inc(loaded, 16)
                sp.wait_ge(loaded, 16 * 6)

            @block.scalar
            def _(act):
                with act.Fori(0, NT) as t:
                    nc.scalar.activation(out[:, bass.ds(t, 1), 0:F].rearrange("p t f -> p (t f)"),
                                         m.rows[:, bass.ds(t, 1), :].rearrange("p t f -> p (t f)"), ACT.Square,
                                         accum_out=norm[:, bass.ds(t, 1)]).then_inc(sq_done, 1)
                act.wait_ge(sq_done, NT)
                nc.scalar.activation(norm[:], norm[:], ACT.Sqrt).then_inc(root, 1)
                act.wait_ge(lns, 1)
                nc.scalar.activation(f1[:], f1[:], ACT.Ln).then_inc(ln, 1)
                act.sem_inc(tcopied, 4)
                with act.Fori(0, TU) as tt:
                    for u in range(U):
                        act.wait_ge(turned, tt * U + u + 1)
                        nc.scalar.activation(m.xT[:, :, bass.ds((tt * U + u) * P, P)],
                                             banks[u][:, 0:F].rearrange("p (f n) -> p f n", f=FT), ACT.Copy).then_inc(tcopied, 1)
                act.wait_ge(var_in, 1)
                nc.scalar.activation(sc[:], sc[:], ACT.Sqrt).then_inc(var_out, 1)
                act.wait_ge(tables, 1)
                act.sem_inc(relued, 2)

                def body(t, u):
                    act.wait_ge(pre, t + 1)
                    act.wait_ge(wide_made, t + 1)
                    for k in range(MT):
                        b, o = divmod(k * P, 512)
                        ins = nc.scalar.activation(rT[:, u, k], banks[b][:, o:o + P], ACT.Relu, scale=sc[:, k:k + 1], bias=bi[:, k:k + 1])
                    ins.then_inc(relued, 1)
                    act.wait_ge(wide_made, t + 3)
                    for b in range(3):
                        ins = nc.scalar.activation(junk[:, u, b], banks[2 + b][:, :], ACT.Square, accum_out=sq[:, u, b:b + 1])
                    ins.then_inc(wide_sq, 1)
                    act.wait_ge(fin, t + 1)
                    nc.scalar.activation(sq[:, u, 3:4], sq[:, u, 3:4], ACT.Sqrt).then_inc(fout, 1)
                with act.Fori(0, NT // 2) as half:
                    t = half * 2
                    body(t, 0)
                    body(t + 1, 1)
                body(NT - 1, 0)
                act.wait_ge(o_ready, NT)
                act.sem_inc(nsq, 1)
                with act.Fori(0, NT) as t:
                    act.wait_ge(nsq, t + 1)
                    nc.scalar.activation(junk[:, 0, 0], out[:, bass.ds(t, 1), :].rearrange("p t c -> p (t c)"), ACT.Square,
                                         accum_out=norm[:, bass.ds(t, 1)]).then_inc(nsq, 1)
                act.wait_ge(nsq, NT + 1)
                nc.scalar.activation(norm[:], norm[:], ACT.Sqrt).then_inc(nroot, 1)
                act.sem_inc(ocopy, 2)

                def turn_copy(t, u):
                    act.wait_ge(orot, t + 1)
                    act.wait_ge(resed, t + 1)
                    nc.scalar.activation(oT[:, u], banks[u][:, :], ACT.Copy).then_inc(ocopy, 1)
                with act.Fori(0, NT // 2) as half:
                    t = half * 2
                    turn_copy(t, 0)
                    turn_copy(t + 1, 1)
                turn_copy(NT - 1, 0)
                act.wait_ge(ftd, 2 + NT)
                with act.Fori(0, NT) as t:
                    nc.scalar.activation(out[:, bass.ds(t, 1), 0:F].rearrange("p t f -> p (t f)"),
                                         m.rows[:, bass.ds(t, 1), :].rearrange("p t f -> p (t f)"), ACT.Square,
                                         accum_out=f1[:, bass.ds(t, 1)]).then_inc(own_act, 1)
                act.wait_ge(own_act, NT)
                nc.scalar.activation(f1[:], f1[:], ACT.Sqrt).then_inc(tanh, 1)
                act.wait_ge(tanh, 2)
                nc.scalar.activation(f2[:], f1[:], ACT.Tanh).then_inc(tanh, 1)

            @block.vector
            def _(dve):
                c = Chain(dve, own)
                dve.wait_ge(root, 1)
                c(nc.vector.tensor_scalar(f2[:], norm[:], MAX_NORM, None, ALU.min))
                c(nc.vector.tensor_scalar(f1[:], f2[:], -1.0, 1.0, ALU.mult, ALU.add))
                c(nc.vector.reciprocal(f1[:], f1[:]))
                c(nc.vector.scalar_tensor_tensor(f1[:], f2[:], 1.0, f1[:], ALU.add, ALU.mult))
                dve.sem_inc(lns, 1)
                c(nc.vector.tensor_scalar(norm[:], norm[:], MIN_NORM, None, ALU.max))
                c(nc.vector.reciprocal(norm[:], norm[:]))
                c(nc.vector.tensor_tensor(small[:], f2[:], f2[:], ALU.mult))
                c(nc.vector.tensor_scalar(junk2[:, 0:NT], small[:], 0.2, 1.0 / 3.0, ALU.mult, ALU.add))
                c(nc.vector.tensor_tensor(small[:], small[:], junk2[:, 0:NT], ALU.mult))
                c(nc.vector.tensor_scalar(small[:], small[:], 1.0, None, ALU.add))
                c(nc.vector.tensor_scalar(f2[:], f2[:], 0.05, None, ALU.is_lt))
                dve.wait_ge(ln, 1)
                c(nc.vector.scalar_tensor_tensor(f1[:], f1[:], 0.5, norm[:], ALU.mult, ALU.mult))
                c(nc.vector.tensor_tensor(small[:], small[:], f1[:], ALU.subtract))
                c(nc.vector.tensor_tensor(small[:], small[:], f2[:], ALU.mult))
                c(nc.vector.tensor_tensor(f1[:], f1[:], small[:], ALU.add))
                with dve.Fori(0, NT) as t:
                    nc.vector.tensor_scalar(m.rows[:, bass.ds(t, 1), :], m.rows[:, bass.ds(t, 1), :], f1[:, bass.ds(t, 1)], None,
                                            ALU.mult).then_inc(scaled, 1)
                dve.sem_inc(h_seen, 2)
                dve.wait_ge(loaded, 96)
                for k in range(MT):
                    c(nc.vector.tensor_copy(mix[:, k, 0], m.ident[:]))
                    c(nc.vector.tensor_scalar(mix[:, k, 1], mix[:, k, 1], wdw[:, k:k + 1], None, ALU.mult))
                for k in range(MT):
                    with dve.Fori(0, NC // 2) as ii:
                        for u in range(2):
                            dve.wait_ge(h_made, ii * 2 + u + 1 + k * NC)
                            nc.vector.bn_stats(stats[:, k, bass.ds(ii * 2 + u, 1), :], banks[6 + u][:, 0:CW].unsqueeze(1)).then_inc(h_seen, 1)
                    dve.wait_ge(h_seen, 2 + (k + 1) * NC + k)
                    nc.vector.bn_stats(stats[:, k, NC - 1, :], banks[7][:, 0:TAIL]).then_inc(h_seen, 1)
                dve.wait_ge(h_seen, 2 + MT * (NC + 1))
                for k in range(MT):
                    c(nc.vector.bn_aggr(mv[:, k], stats[:, k].rearrange("p i s -> p (i s)")))
                nc.vector.tensor_scalar(sc[:], mv[:, :, 1], 1e-5, None, ALU.add).then_inc(var_in, 1)
                dve.wait_ge(var_out, 1)
                c(nc.vector.reciprocal(sc[:], sc[:]))
                c(nc.vector.tensor_tensor(sc[:], sc[:], gb[:, 0], ALU.mult))
                c(nc.vector.tensor_tensor(bi[:], mv[:, :, 0], sc[:], ALU.mult))
                c(nc.vector.tensor_tensor(bi[:], gb[:, 1], bi[:], ALU.subtract))
                dve.sem_inc(tables, 1)
                dve.sem_inc(z_ready, 1)
                start = c.n

                def body(t, u):
                    k = start

                    def dep(ins):
                        nonlocal k
                        k += 1
                        ins.then_inc(own, 1)
                        dve.wait_ge(own, t * PER + k)
                    dve.wait_ge(wide_sq, t + 1)
                    dep(nc.vector.tensor_reduce(sq[:, u, 3:4], sq[:, u, 0:3], AX.X, ALU.add))
                    dve.sem_inc(fin, 1)
                    dve.wait_ge(fout, t + 1)
                    dep(nc.vector.tensor_scalar(sq[:, u, 3:4], sq[:, u, 3:4], MIN_NORM, None, ALU.max))
                    dep(nc.vector.reciprocal(sq[:, u, 3:4], sq[:, u, 3:4]))
                    dep(nc.vector.tensor_scalar(sq[:, u, 3:4], sq[:, u, 3:4], REACH, 1.0, ALU.mult, ALU.min))
                    for b in range(3):
                        to = z[:, u].rearrange("p (h k n) -> p h k n", h=2, k=MT)[:, :, 2 * b:2 * b + 2]
                        ins = nc.vector.tensor_scalar(to, banks[2 + b][:, :].rearrange("p (k h n) -> p h k n", k=2, h=2),
                                                      sq[:, u, 3:4], None, ALU.mult)
                        if b == 2:
                            nc_ins = ins
                    nc_ins.then_inc(z_ready, 1)
                    dve.wait_ge(z_ready, t + 2)
                    g = z[:, u].rearrange("p (g x) -> p g x", g=MG)
                    qv, kv, vv = (g[:, :, j * 32:(j + 1) * 32] for j in range(3))
                    zz = zq[:].rearrange("p (g x) -> p g x", g=MG)
                    dep(nc.vector.tensor_scalar(zz, kv, 0.0, None, ALU.max))
                    dep(nc.vector.tensor_reduce(ksum[:], zz, AX.X, ALU.add))
                    dep(nc.vector.tensor_scalar(zz, vv, MIN_NORM, None, ALU.add))
                    dep(nc.vector.reciprocal(zz, zz))
                    dep(nc.vector.scalar_tensor_tensor(qv, qv, 0.0, ksum[:].unsqueeze(2).to_broadcast([P, MG, 32]), ALU.max, ALU.mult))
                    dep(nc.vector.tensor_tensor(qv, qv, vv, ALU.mult))
                    nc.vector.tensor_tensor(out[:, bass.ds(t, 1), :].rearrange("p t (g x) -> p (t g) x", g=MG), qv, zz, ALU.mult).then_inc(o_ready, 1)
                    assert k - start == PER
                PER = 10
                with dve.Fori(0, NT // 2) as half:
                    t = half * 2
                    body(t, 0)
                    body(t + 1, 1)
                body(NT - 1, 0)
                c.n = start + PER * NT
                dve.wait_ge(nroot, 1)
                c(nc.vector.tensor_scalar(norm[:], norm[:], MIN_NORM, None, ALU.max))
                c(nc.vector.reciprocal(norm[:], norm[:]))
                c(nc.vector.tensor_scalar(norm[:], norm[:], REACH, 1.0, ALU.mult, ALU.min))
                dve.sem_inc(ftd, 2)

                def residual(t, u):
                    dve.wait_ge(resed, t + 3)
                    nc.vector.scalar_tensor_tensor(m.rows[:, bass.ds(t, 1), :], banks[2 + u][:, 0:F].unsqueeze(1), norm[:, bass.ds(t, 1)],
                                                   bres[:].unsqueeze(1), ALU.mult, ALU.add).then_inc(ftd, 1)
                with dve.Fori(0, NT // 2) as half:
                    t = half * 2
                    residual(t, 0)
                    residual(t + 1, 1)
                residual(NT - 1, 0)
                dve.wait_ge(tanh, 1)
                c(nc.vector.tensor_scalar(f1[:], f1[:], MIN_NORM, None, ALU.max))
                dve.sem_inc(tanh, 1)
                dve.wait_ge(tanh, 3)
                c(nc.vector.reciprocal(f1[:], f1[:]))
                c(nc.vector.scalar_tensor_tensor(f1[:], f2[:], MAX_NORM, f1[:], ALU.min, ALU.mult))
                with dve.Fori(0, NT) as t:
                    x = m.x[:, bass.ds(t, 1), :]
                    nc.vector.scalar_tensor_tensor(x, m.rows[:, bass.ds(t, 1), :], f1[:, bass.ds(t, 1)], x, ALU.mult, ALU.add)

            @block.tensor
            def _(pe):
                pe.wait_ge(loaded, 96)
                pe.sem_inc(tcopied, 1)
                for tt in range(TU):
                    for u in range(U):
                        pe.wait_ge(scaled, tt * U + u + 1)
                        pe.wait_ge(tcopied, tt * U + u + 1)
                        for f in range(FT):
                            tr = nc.tensor.transpose(banks[u][:, f * P:(f + 1) * P], m.rows[:, bass.ds(tt * U + u, 1), f * P:(f + 1) * P], m.ident[:])
                        tr.then_inc(turned, 1)
                pe.wait_ge(tcopied, NT + 5)
                for k in range(MT):
                    with pe.Fori(0, NC // 2) as ii:
                        for u in range(2):
                            pe.wait_ge(h_seen, ii * 2 + u + 1 + k * (NC + 1))
                            for f in range(FT):
                                mm = nc.tensor.matmul(banks[6 + u][:, 0:CW], w[:, f, k * P:(k + 1) * P], m.xT[:, f, bass.ds((ii * 2 + u) * CW, CW)],
                                                      start=f == 0, stop=f == FT - 1)
                            mm.then_inc(h_made, 1)
                pe.wait_ge(tables, 1)
                pe.sem_inc(wide_made, 2)

                def front(t, u):
                    pe.wait_ge(relued, t + 2)
                    for k in range(MT):
                        b, o = divmod(k * P, 512)
                        for f in range(FT):
                            mm = nc.tensor.matmul(banks[b][:, o:o + P], w[:, f, k * P:(k + 1) * P], m.xT[:, f, bass.ds(t * P, P)],
                                                  start=f == 0, stop=f == FT - 1)
                    mm.then_inc(pre, 1)

                def back(t, u):
                    pe.wait_ge(relued, t + 3)
                    pe.wait_ge(z_ready, t + 1)
                    for k in range(MT):
                        mm = nc.tensor.matmul(banks[2 + k // 2][:, (k % 2) * F:(k % 2) * F + F], rT[:, u, k],
                                              mix[:, k].rearrange("p h n -> p (h n)"), start=True, stop=True)
                    mm.then_inc(wide_made, 1)
                front(0, 0)
                with pe.Fori(0, NT // 2) as half:
                    t = half * 2
                    back(t, 0)
                    front(t + 1, 1)
                    back(t + 1, 1)
                    front(t + 2, 0)
                back(NT - 1, 0)
                pe.wait_ge(o_ready, NT)
                pe.sem_inc(resed, 2)

                def turn(t, u):
                    pe.wait_ge(ocopy, t + 1)
                    for k in range(OT):
                        tr = nc.tensor.transpose(banks[u][:, k * P:(k + 1) * P],
                                                 out[:, bass.ds(t, 1), k * P:(k + 1) * P].rearrange("p t c -> p (t c)"), m.ident[:])
                    tr.then_inc(orot, 1)

                def project(t, u):
                    pe.wait_ge(ocopy, t + 3)
                    pe.wait_ge(ftd, t + 1)
                    for k in range(OT):
                        mm = nc.tensor.matmul(banks[2 + u][:, 0:F], oT[:, u, k * P:(k + 1) * P], wres[:, k], start=k == 0, stop=k == OT - 1)
                    mm.then_inc(resed, 1)
                turn(0, 0)
                for t in range(0, NT - 1, 2):
                    turn(t + 1, 1)
                    project(t, 0)
                    turn(t + 2, 0)
                    project(t + 1, 1)
                project(NT - 1, 0)


def top_expert(nc, a, m, banks):
    CH = 2 * CW
    with Stage(nc, "top") as st:
        w1 = st.sb("w1", [P, FT, HID])
        b1 = st.sb("b1", [P, HT])
        wg = st.sb("wg", [P, HT, XQ])
        bg = st.sb("bg", [P, XQ])
        bd = st.sb("bd", [XQ, F])
        wd = st.sb("wd", [P, XQ, HT, F])
        hT = st.sb("hT", [P, HT, CH])
        z = st.sb("z", [P, U, XQ])
        p = st.sb("p", [P, U, XQ])
        order = st.sb("order", [P, U, XQ])
        sel = st.sb("sel", [P, U, XQ])
        top = st.sb("top", [P, U])
        total = st.sb("total", [P, U])
        cT = st.sb("cT", [XQ, U * P])
        loaded, own, hid, gelu, logits, zs, exps, coef, turned, copied, biased, outs, summed, stored = (
            st.sem(x) for x in ("loaded", "own", "hid", "gelu", "logits", "zs", "exps", "coef", "turned", "copied",
                                "biased", "outs", "summed", "stored"))
        experts = st.sem("experts")
        LOADS = 6
        FREE = 2
        with nc.Block() as block:
            @block.sync
            def _(sp):
                for to, x in ((w1, "top_w1"), (b1, "top_b1"), (wg, "top_wg"), (bg, "top_bg"), (bd, "top_bd")):
                    sp.dma_start(to[:], a[x]).then_inc(loaded, 16)
                for e in range(XQ):
                    sp.dma_start(wd[:, e], a["top_wd"][e]).then_inc(experts, 16)
                for ch in range(TU):
                    sp.wait_ge(summed, U + (ch + 1) * XQ * U)
                    rows = min(U * P, N - ch * U * P)
                    full = rows // P
                    sp.dma_start(m.out[ch * U * P:(ch * U + full) * P, :].rearrange("(t p) f -> p t f", p=P),
                                 m.x[:, ch * U:ch * U + full, :]).then_inc(stored, 16)
                    if rows % P:
                        sp.dma_start(m.out[(ch * U + full) * P:N, :], m.x[0:rows % P, ch * U + full, :]).then_inc(stored, 16)
                sp.wait_ge(stored, 16 * (TU + 1))

            @block.gpsimd
            def _(pool):
                nc.gpsimd.iota(order[:], [[0, U], [-1, XQ]], base=XQ, channel_multiplier=0,
                               allow_small_or_imprecise_dtypes=True).then_inc(loaded, 16)

            @block.tensor
            def _(pe):
                pe.wait_ge(loaded, 16 * LOADS)
                pe.wait_ge(experts, 16 * XQ)
                with pe.Fori(0, TU) as ch:
                    for k in range(HT):
                        for hf in range(2):
                            n = k * 2 + hf
                            pe.wait_ge(gelu, ch * 16 + n + 1)
                            for f in range(FT):
                                mm = nc.tensor.matmul(banks[n % FREE][:, 0:CW], w1[:, f, k * P:(k + 1) * P],
                                                      m.xT[:, f, bass.ds(ch * CH + hf * CW, CW)], start=f == 0, stop=f == FT - 1)
                            mm.then_inc(hid, 1)
                    pe.wait_ge(gelu, ch * 16 + 16 + FREE)
                    for u in range(U):
                        for k in range(HT):
                            mm = nc.tensor.matmul(banks[7][:, u * XQ:(u + 1) * XQ], hT[:, k, u * P:(u + 1) * P], wg[:, k],
                                                  start=k == 0, stop=k == HT - 1)
                    mm.then_inc(logits, 1)
                    pe.wait_ge(coef, ch + 1)
                    for u in range(U):
                        nc.tensor.matmul(banks[0 if u < 4 else 1][0:XQ, (u % 4) * P:(u % 4 + 1) * P], p[:, u], m.ident[:],
                                         start=True, stop=True).then_inc(turned, 1)
                    pe.wait_ge(copied, ch * 2 + 2)
                    for u in range(U):
                        pe.wait_ge(summed, ch * (XQ * U) + u + 1)
                        nc.tensor.matmul(banks[FREE + u][:, 0:F], cT[:, u * P:(u + 1) * P], bd[:],
                                         start=True, stop=True).then_inc(turned, 1)
                    for e in range(XQ):
                        for u in range(U):
                            j = e * U + u
                            if e == 0:
                                pe.wait_ge(biased, ch * U + u + 1)
                            pe.wait_ge(summed, ch * (XQ * U) + j + 1)
                            for k in range(HT):
                                mm = nc.tensor.matmul(banks[FREE + u][:, 0:F], hT[:, k, u * P:(u + 1) * P], wd[:, e, k], start=k == 0, stop=k == HT - 1)
                            mm.then_inc(outs, 1)

            @block.scalar
            def _(act):
                act.sem_inc(gelu, FREE)
                act.wait_ge(loaded, 16 * LOADS)
                with act.Fori(0, TU) as ch:
                    for k in range(HT):
                        for hf in range(2):
                            act.wait_ge(hid, ch * 16 + k * 2 + hf + 1)
                            nc.scalar.activation(hT[:, k, hf * CW:(hf + 1) * CW], banks[(k * 2 + hf) % FREE][:, 0:CW], ACT.Gelu,
                                                 bias=b1[:, k:k + 1]).then_inc(gelu, 1)
                    act.wait_ge(zs, ch + 1)
                    nc.scalar.activation(p[:], z[:], ACT.Exp).then_inc(exps, 1)
                    act.wait_ge(turned, ch * (2 * U) + U)
                    nc.scalar.activation(cT[:, 0:4 * P], banks[0][0:XQ, 0:4 * P], ACT.Copy).then_inc(copied, 1)
                    nc.scalar.activation(cT[:, 4 * P:5 * P], banks[1][0:XQ, 0:P], ACT.Copy).then_inc(copied, 1)

            @block.vector
            def _(dve):
                dve.sem_inc(summed, U)
                dve.wait_ge(loaded, 16 * LOADS)
                c = Chain(dve, own)
                PER = 11
                with dve.Fori(0, TU) as ch:
                    c.enter(ch, PER)
                    dve.wait_ge(logits, ch + 1)
                    c(nc.vector.tensor_tensor(z[:], banks[7][:, 0:U * XQ].rearrange("p (t e) -> p t e", e=XQ),
                                              bg[:].unsqueeze(1).to_broadcast([P, U, XQ]), ALU.add))

                    def act_exp():
                        dve.sem_inc(zs, 1)
                        dve.wait_ge(exps, ch + 1)
                    softmax_rows(nc, c, act_exp, z, p, top, total)
                    c(nc.vector.tensor_reduce(top[:], p[:], AX.X, ALU.max))
                    wide_top = top[:].unsqueeze(2).to_broadcast([P, U, XQ])
                    c(nc.vector.tensor_tensor(sel[:], p[:], wide_top, ALU.is_equal))
                    c(nc.vector.tensor_tensor(sel[:], sel[:], order[:], ALU.mult))
                    c(nc.vector.tensor_reduce(total[:], sel[:], AX.X, ALU.max))
                    c(nc.vector.tensor_tensor(sel[:], sel[:], total[:].unsqueeze(2).to_broadcast([P, U, XQ]), ALU.is_equal))
                    nc.vector.tensor_tensor(p[:], p[:], sel[:], ALU.mult).then_inc(coef, 1)
                    for u in range(U):
                        dve.wait_ge(turned, ch * (2 * U) + U + u + 1)
                        x = m.x[:, bass.ds(ch * U + u, 1), :]
                        nc.vector.tensor_tensor(x, x, banks[FREE + u][:, 0:F].unsqueeze(1), ALU.add).then_inc(biased, 1)
                    for e in range(XQ):
                        for u in range(U):
                            dve.wait_ge(outs, ch * (XQ * U) + e * U + u + 1)
                            x = m.x[:, bass.ds(ch * U + u, 1), :]
                            nc.vector.scalar_tensor_tensor(x, banks[FREE + u][:, 0:F].unsqueeze(1), p[:, u, e:e + 1], x, ALU.mult, ALU.add).then_inc(summed, 1)


class Memory:
    pass


def network(nc, a, out, stages=99):
    ctx = ExitStack()
    with ctx:
        m = Memory()

        def sb(name, shape, dt=F32):
            return ctx.enter_context(nc.sbuf_tensor(name, shape, dt))
        banks = [ctx.enter_context(nc.psum_tensor(f"bank{i}", [P, 512], F32)) for i in range(8)]
        m.out = out
        m.ident = sb("ident", [P, P])
        m.zeros = sb("zeros", [P, 512])
        m.x = sb("x", [P, NT, F])
        m.rows = sb("rows", [P, NT, F])
        m.xT = sb("xT", [P, FT, NP])
        edge_ctx = ctx.enter_context(ExitStack())
        m.node_no, m.src, m.dst, m.ranges, m.sums = (
            edge_ctx.enter_context(nc.sbuf_tensor(name, shape, dt)) for name, shape, dt in (
                ("node_no", [P, NP], F32), ("src", [P, ET], I32), ("dst", [P, ET], F32),
                ("ranges", [1, NT * 3], I32), ("sums", [P, NT, F + HEADS], F32)))
        m.d_q, m.d_k, m.d_v, m.d_h = (nc.dram_tensor(f"table_{x}", (NP, F), F32, kind="Internal").ap() for x in "qkvh")
        m.d_probs = nc.dram_tensor("edge_probs", (EP, HEADS), F32, kind="Internal").ap()

        constants(nc, a, m, banks)
        layer_norm(nc, "norm0", m.x, m.rows, m.xT, m.ident, banks)
        with nc.sbuf_tensor("probs", [P, ET, HEADS], F32) as m.probs:
            node_tables(nc, "qkv", m.xT, [a["gnn_wq"], a["gnn_wk"], a["gnn_wv"]], [a["gnn_bq"], a["gnn_bk"], a["gnn_bv"]],
                        [m.d_q, m.d_k, m.d_v], banks)
            edge_scores(nc, a, m, banks)
            attention_sums(nc, a, m, banks)
        with nc.sbuf_tensor("big", [P, FT, NP], F32) as m.big:
            with nc.sbuf_tensor("context", [P, FT, P], F32) as m.context, nc.sbuf_tensor("gain", [P, 2, FT], F32) as gain:
                linear_attention(nc, a, m, banks)
                load_small(nc, gain, a["mix_ln"])
                layer_norm(nc, "norm_mix", m.rows, m.rows, m.big, m.ident, banks, gain[:, 0], gain[:, 1])
                gated_mix(nc, a, m, banks)
            first_update(nc, a, m, banks)
        if stages > 1:
            layer_norm(nc, "norm1", m.x, m.rows, m.xT, m.ident, banks)
            soft_experts(nc, a, m, banks)
        if stages > 2:
            layer_norm(nc, "norm2", m.x, m.rows, m.xT, m.ident, banks)
            node_tables(nc, "h", m.xT, [a["gnn1_wnode"]], [a["gnn1_bnode"]], [m.d_h], banks)
            edge_convolution(nc, a, m, banks)
        if stages > 3:
            spline_layer(nc, a, m, banks)
            edge_ctx.close()
            recycle_semaphores(nc)
        if stages > 4:
            ball_attention(nc, a, m, banks)
        if stages > 5:
            layer_norm(nc, "norm3", m.x, m.rows, m.xT, m.ident, banks)
            top_expert(nc, a, m, banks)
        else:
            with Stage(nc, "dbg") as st:
                s = st.sem("s")
                with nc.Block() as block:
                    @block.sync
                    def _(sp):
                        src = m.sums if stages == 3 else m.x
                        sp.dma_start(m.out[0:24 * P, :].rearrange("(t p) f -> p t f", p=P), src[:, 0:24, 0:F]).then_inc(s, 16)
                        sp.dma_start(m.out[24 * P:N, :], src[0:N - 24 * P, 24, 0:F]).then_inc(s, 16)
                        sp.wait_ge(s, 32)


def load_small(nc, to, src):
    with Stage(nc, "small") as st:
        loaded = st.sem("loaded")
        with nc.Block() as block:
            @block.sync
            def _(sp):
                sp.dma_start(to[:], src).then_inc(loaded, 16)
                sp.wait_ge(loaded, 16)



def _kxn(w):
    k, n = w.shape
    return w.reshape(k // P, P, n).transpose(1, 0, 2)


def _col(v):
    v = v.reshape(v.shape[:-1] + (v.shape[-1] // P, P))
    return np.moveaxis(v, -1, 0)


def _row(v):
    return np.broadcast_to(v, (P,) + v.shape)


def _layouts(i):
    f = {k: np.asarray(v) for k, v in i.items()}
    a = {}
    a["x"] = np.concatenate([f["x"], np.zeros((NP - N, F), np.float32)])
    src = np.concatenate([f["src"], np.zeros(EP - E, np.int32)])
    dst = np.concatenate([f["dst"], np.full(EP - E, -1, np.int32)])
    a["src_tiles"], a["dst_tiles"] = src.reshape(ET, P).T, dst.reshape(ET, P).T
    a["src_scan"], a["dst_scan"] = src.reshape(P, ET), dst.reshape(P, ET)
    end = np.full(1, -2, np.int32)
    a["before_scan"] = np.concatenate([end, dst[:-1]]).reshape(P, ET)
    a["after_scan"] = np.concatenate([dst[1:], end]).reshape(P, ET)
    e = np.concatenate([f["edge_attr_384"], np.zeros((EP - E, ED), np.float32)])
    a["edges"] = e.reshape(ET, P, EC, P).transpose(0, 3, 2, 1)
    for n in "qkv":
        a[f"gnn_w{n}"], a[f"gnn_b{n}"] = _kxn(f[f"L0_gnn_W{n}"].T), _row(f[f"L0_gnn_b{n}"])
    a["gnn_wskip"], a["gnn_bskip"] = _kxn(f["L0_gnn_Wskip"].T), _row(f["L0_gnn_bskip"])
    a["gnn_wgate"] = _row(f["L0_gnn_Wgate"].reshape(3, F))
    a["gnn_bgate"], a["gnn_slope"] = _row(f["L0_gnn_bgate"]), _row(f["L0_gnn_prelu_a"].reshape(1))
    a["gnn_ln_w"], a["gnn_ln_b"] = _row(f["L0_gnn_ln_w"]), _row(f["L0_gnn_ln_b"])
    for j, n in enumerate("qkv"):
        a[f"mix_w{n}"] = _kxn(f["L0_mix_Wqkv"][:, j * F:(j + 1) * F])
    a["mix_wproj"], a["mix_bproj"] = _kxn(f["L0_mix_Wproj"]), _row(f["L0_mix_bproj"])
    a["mix_ln"] = _col(np.stack([f["L0_mix_ln_g"], f["L0_mix_ln_b"]]))
    a["mix_wg1"], a["mix_bg1"] = _kxn(f["L0_mix_Wg1"]), f["L0_mix_bg1"][:, None]
    a["mix_wg2"], a["mix_bg2"] = f["L0_mix_Wg2"], _col(f["L0_mix_bg2"])
    a["ffn_wr"], a["ffn_br"] = _kxn(f["L0_ffn_Wr"]), _row(f["L0_ffn_br"])
    for x, n in (("w1", "W1"), ("w2", "W2"), ("wo", "Wo")):
        a[f"ffn_{x}"] = np.stack([_kxn(w) for w in f[f"L0_ffn_{n}"]])
    for j in "12":
        raw = np.stack([f[f"L0_ffn_{n}{j}"] for n in ("b", "g", "be", "m", "v")])
        a[f"ffn_bn{j}"] = _col(raw).reshape(P, 5, XQ * FT)
    a["ffn_bo"] = f["L0_ffn_bo"]
    a["gnn1_wedge"], a["gnn1_bedge"] = _kxn(f["L1_gnn_W_edge"].T), _row(f["L1_gnn_b_edge"])
    a["gnn1_wnode"], a["gnn1_bnode"] = _kxn(f["L1_gnn_W_node"].T), _row(f["L1_gnn_b_node"])
    a["base_w"] = _kxn(f["L1_gnn_base_weight"].T)
    a["spline_w"] = f["L1_gnn_spline_weight"].transpose(1, 2, 0).reshape(FT, P, KS, F).transpose(1, 0, 2, 3)
    a["spline_scaler"] = _kxn(f["L1_gnn_spline_scaler"].T)
    a["ball_w"] = _kxn(f["L1_mix_w_qkv"][:, :, 2].T)
    a["ball_bn"] = _col(np.stack([f["L1_mix_bn_gamma"], f["L1_mix_bn_beta"]]))
    a["ball_wdw"] = _col(f["L1_mix_w_dw"][:, 0, 2])
    pw = np.zeros((MT, P, P), np.float32)
    w = f["L1_mix_w_pw"][:, :, 0].reshape(MT, P // 32, 32, 32)
    for b in range(P // 32):
        pw[:, b * 32:(b + 1) * 32, b * 32:(b + 1) * 32] = w[:, b].transpose(0, 2, 1)
    a["ball_wpw"] = pw.transpose(1, 0, 2)
    a["ball_wres"], a["ball_bres"] = _kxn(f["L1_mix_w_res"][:, :, 0].T), _row(f["L1_mix_b_res"])
    a["top_w1"], a["top_b1"] = _kxn(f["L1_ffn_W1"]), _col(f["L1_ffn_b1"])
    a["top_wg"], a["top_bg"] = _kxn(f["L1_ffn_Wg"]), _row(f["L1_ffn_bg"])
    a["top_wd"] = np.stack([_kxn(w) for w in f["L1_ffn_Wd"]])
    a["top_bd"] = f["L1_ffn_bd"]
    return {k: np.ascontiguousarray(v) for k, v in a.items()}


STAGES = 99


def kernel(**inputs):
    import concourse.bacc as bacc
    from concourse.bass_utils import run_bass_kernel_spmd

    arrays = _layouts(inputs)
    nc = bacc.Bacc("TRN2", target_bir_lowering=False, num_devices=1)
    aps = {k: nc.dram_tensor(f"in_{k}", v.shape, mybir.dt.from_np(v.dtype), kind="ExternalInput").ap()
           for k, v in arrays.items()}
    out = nc.dram_tensor("out", (N, F), F32, kind="ExternalOutput").ap()
    network(nc, aps, out, STAGES)
    r = run_bass_kernel_spmd(nc, [{f"in_{k}": v for k, v in arrays.items()}], core_ids=[0])
    return r.results[0]["out"]
```

```python
from contextlib import ExitStack

import numpy as np

import concourse.bass as bass
from concourse import mybir
from concourse.alu_op_type import AluOpType as ALU

F32 = mybir.dt.float32
I32 = mybir.dt.int32
ACT = mybir.ActivationFunctionType
AX = mybir.AxisListType

P = 128
N = 3125
NT = -(-N // P)
NP = NT * P
F = 256
FT = F // P
U = 5
TU = NT // U
CW = NP // 10
NC = NP // CW
E = 50000
G = 6
LEAST = 2
ET = -(-E // P) + LEAST * G
ROW_TILES = 4
ET += -ET % ROW_TILES
EP = ET * P
NOWHERE = 1 << 20
HEADS = 4
HD = F // HEADS
ED = 384
EC = ED // P
BIG = 1.0e30
LN_EPS = 1e-5
BN_EPS = 1e-3
MIN_NORM = 1e-15
MAX_NORM = 1.0 - 1e-5
REACH = float(np.arctanh(MAX_NORM))
XQ = 8
HID = 1024
HT = HID // P
MC = 768
MT = MC // P
MG = 2 * MC // 96


class Chain:

    def __init__(self, eng, sem):
        self.eng, self.sem, self.n, self.base = eng, sem, 0, 0

    def __call__(self, ins):
        self.n += 1
        ins.then_inc(self.sem, 1)
        self.eng.wait_ge(self.sem, self.base + self.n)

    def enter(self, i, per):
        self.start, self.base, self.per = self.n, i * per, per

    def leave(self, passes):
        assert self.n - self.start == self.per, (self.n - self.start, self.per)
        self.n, self.base = self.start + self.per * passes, 0


class Stage:

    def __init__(self, nc, name):
        self.nc, self.name, self.ctx = nc, name, ExitStack()

    def __enter__(self):
        return self

    def __exit__(self, *a):
        self.ctx.close()

    def sb(self, name, shape, dt=F32):
        return self.ctx.enter_context(self.nc.sbuf_tensor(f"{self.name}_{name}", shape, dt))

    def gather_sem(self, name):
        return self.nc.alloc_semaphore(f"{self.name}_{name}")

    def sem(self, name):
        return self.ctx.enter_context(self.nc.semaphore(f"{self.name}_{name}"))


def recycle_semaphores(nc):
    used = sorted(nc.released_uncleared_semaphores)
    with nc.Block() as block:
        @block.sync
        def _(sp):
            start = used[0]
            for i, n in enumerate(used):
                if i + 1 == len(used) or used[i + 1] != n + 1:
                    sp.sem_clear(range(start, n + 1))
                    start = used[i + 1] if i + 1 < len(used) else None


def mean_and_variance(nc, c, stats, mv, work):
    even, odd = stats[:, :, 1], stats[:, :, 4]
    c(nc.vector.tensor_tensor(mv[:, :, 0], even, odd, ALU.add))
    c(nc.vector.tensor_tensor(work[:], even, odd, ALU.subtract))
    c(nc.vector.tensor_scalar(mv[:, :, 0], mv[:, :, 0], 0.5, None, ALU.mult))
    c(nc.vector.scalar_tensor_tensor(work[:], work[:], 0.25, work[:], ALU.mult, ALU.mult))
    c(nc.vector.tensor_tensor(mv[:, :, 1], stats[:, :, 2], stats[:, :, 5], ALU.add))
    c(nc.vector.scalar_tensor_tensor(mv[:, :, 1], mv[:, :, 1], 1.0 / F, work[:], ALU.mult, ALU.add))
    c(nc.vector.tensor_scalar(mv[:, :, 1], mv[:, :, 1], LN_EPS, None, ALU.add))


def layer_norm(nc, name, src, rows, cols, ident, banks, gain=None, shift=None):
    with Stage(nc, name) as st:
        stats = st.sb("stats", [P, NT, 6])
        mv = st.sb("mean_var", [P, NT, 2])
        rstd = st.sb("rstd", [P, NT])
        var_ready, std_ready, rows_ready = st.sem("var"), st.sem("std"), st.sem("rows")
        transposed, copied, own = st.sem("transposed"), st.sem("copied"), st.sem("own")
        with nc.Block() as block:
            @block.vector
            def _(dve):
                c = Chain(dve, own)
                with dve.Fori(0, NT) as t:
                    nc.vector.bn_stats(stats[:, bass.ds(t, 1), :], src[:, bass.ds(t, 1), :]).then_inc(own, 1)
                c.n = NT
                dve.wait_ge(own, NT)
                mean_and_variance(nc, c, stats, mv, rstd)
                dve.sem_inc(var_ready, 1)
                dve.wait_ge(std_ready, 1)
                c(nc.vector.reciprocal(rstd[:], rstd[:]))
                with dve.Fori(0, NT) as t:
                    nc.vector.tensor_scalar(rows[:, bass.ds(t, 1), :], src[:, bass.ds(t, 1), :],
                                            mv[:, bass.ds(t, 1), 0], rstd[:, bass.ds(t, 1)],
                                            ALU.subtract, ALU.mult).then_inc(rows_ready, 1)

            @block.tensor
            def _(pe):
                for tt in range(TU):
                    for u in range(U):
                        pe.wait_ge(rows_ready, tt * U + u + 1)
                        pe.wait_ge(copied, (tt * U + u) * FT + FT)
                        for f in range(FT):
                            nc.tensor.transpose(banks[u][:, f * P:(f + 1) * P],
                                                rows[:, bass.ds(tt * U + u, 1), f * P:(f + 1) * P],
                                                ident[:]).then_inc(transposed, 1)

            @block.scalar
            def _(act):
                act.sem_inc(copied, U * FT)
                act.wait_ge(var_ready, 1)
                nc.scalar.activation(rstd[:], mv[:, :, 1], ACT.Sqrt).then_inc(std_ready, 1)
                with act.Fori(0, TU) as tt:
                    for u in range(U):
                        act.wait_ge(transposed, (tt * U + u) * FT + FT)
                        for f in range(FT):
                            to = cols[:, f, bass.ds((tt * U + u) * P, P)]
                            if gain is None:
                                nc.scalar.activation(to, banks[u][:, f * P:(f + 1) * P], ACT.Copy).then_inc(copied, 1)
                            else:
                                nc.scalar.activation(to, banks[u][:, f * P:(f + 1) * P], ACT.Identity,
                                                     scale=gain[:, f:f + 1], bias=shift[:, f:f + 1]).then_inc(copied, 1)


def node_tables(nc, name, cols, weights, biases, tables, banks):
    n = len(tables)
    with Stage(nc, name) as st:
        w = st.sb("w", [P, n, FT, F])
        b = st.sb("b", [P, n, F])
        rows = st.sb("rows", [P, U, n, F])
        loaded, product, added = st.sem("loaded"), st.sem("product"), st.sem("added")
        stored = [st.sem(f"stored{u}") for u in range(U)]

        def bank(k):
            return banks[k % U][:, 0:F]
        with nc.Block() as block:
            @block.sync
            def _(sp):
                for j in range(n):
                    sp.dma_start(w[:, j], weights[j]).then_inc(loaded, 16)
                    sp.dma_start(b[:, j], biases[j]).then_inc(loaded, 16)
                for u in range(U):
                    sp.sem_inc(stored[u], 16 * n)
                with sp.Fori(0, TU) as tt:
                    for u in range(U):
                        sp.wait_ge(added, (tt * U + u) * n + n + U)
                        for j in range(n):
                            sp.dma_start(tables[j][bass.ds((tt * U + u) * P, P), :],
                                         rows[:, u, j]).then_inc(stored[u], 16)
                for u in range(U):
                    sp.wait_ge(stored[u], 16 * n * (TU + 1))

            @block.tensor
            def _(pe):
                pe.wait_ge(loaded, 32 * n)
                for tt in range(TU):
                    for u in range(U):
                        for j in range(n):
                            pe.wait_ge(added, (tt * U + u) * n + j + 1)
                            for f in range(FT):
                                mm = nc.tensor.matmul(bank(u * n + j), cols[:, f, bass.ds((tt * U + u) * P, P)],
                                                      w[:, j, f], start=f == 0, stop=f == FT - 1)
                            mm.then_inc(product, 1)

            @block.vector
            def _(dve):
                dve.sem_inc(added, U)
                with dve.Fori(0, TU) as tt:
                    for u in range(U):
                        dve.wait_ge(stored[u], (tt + 1) * (16 * n))
                        for j in range(n):
                            dve.wait_ge(product, (tt * U + u) * n + j + 1)
                            nc.vector.tensor_tensor(rows[:, u, j], bank(u * n + j), b[:, j], ALU.add).then_inc(added, 1)


def constants(nc, a, m, banks):
    with Stage(nc, "const") as st:
        dst_i = st.sb("dst_i", [P, ET], I32)
        tile_of = st.sb("tile_of", [P, ET])
        from_start = st.sb("from_start", [P, ET])
        from_end = st.sb("from_end", [P, ET])
        hits = st.sb("hits", [P, 2, ET])
        tile_no = st.sb("tile_no", [P, NT])
        most = st.sb("most", [P, 2 * NT])
        most_of_all = st.sb("most_of_all", [2 * NT, 1])
        row = st.sb("row", [1, 2 * NT])
        work = st.sb("work", [1, 4, NT])
        rng_f = st.sb("rng_f", [1, NT, 4])
        count_i = st.sb("count_i", [1, NT], I32)
        edges, nodes, filled, made = st.sem("edges"), st.sem("nodes"), st.sem("filled"), st.sem("made")
        own, tables, turned = st.sem("own"), st.sem("tables"), st.sem("turned")
        with nc.Block() as block:
            @block.sync
            def _(sp):
                sp.dma_start(dst_i[:], a["dst_tiles"]).then_inc(edges, 16)
                sp.dma_start(m.src[:], a["src_tiles"]).then_inc(nodes, 16)
                sp.dma_start(m.x[:], a["x"].rearrange("(t p) f -> p t f", p=P)).then_inc(nodes, 16)
                sp.wait_ge(nodes, 32)

            @block.gpsimd
            def _(pool):
                nc.gpsimd.memset(m.ident[:], 0.0).then_inc(filled, 1)
                pool.wait_ge(filled, 1)
                nc.gpsimd.affine_select(out=m.ident[:], in_=m.ident[:], compare_op=ALU.not_equal, fill=1.0,
                                        base=0, pattern=[[-1, P]], channel_multiplier=1).then_inc(made, 1)
                nc.gpsimd.iota(from_start[:], [[1, ET]], base=1, channel_multiplier=0,
                               allow_small_or_imprecise_dtypes=True).then_inc(made, 1)
                nc.gpsimd.iota(from_end[:], [[-1, ET]], base=ET, channel_multiplier=0,
                               allow_small_or_imprecise_dtypes=True).then_inc(made, 1)
                nc.gpsimd.iota(tile_no[:], [[1, NT]], base=0, channel_multiplier=0,
                               allow_small_or_imprecise_dtypes=True).then_inc(made, 1)
                nc.gpsimd.iota(m.node_no[:], [[1, NP]], base=0, channel_multiplier=0,
                               allow_small_or_imprecise_dtypes=True).then_inc(made, 1)

            @block.vector
            def _(dve):
                c = Chain(dve, own)
                c(nc.vector.memset(m.zeros[:], 0.0))
                dve.wait_ge(edges, 16)
                c(nc.vector.tensor_copy(m.dst[:], dst_i[:]))
                c(nc.vector.tensor_scalar(dst_i[:], dst_i[:], 7, None, ALU.arith_shift_right))
                c(nc.vector.tensor_copy(tile_of[:], dst_i[:]))
                dve.wait_ge(made, 5)
                with dve.Fori(0, NT) as t:
                    c.enter(t, 4)
                    c(nc.vector.scalar_tensor_tensor(hits[:, 0], tile_of[:], tile_no[:, bass.ds(t, 1)], from_start[:],
                                                     ALU.is_equal, ALU.mult))
                    c(nc.vector.scalar_tensor_tensor(hits[:, 1], tile_of[:], tile_no[:, bass.ds(t, 1)], from_end[:],
                                                     ALU.is_equal, ALU.mult))
                    c(nc.vector.tensor_reduce(most[:, bass.ds(t, 1)], hits[:, 0], AX.X, ALU.max))
                    c(nc.vector.tensor_reduce(most[:, bass.ds(t + NT, 1)], hits[:, 1], AX.X, ALU.max))
                c.leave(NT)
                dve.sem_inc(tables, 1)
                dve.wait_ge(turned, 1)
                c(nc.vector.tensor_reduce(most_of_all[:], banks[0][0:2 * NT, 0:P], AX.X, ALU.max))
                dve.sem_inc(tables, 1)
                dve.wait_ge(turned, 2)
                c(nc.vector.tensor_copy(row[:], banks[1][0:1, 0:2 * NT]))
                end, first, count, ones = (work[:, k] for k in range(4))
                c(nc.vector.memset(ones, 1.0))
                c(nc.vector.tensor_scalar(end, row[:, 0:NT], 1.0, None, ALU.max))
                c(nc.vector.tensor_scalar(first, row[:, NT:2 * NT], -1.0, float(ET), ALU.mult, ALU.add))
                c(nc.vector.scalar_tensor_tensor(first, end, -1.0, first, ALU.add, ALU.min))
                c(nc.vector.tensor_tensor(count, end, first, ALU.subtract))
                c(nc.vector.tensor_scalar(count, count, float(G - 1), float(-(-2 ** 16 // G)), ALU.add, ALU.mult))
                c(nc.vector.tensor_copy(count_i[:], count))
                c(nc.vector.tensor_scalar(count_i[:], count_i[:], 16, None, ALU.arith_shift_right))
                c(nc.vector.tensor_copy(count, count_i[:]))
                c(nc.vector.tensor_scalar(count, count, float(LEAST), None, ALU.max))
                c(nc.vector.tensor_tensor_scan(rng_f[:, :, 1], ones, count, 0.0, ALU.mult, ALU.add))
                c(nc.vector.tensor_scalar(rng_f[:, :, 3], rng_f[:, :, 1], -1.0, None, ALU.add))
                c(nc.vector.tensor_tensor(rng_f[:, :, 0], rng_f[:, :, 1], count, ALU.subtract))
                c(nc.vector.scalar_tensor_tensor(rng_f[:, :, 2], rng_f[:, :, 0], -float(G), first, ALU.mult, ALU.add))
                c(nc.vector.tensor_copy(m.ranges[:], rng_f[:].rearrange("p t k -> p (t k)")))

            @block.tensor
            def _(pe):
                pe.wait_ge(tables, 1)
                nc.tensor.transpose(banks[0][0:2 * NT, 0:P], most[:], m.ident[:]).then_inc(turned, 1)
                pe.wait_ge(tables, 2)
                nc.tensor.matmul(banks[1][0:1, 0:2 * NT], most_of_all[:], m.ident[0:2 * NT, 0:2 * NT],
                                 start=True, stop=True).then_inc(turned, 1)


def steps_of(eng, m, t):
    most = NT * (-(-ET // G) + LEAST)
    first = eng.value_load(m.ranges[0:1, bass.ds(t * 4, 1)], min_val=0, max_val=most)
    end = eng.value_load(m.ranges[0:1, bass.ds(t * 4 + 1, 1)], min_val=LEAST, max_val=most)
    shift = eng.value_load(m.ranges[0:1, bass.ds(t * 4 + 2, 1)])
    return first, end, shift


def tile_of_step(eng, s, shift):
    return eng.bass.s_assert_within(s * G + shift, 0, ET - G,
                                    skip_runtime_bounds_check_because="the steps are made of tiles that exist")


def last_step(eng, m, t):
    return eng.value_load(m.ranges[0:1, bass.ds(t * 4 + 3, 1)], min_val=1, max_val=NT * (-(-ET // G) + LEAST))


def edge_scores(nc, a, m, banks):
    Q = 2
    H = G // Q
    with Stage(nc, "scores") as st:
        k = st.sb("k", [P, NT, F])
        ix = st.sb("ix", [P, G], I32)
        q = st.sb("q", [P, G, F])
        hot = st.sb("hot", [P, G, P])
        hotT = st.sb("hotT", [P, G, P])
        qk = st.sb("qk", [P, Q, F])
        dot = st.sb("dot", [P, Q, HEADS])
        own, index, hots, turned, copied, k_made, scored = (
            st.sem(x) for x in ("own", "index", "hots", "turned", "copied", "k_made", "scored"))
        k_loaded, gathers = st.sem("k_loaded"), st.sem("gathers")
        gathered = [st.gather_sem(f"gathered{g}") for g in range(G)]
        with nc.Block() as block:
            @block.sync
            def _(sp):
                sp.dma_start(k[:], m.d_k.rearrange("(t p) f -> p t f", p=P)).then_inc(k_loaded, 16)
                sp.wait_ge(k_loaded, 16)

            @block.scalar
            def _(act):
                act.sem_inc(copied, H)
                with act.Fori(0, NT) as t:
                    first, end, shift = steps_of(act, m, t)
                    with act.Fori(first, end) as s:
                        for h in range(H):
                            act.wait_ge(turned, s * H + (h + 1))
                            act.wait_ge(k_made, s * H + (h + 1))
                            nc.scalar.activation(hotT[:, h * Q:(h + 1) * Q].rearrange("p g n -> p (g n)"),
                                                 banks[h][:, 0:Q * P], ACT.Copy).then_inc(copied, 1)

            @block.gpsimd
            def _(pool):
                with pool.Fori(0, NT) as t:
                    first, end, shift = steps_of(pool, m, t)
                    with pool.Fori(first, end) as s:
                        i = tile_of_step(pool, s, shift)
                        for h in range(H):
                            pool.wait_ge(scored, s * H + (h + 1))
                            pool.sem_inc(gathers, 1)
                            nc.gpsimd.tensor_copy(ix[:, h * Q:(h + 1) * Q], m.src[:, bass.ds(i + h * Q, Q)]).then_inc(index, 1)
                            pool.wait_ge(index, s * H + (h + 1))
                            pool.sem_inc(gathers, 1)
                            for g in range(h * Q, (h + 1) * Q):
                                nc.gpsimd.indirect_dma_start(
                                    out=q[:, g, :], out_offset=None, in_=m.d_q,
                                    in_offset=bass.IndirectOffsetOnAxis(ap=ix[:, g:g + 1], axis=0)
                                ).then_inc(gathered[g], 16)

            @block.tensor
            def _(pe):
                pe.sem_inc(k_made, H)
                pe.wait_ge(k_loaded, 16)
                with pe.Fori(0, NT) as t:
                    first, end, shift = steps_of(pe, m, t)

                    def turn(s, h):
                        pe.wait_ge(hots, s * H + (h + 1))
                        pe.wait_ge(copied, s * H + (h + 1))
                        for g in range(Q):
                            tr = nc.tensor.transpose(banks[h][:, g * P:(g + 1) * P], hot[:, h * Q + g], m.ident[:])
                        tr.then_inc(turned, 1)

                    def spread(s, h):
                        pe.wait_ge(copied, s * H + (h + 1 + H))
                        pe.wait_ge(scored, s * H + (h + 1))
                        for g in range(Q):
                            mm = nc.tensor.matmul(banks[H + h][:, g * F:(g + 1) * F], hotT[:, h * Q + g],
                                                  k[:, bass.ds(t, 1), :].rearrange("p t f -> p (t f)"), start=True, stop=True)
                        mm.then_inc(k_made, 1)
                    turn(first, 0)
                    turn(first, 1)
                    spread(first, 0)
                    last = last_step(pe, m, t)
                    with pe.Fori(first, last) as s:
                        for h in range(H):
                            spread(s + (h + 1) // H, (h + 1) % H)
                            turn(s + (h + 2) // H, (h + 2) % H)
                    for h in range(1, H):
                        spread(last, h)
                        if h + 1 < H:
                            turn(last, h + 1)

            @block.vector
            def _(dve):
                c = Chain(dve, own)
                c(nc.vector.memset(m.scores[:], 0.0))
                start = c.n
                dve.sem_inc(scored, H)
                with dve.Fori(0, NT) as t:
                    first, end, shift = steps_of(dve, m, t)
                    last = last_step(dve, m, t)

                    def one_hot(s, h):
                        dve.wait_ge(copied, s * H + (h + 1))
                        i = tile_of_step(dve, s, shift)
                        for g in range(h * Q, (h + 1) * Q):
                            ins = nc.vector.tensor_scalar(hot[:, g], m.node_no[:, bass.ds(t * P, P)],
                                                          m.dst[:, bass.ds(i + g, 1)], None, ALU.is_equal)
                        ins.then_inc(hots, 1)

                    def score(s, h):
                        for g in range(h * Q, (h + 1) * Q):
                            dve.wait_ge(gathered[g], (s + 1) * 16)
                        dve.wait_ge(k_made, s * H + (h + 1 + H))
                        dve.wait_ge(own, s * (2 * H) + (2 * h + start))
                        nc.vector.tensor_tensor(qk[:].rearrange("p g f -> p (g f)"), q[:, h * Q:(h + 1) * Q].rearrange("p g f -> p (g f)"),
                                                banks[H + h][:, 0:Q * F], ALU.mult).then_inc(own, 1)
                        dve.wait_ge(own, s * (2 * H) + (2 * h + 1 + start))
                        dve.wait_ge(scored, s * H + (h + H))
                        nc.vector.tensor_reduce(dot[:], qk[:].rearrange("p g (h d) -> p g h d", h=HEADS), AX.X, ALU.add).then_inc(own, 1)
                        dve.wait_ge(own, s * (2 * H) + (2 * h + 2 + start))
                        at = m.scores[:, :, bass.ds(tile_of_step(dve, s, shift) + h * Q, Q)]
                        nc.vector.tensor_tensor(at, at, dot[:].rearrange("p g h -> p h g"), ALU.add).then_inc(scored, 1)
                    one_hot(first, 0)
                    one_hot(first, 1)
                    with dve.Fori(first, last) as s:
                        for h in range(H):
                            one_hot(s + (h + 2) // H, (h + 2) % H)
                            score(s, h)
                    for h in range(H):
                        if h + 2 < H:
                            one_hot(last, h + 2)
                        score(last, h)


def largest_scores(nc, a, m, banks):
    TR = ROW_TILES
    R = ET // TR
    ROW = TR * P
    with Stage(nc, "largest") as st:
        dst = st.sb("dst", [R, 3, ROW], I32)
        S = st.sb("S", [R, HEADS, ROW])
        V = st.sb("V", [R, HEADS, ROW])
        W = st.sb("W", [R, HEADS, ROW])
        bound = st.sb("bound", [R, 2, ROW])
        down = st.sb("down", [R, ROW])
        downs = st.sb("downs", [R, 1])
        tails = st.sb("tails", [R, 2, HEADS])
        low = st.sb("low", [R, 2, 1])
        scan_in = st.sb("scan_in", [HEADS, 2, R])
        carried = st.sb("carried", [HEADS, R + 1])
        carry = st.sb("carry", [R, HEADS])
        loaded, own, rows, scans, turned, done, backs, kept = (
            st.sem(x) for x in ("loaded", "own", "rows", "scans", "turned", "done", "backs", "kept"))
        with nc.Block() as block:
            @block.sync
            def _(sp):
                for j, x in enumerate(("dst_scan", "before_scan", "after_scan")):
                    sp.dma_start(dst[:, j], a[x]).then_inc(loaded, 16)
                sp.wait_ge(loaded, 48)

            @block.tensor
            def _(pe):
                for h in range(HEADS):
                    for b in range(TR):
                        tr = nc.tensor.transpose(banks[h][0:R, b * P:(b + 1) * P],
                                                 m.scores[:, h].rearrange("p (r b) -> p b r", b=TR)[:, b], m.ident[:])
                    tr.then_inc(rows, 1)
                for j in range(2):
                    pe.wait_ge(scans, 2 * j + 1)
                    for i in range(2):
                        nc.tensor.transpose(banks[4 + i][0:HEADS, 0:R], tails[:, i], m.ident[0:R, 0:R]).then_inc(turned, 1)
                    if j == 0:
                        nc.tensor.transpose(banks[7][0:1, 0:R], downs[:], m.ident[0:R, 0:R])
                    pe.wait_ge(scans, 2 * j + 2)
                    part = carried[:, 1:R + 1] if j else carried[:, 0:R]
                    nc.tensor.transpose(banks[6][0:R, 0:HEADS], part, m.ident[0:HEADS, 0:HEADS]).then_inc(turned, 1)
                pe.wait_ge(done, 1)
                for b in range(TR):
                    for h in range(HEADS):
                        tr = nc.tensor.transpose(banks[b][:, h * R:(h + 1) * R], W[:, h, b * P:(b + 1) * P], m.ident[0:R, 0:R])
                    tr.then_inc(backs, 1)

            @block.scalar
            def _(act):
                for b in range(TR):
                    act.wait_ge(backs, b + 1)
                    nc.scalar.activation(m.probs[:].rearrange("p (r b) h -> p b r h", b=TR)[:, b],
                                         banks[b][:, 0:HEADS * R].rearrange("p (h r) -> p r h", h=HEADS), ACT.Copy)

            @block.vector
            def _(dve):
                c = Chain(dve, own)
                dve.wait_ge(loaded, 48)
                for j in range(2):
                    c(nc.vector.tensor_tensor(bound[:, j], dst[:, 0], dst[:, j + 1], ALU.not_equal))
                    c(nc.vector.tensor_scalar(bound[:, j], bound[:, j], -BIG, None, ALU.mult))
                    c(nc.vector.tensor_reduce(low[:, j], bound[:, j], AX.X, ALU.min))
                c(nc.vector.tensor_tensor(down[:], dst[:, 1], dst[:, 0], ALU.is_gt))
                c(nc.vector.tensor_reduce(downs[:], down[:], AX.X, ALU.max))
                for h in range(HEADS):
                    dve.wait_ge(rows, h + 1)
                    c(nc.vector.tensor_copy(S[:, h], banks[h][0:R, 0:ROW]))

                def scan(out, by, seen, first, back):
                    step = slice(None, None, -1) if back else slice(None)
                    for h in range(HEADS):
                        c(nc.vector.tensor_tensor_scan(out[:, h, step], by[:, step], seen[:, h, step],
                                                       -BIG if first is None else first[:, h:h + 1], ALU.add, ALU.max))

                for j, (seen, out) in enumerate(((S, V), (V, W))):
                    back = j == 1
                    edge = 0 if back else ROW - 1
                    scan(W, bound[:, j], seen, None, back)
                    c(nc.vector.tensor_copy(tails[:, 0], W[:, :, edge]))
                    nc.vector.tensor_copy(tails[:, 1], low[:, j].to_broadcast([R, HEADS])).then_inc(scans, 1)
                    dve.wait_ge(turned, 3 * j + 2)
                    c(nc.vector.tensor_copy(scan_in[:, 0], banks[4][0:HEADS, 0:R]))
                    c(nc.vector.tensor_copy(scan_in[:, 1], banks[5][0:HEADS, 0:R]))
                    c(nc.vector.memset(carried[:], -BIG))
                    step = slice(R - 1, None, -1) if back else slice(None)
                    out_c = carried[:, R - 1::-1] if back else carried[:, 1:R + 1]
                    c(nc.vector.tensor_tensor_scan(out_c, scan_in[:, 1, step], scan_in[:, 0, step], -BIG, ALU.add, ALU.max))
                    dve.sem_inc(scans, 1)
                    dve.wait_ge(turned, 3 * j + 3)
                    if j == 0:
                        c(nc.vector.tensor_reduce(downs[0:1], banks[7][0:1, 0:R], AX.X, ALU.max))
                        c(nc.vector.tensor_copy(m.unsorted[:], downs[0:1]))
                    c(nc.vector.tensor_copy(carry[:], banks[6][0:R, 0:HEADS]))
                    scan(out, bound[:, j], seen, carry, back)
                dve.sem_inc(done, 1)
        unordered_scores(nc, a, m, st, S)


def unordered_scores(nc, a, m, st, S):
    R, _, ROW = S.shape
    node_of = st.sb("node_of", [P, NT])
    to = st.sb("to", [P, ROW], I32)
    mask = st.sb("mask", [P, 2, ROW])
    row = st.sb("row", [P, HEADS, ROW])
    best = st.sb("best", [P, NT, HEADS])
    wide = st.sb("wide", [P, HEADS, ROW])
    row_best = st.sb("row_best", [P, HEADS])
    index = st.sb("index", [P, ET], I32)
    ix = st.sb("ix", [P, 1], I32)
    got = st.sb("got", [P, HEADS])
    named, kept, arrived, used, maxed, stored, own, indexed, taken, gathers = (
        st.sem(x) for x in ("named", "rows_kept", "arrived", "used", "maxed", "stored", "own2", "indexed", "taken", "gathers"))
    gathered = st.gather_sem("gathered")
    rows_begun = st.sem("rows_begun")
    with nc.Block() as block:
        @block.sync
        def _(sp):
            with sp.If(sp.value_load(m.unsorted[0:1, 0:1], min_val=0, max_val=1) > 0):
                sp.dma_start(m.d_rows, S[:].rearrange("r h e -> r (h e)")).then_inc(kept, 16)
                sp.wait_ge(kept, 16)
                with sp.Fori(0, R) as r:
                    sp.wait_ge(used, r + 1)
                    sp.dma_start(row[:].rearrange("p h e -> p (h e)"),
                                 m.d_rows[bass.ds(r, 1), :].to_broadcast([P, HEADS * ROW])).then_inc(arrived, 16)
                    sp.dma_start(to[:], a["dst_scan"][bass.ds(r, 1), :].to_broadcast([P, ROW])).then_inc(arrived, 16)
                sp.wait_ge(maxed, 1)
                sp.dma_start(m.d_best.rearrange("(t p) h -> p t h", p=P), best[:]).then_inc(stored, 16)
                sp.wait_ge(stored, 16)

        @block.gpsimd
        def _(pool):
            nc.gpsimd.iota(node_of[:], [[P, NT]], base=0, channel_multiplier=1,
                           allow_small_or_imprecise_dtypes=True).then_inc(named, 1)
            with pool.If(pool.value_load(m.unsorted[0:1, 0:1], min_val=0, max_val=1) > 0):
                pool.wait_ge(stored, 16)
                with pool.Fori(0, ET) as j:
                    pool.wait_ge(taken, j + 1)
                    pool.sem_inc(gathers, 1)
                    nc.gpsimd.tensor_copy(ix[:], index[:, bass.ds(j, 1)]).then_inc(indexed, 1)
                    pool.wait_ge(indexed, j + 1)
                    pool.sem_inc(gathers, 1)
                    nc.gpsimd.indirect_dma_start(out=got[:], out_offset=None, in_=m.d_best,
                                                 in_offset=bass.IndirectOffsetOnAxis(ap=ix[:], axis=0)).then_inc(gathered, 16)

        @block.vector
        def _(dve):
            with dve.If(dve.value_load(m.unsorted[0:1, 0:1], min_val=0, max_val=1) > 0):
                c = Chain(dve, own)
                dve.wait_ge(named, 1)
                c(nc.vector.memset(best[:], -BIG))
                c(nc.vector.tensor_scalar(index[:], m.dst[:], float(NP - 1), None, ALU.min))
                start = c.n
                dve.sem_inc(used, 1)
                with dve.Fori(0, R) as r:
                    dve.wait_ge(arrived, r * 32 + 32)
                    nc.vector.tensor_copy(mask[:, 0], to[:]).then_inc(own, 1)
                    dve.wait_ge(own, r * (4 * NT + 1) + (start + 1))
                    dve.sem_inc(rows_begun, 1)
                    with dve.Fori(0, NT) as t:
                        done = r * (4 * NT + 1) + t * 4 + (start + 1)
                        nc.vector.tensor_scalar(mask[:, 1], mask[:, 0], node_of[:, bass.ds(t, 1)], -BIG,
                                                ALU.not_equal, ALU.mult).then_inc(own, 1)
                        dve.wait_ge(own, done + 1)
                        nc.vector.tensor_tensor(wide[:], row[:], mask[:, 1].unsqueeze(1).to_broadcast([P, HEADS, ROW]), ALU.add).then_inc(own, 1)
                        dve.wait_ge(own, done + 2)
                        nc.vector.tensor_reduce(row_best[:], wide[:], AX.X, ALU.max).then_inc(own, 1)
                        dve.wait_ge(own, done + 3)
                        b = best[:, bass.ds(t, 1), :]
                        nc.vector.tensor_tensor(b, b, row_best[:].unsqueeze(1), ALU.max).then_inc(own, 1)
                        dve.wait_ge(own, done + 4)
                    dve.sem_inc(used, 1)
                dve.sem_inc(maxed, 1)
                dve.sem_inc(taken, 1)
                with dve.Fori(0, ET) as j:
                    dve.wait_ge(gathered, j * 16 + 16)
                    nc.vector.tensor_copy(m.probs[:, bass.ds(j, 1), :], got[:].unsqueeze(1)).then_inc(taken, 1)


def attention_sums(nc, a, m, banks):
    WIDE = F + HEADS
    with Stage(nc, "attend") as st:
        ix = st.sb("ix", [P, G], I32)
        v = st.sb("v", [P, G, F])
        pv = st.sb("pv", [P, G, WIDE])
        hot = st.sb("hot", [P, G, P])
        index, weighted, multiplied, summed, kept = (st.sem(x) for x in ("index", "weighted", "multiplied", "summed", "kept"))
        gathers, diff, exps = st.sem("gathers"), st.sem("diff"), st.sem("exps")
        gathered = [st.gather_sem(f"gathered{g}") for g in range(G)]
        acc = banks[0][:, 0:WIDE]
        with nc.Block() as block:
            @block.scalar
            def _(act):
                act.wait_ge(diff, 2)
                nc.scalar.activation(m.probs[:], m.probs[:], ACT.Exp, scale=float(HD) ** -0.5).then_inc(exps, 1)
                with act.Fori(0, NT) as t:
                    first, end, shift = steps_of(act, m, t)
                    with act.Fori(first, end) as s:
                        i = tile_of_step(act, s, shift)
                        for g in range(G):
                            act.wait_ge(weighted, s * G + g + 1)
                            nc.scalar.activation(ix[:, g:g + 1], m.src[:, bass.ds(i + g, 1)], ACT.Copy).then_inc(index, 1)

            @block.gpsimd
            def _(pool):
                with pool.Fori(0, NT) as t:
                    first, end, shift = steps_of(pool, m, t)
                    with pool.Fori(first, end) as s:
                        for g in range(G):
                            pool.wait_ge(index, s * G + g + 1)
                            pool.wait_ge(weighted, s * G + g + 1)
                            pool.sem_inc(gathers, 1)
                            nc.gpsimd.indirect_dma_start(
                                out=v[:, g, :], out_offset=None, in_=m.d_v,
                                in_offset=bass.IndirectOffsetOnAxis(ap=ix[:, g:g + 1], axis=0)
                            ).then_inc(gathered[g], 16)

            @block.vector
            def _(dve):
                dve.sem_inc(weighted, G)
                nc.vector.tensor_tensor(m.probs[:], m.scores[:].rearrange("p h j -> p j h"), m.probs[:],
                                        ALU.subtract).then_inc(diff, 1)
                dve.wait_ge(diff, 1)
                nc.vector.tensor_scalar(m.probs[:], m.probs[:], 0.0, None, ALU.min).then_inc(diff, 1)
                dve.wait_ge(exps, 1)
                with dve.Fori(0, NT) as t:
                    first, end, shift = steps_of(dve, m, t)
                    with dve.Fori(first, end) as s:
                        i = tile_of_step(dve, s, shift)
                        for g in range(G):
                            dve.wait_ge(multiplied, s * G + g + 1)
                            nc.vector.tensor_scalar(hot[:, g], m.node_no[:, bass.ds(t * P, P)],
                                                    m.dst[:, bass.ds(i + g, 1)], None, ALU.is_equal)
                            prob = m.probs[:, bass.ds(i + g, 1), :].rearrange("p j h -> p (j h)")
                            nc.vector.tensor_copy(pv[:, g, F:WIDE], prob)
                            dve.wait_ge(gathered[g], (s + 1) * 16)
                            nc.vector.tensor_tensor(pv[:, g, 0:F].rearrange("p (h d) -> p h d", h=HEADS),
                                                    v[:, g].rearrange("p (h d) -> p h d", h=HEADS),
                                                    prob.unsqueeze(2).to_broadcast([P, HEADS, HD]),
                                                    ALU.mult).then_inc(weighted, 1)
                    dve.wait_ge(summed, t + 1)
                    nc.vector.tensor_copy(m.sums[:, bass.ds(t, 1), :], acc.unsqueeze(1)).then_inc(kept, 1)

            @block.tensor
            def _(pe):
                pe.sem_inc(multiplied, G)
                with pe.Fori(0, NT) as t:
                    first, end, shift = steps_of(pe, m, t)
                    pe.wait_ge(kept, t + 1)
                    nc.tensor.matmul(acc, m.zeros[:, 0:P], m.zeros[:, 0:WIDE], start=True, stop=False)
                    with pe.Fori(first, end) as s:
                        for g in range(G):
                            pe.wait_ge(weighted, s * G + g + 1 + G)
                            nc.tensor.matmul(acc, hot[:, g], pv[:, g], start=False, stop=False).then_inc(multiplied, 1)
                    nc.tensor.matmul(acc, m.zeros[:, 0:P], m.zeros[:, 0:WIDE], start=False, stop=True).then_inc(summed, 1)

            @block.sync
            def _(sp):
                sp.sem_inc(kept, 1)


def linear_attention(nc, a, m, banks):
    B = 32
    with Stage(nc, "context") as st:
        wk = st.sb("wk", [P, FT, F])
        wv = st.sb("wv", [P, FT, F])
        ek = st.sb("ek", [P, 2, F])
        v = st.sb("v", [P, 2, F])
        top = st.sb("top", [P, FT])
        total = st.sb("total", [P, FT])
        kT = m.big
        loaded, product, copied, shift, exps, own = (st.sem(x) for x in ("loaded", "product", "copied", "shift", "exps", "own"))
        turned, v_made, ek_copied, v_copied, done = (st.sem(x) for x in ("turned", "v_made", "ek_copied", "v_copied", "done"))
        with nc.Block() as block:
            @block.sync
            def _(sp):
                sp.dma_start(wk[:], a["mix_wk"]).then_inc(loaded, 16)
                sp.dma_start(wv[:], a["mix_wv"]).then_inc(loaded, 16)
                sp.wait_ge(loaded, 32)

            @block.tensor
            def _(pe):
                pe.wait_ge(loaded, 32)
                with pe.Fori(0, NC) as i:
                    for c in range(FT):
                        pe.wait_ge(copied, i * FT + c + 1)
                        for f in range(FT):
                            mm = nc.tensor.matmul(banks[c][:, 0:CW], wk[:, f, c * P:(c + 1) * P],
                                                  m.xT[:, f, bass.ds(i * CW, CW)], start=f == 0, stop=f == FT - 1)
                        mm.then_inc(product, 1)
                pe.wait_ge(exps, FT)
                for c in range(FT):
                    nc.tensor.matmul(banks[6 + c][:, 0:P], m.zeros[:, 0:P], m.zeros[:, 0:P], start=True, stop=False)

                def front(t, u):
                    pe.wait_ge(ek_copied, t + 1)
                    for c in range(FT):
                        tr = nc.tensor.transpose(banks[u][:, c * P:(c + 1) * P], kT[:, c, bass.ds(t * P, P)], m.ident[:])
                    tr.then_inc(turned, 1)
                    pe.wait_ge(v_copied, t + 1)
                    for f in range(FT):
                        mm = nc.tensor.matmul(banks[2 + u][:, 0:F], m.xT[:, f, bass.ds(t * P, P)], wv[:, f],
                                              start=f == 0, stop=f == FT - 1)
                    mm.then_inc(v_made, 1)

                def back(t, u):
                    pe.wait_ge(ek_copied, t + 3)
                    pe.wait_ge(v_copied, t + 3)
                    for c in range(FT):
                        mm = nc.tensor.matmul(banks[6 + c][:, 0:P], ek[:, u, c * P:(c + 1) * P], v[:, u, c * P:(c + 1) * P],
                                              start=False, stop=False)
                    mm.then_inc(done, 1)
                front(0, 0)
                for tt in range(NT // 2):
                    front(tt * 2 + 1, 1)
                    back(tt * 2, 0)
                    front(tt * 2 + 2, 0)
                    back(tt * 2 + 1, 1)
                back(NT - 1, 0)
                for c in range(FT):
                    nc.tensor.matmul(banks[6 + c][:, 0:P], m.zeros[:, 0:P], m.zeros[:, 0:P], start=False, stop=True).then_inc(done, 1)

            @block.scalar
            def _(act):
                act.sem_inc(copied, FT)
                with act.Fori(0, NC) as i:
                    for c in range(FT):
                        act.wait_ge(product, i * FT + c + 1)
                        nc.scalar.activation(kT[:, c, bass.ds(i * CW, CW)], banks[c][:, 0:CW], ACT.Copy).then_inc(copied, 1)
                act.wait_ge(shift, FT)
                for c in range(FT):
                    nc.scalar.activation(kT[:, c, 0:N], kT[:, c, 0:N], ACT.Exp, bias=top[:, c:c + 1],
                                         accum_out=total[:, c:c + 1]).then_inc(exps, 1)
                act.sem_inc(ek_copied, 2)
                with act.Fori(0, NT // 2) as half:
                    t = half * 2
                    for u in range(2):
                        act.wait_ge(turned, t + u + 1)
                        act.wait_ge(done, t + u + 1)
                        nc.scalar.activation(ek[:, u], banks[u][:, 0:F], ACT.Copy).then_inc(ek_copied, 1)
                act.wait_ge(turned, NT)
                act.wait_ge(done, NT)
                nc.scalar.activation(ek[:, 0], banks[0][:, 0:F], ACT.Copy).then_inc(ek_copied, 1)

            @block.vector
            def _(dve):
                c_ = Chain(dve, own)
                dve.sem_inc(v_copied, 2)
                dve.sem_inc(done, 2)
                c_(nc.vector.memset(m.context[:], 0.0))
                dve.wait_ge(copied, FT * NC + FT)
                for c in range(FT):
                    nc.vector.tensor_reduce(top[:, c:c + 1], kT[:, c, 0:N], AX.X, ALU.max, negate=True).then_inc(shift, 1)
                with dve.Fori(0, NT // 2) as half:
                    t = half * 2
                    for u in range(2):
                        dve.wait_ge(v_made, t + u + 1)
                        dve.wait_ge(done, t + u + 1)
                        nc.vector.tensor_copy(v[:, u], banks[2 + u][:, 0:F]).then_inc(v_copied, 1)
                dve.wait_ge(v_made, NT)
                dve.wait_ge(done, NT)
                nc.vector.tensor_copy(v[:, 0], banks[2][:, 0:F]).then_inc(v_copied, 1)
                dve.wait_ge(exps, FT)
                c_(nc.vector.reciprocal(total[:], total[:]))
                dve.wait_ge(done, 2 + NT + FT)
                for c in range(FT):
                    for b in range(P // B):
                        at = slice(b * B, (b + 1) * B)
                        nc.vector.tensor_scalar(m.context[at, c, at], banks[6 + c][at, at], total[at, c:c + 1], None, ALU.mult)


def gated_mix(nc, a, m, banks):
    GH = F // 4
    with Stage(nc, "mix") as st:
        wq = st.sb("wq", [P, FT, F])
        wg1 = st.sb("wg1", [P, FT, GH])
        wg2 = st.sb("wg2", [GH, F])
        bg1 = st.sb("bg1", [GH, 1])
        bg2 = st.sb("bg2", [P, FT])
        hT = st.sb("hT", [GH, NP])
        qT = st.sb("qT", [P, FT, CW])
        gate = st.sb("gate", [P, FT, CW])
        loaded, hid, gelu, product, sig, qc, mixed = (st.sem(x) for x in ("loaded", "hid", "gelu", "product", "sig", "qc", "mixed"))
        with nc.Block() as block:
            @block.sync
            def _(sp):
                for to, x in ((wq, "mix_wq"), (wg1, "mix_wg1"), (wg2, "mix_wg2"), (bg1, "mix_bg1"), (bg2, "mix_bg2")):
                    sp.dma_start(to[:], a[x]).then_inc(loaded, 16)
                sp.wait_ge(loaded, 80)

            @block.tensor
            def _(pe):
                pe.wait_ge(loaded, 80)
                with pe.Fori(0, NC // 2) as ii:
                    for u in range(2):
                        pe.wait_ge(gelu, ii * 2 + u + 1)
                        for f in range(FT):
                            mm = nc.tensor.matmul(banks[u][0:GH, 0:CW], wg1[:, f], m.big[:, f, bass.ds((ii * 2 + u) * CW, CW)],
                                                  start=f == 0, stop=f == FT - 1)
                        mm.then_inc(hid, 1)
                with pe.Fori(0, NC) as i:
                    for c in range(FT):
                        pe.wait_ge(qc, i * FT + c + 1)
                        for f in range(FT):
                            mm = nc.tensor.matmul(banks[2 + c][:, 0:CW], wq[:, f, c * P:(c + 1) * P],
                                                  m.xT[:, f, bass.ds(i * CW, CW)], start=f == 0, stop=f == FT - 1)
                        mm.then_inc(product, 1)
                    for c in range(FT):
                        pe.wait_ge(gelu, NC + 2)
                        pe.wait_ge(sig, i * FT + c + 1)
                        nc.tensor.matmul(banks[4 + c][:, 0:CW], wg2[:, c * P:(c + 1) * P], hT[:, bass.ds(i * CW, CW)],
                                         start=True, stop=True).then_inc(product, 1)
                    for c in range(FT):
                        pe.wait_ge(qc, i * FT + c + 1 + FT)
                        pe.wait_ge(mixed, i * FT + c + 1)
                        nc.tensor.matmul(banks[6 + c][:, 0:CW], m.context[:, c], qT[:, c], start=True, stop=True).then_inc(product, 1)

            @block.scalar
            def _(act):
                act.wait_ge(loaded, 80)
                act.sem_inc(gelu, 2)
                act.sem_inc(sig, FT)
                with act.Fori(0, NC // 2) as ii:
                    for u in range(2):
                        act.wait_ge(hid, ii * 2 + u + 1)
                        nc.scalar.activation(hT[:, bass.ds((ii * 2 + u) * CW, CW)], banks[u][0:GH, 0:CW], ACT.Gelu,
                                             bias=bg1[:]).then_inc(gelu, 1)
                with act.Fori(0, NC) as i:
                    for c in range(FT):
                        act.wait_ge(product, i * 6 + 3 + c)
                        act.wait_ge(mixed, i * FT + c + 1)
                        nc.scalar.activation(gate[:, c], banks[4 + c][:, 0:CW], ACT.Sigmoid, bias=bg2[:, c:c + 1]).then_inc(sig, 1)

            @block.vector
            def _(dve):
                dve.sem_inc(qc, FT)
                dve.sem_inc(mixed, FT)
                with dve.Fori(0, NC) as i:
                    for c in range(FT):
                        dve.wait_ge(product, i * 6 + 1 + c)
                        dve.wait_ge(mixed, i * FT + c + 1)
                        nc.vector.tensor_copy(qT[:, c], banks[2 + c][:, 0:CW]).then_inc(qc, 1)
                    for c in range(FT):
                        dve.wait_ge(product, i * 6 + 5 + c)
                        dve.wait_ge(sig, i * FT + c + 1 + FT)
                        nc.vector.tensor_tensor(m.big[:, c, bass.ds(i * CW, CW)], banks[6 + c][:, 0:CW], gate[:, c],
                                                ALU.mult).then_inc(mixed, 1)


def first_update(nc, a, m, banks):
    with Stage(nc, "update") as st:
        names = ("gnn_wskip", "mix_wproj")
        w = st.sb("w", [P, 2, FT, F])
        rows = st.sb("rows", [P, 6, F])
        wgate = st.sb("wgate", [P, 3, F])
        bgate = st.sb("bgate", [P, 1])
        slope = st.sb("slope", [P, 1])
        skip = m.rows
        inv = st.sb("inv", [P, NT, HEADS])
        dots = st.sb("dots", [P, 2, NT])
        g = st.sb("g", [P, NT])
        junk = st.sb("junk", [P, F])
        res = st.sb("res", [P, NT, F])
        neg = m.rows
        stats = st.sb("stats", [P, NT, 6])
        mv = st.sb("mv", [P, NT, 2])
        rstd = st.sb("rstd", [P, NT])
        loaded, skipped, kept, own, z_ready, gate_ready, var_ready, std_ready, projected, added = (
            st.sem(x) for x in ("loaded", "skipped", "kept", "own", "z", "gate", "var", "std", "projected", "added"))
        LOADS = 9

        def row(k):
            return rows[:, k].unsqueeze(1).to_broadcast([P, NT, F])
        with nc.Block() as block:
            @block.sync
            def _(sp):
                for j, x in enumerate(names):
                    sp.dma_start(w[:, j], a[x]).then_inc(loaded, 16)
                for j, x in enumerate(("gnn_bskip", "gnn_ln_w", "gnn_ln_b", "mix_bproj")):
                    sp.dma_start(rows[:, j], a[x]).then_inc(loaded, 16)
                sp.dma_start(wgate[:], a["gnn_wgate"]).then_inc(loaded, 16)
                sp.dma_start(bgate[:], a["gnn_bgate"]).then_inc(loaded, 16)
                sp.dma_start(slope[:], a["gnn_slope"]).then_inc(loaded, 16)
                sp.wait_ge(loaded, 16 * LOADS)

            @block.tensor
            def _(pe):
                pe.wait_ge(loaded, 16 * LOADS)
                for j, (src, sem, free) in enumerate(((m.xT, skipped, kept), (m.big, projected, added))):
                    if j:
                        pe.wait_ge(kept, NT + U)
                    for tt in range(TU):
                        for u in range(U):
                            pe.wait_ge(free, tt * U + u + 1)
                            for f in range(FT):
                                mm = nc.tensor.matmul(banks[u][:, 0:F], src[:, f, bass.ds((tt * U + u) * P, P)], w[:, j, f],
                                                      start=f == 0, stop=f == FT - 1)
                            mm.then_inc(sem, 1)

            @block.scalar
            def _(act):
                act.wait_ge(loaded, 16 * LOADS)
                act.wait_ge(z_ready, 1)
                nc.scalar.activation(g[:], dots[:, 0], ACT.Sigmoid, bias=bgate[:]).then_inc(gate_ready, 1)
                act.wait_ge(var_ready, 1)
                nc.scalar.activation(rstd[:], mv[:, :, 1], ACT.Sqrt).then_inc(std_ready, 1)

            @block.vector
            def _(dve):
                c = Chain(dve, own)
                dve.sem_inc(kept, U)
                dve.sem_inc(added, U)
                dve.wait_ge(loaded, 16 * LOADS)
                c(nc.vector.tensor_tensor(rows[:, 4], wgate[:, 0], wgate[:, 2], ALU.add))
                c(nc.vector.tensor_tensor(rows[:, 5], wgate[:, 1], wgate[:, 2], ALU.subtract))
                with dve.Fori(0, TU) as tt:
                    for u in range(U):
                        dve.wait_ge(skipped, tt * U + u + 1)
                        nc.vector.tensor_tensor(skip[:, bass.ds(tt * U + u, 1), :], banks[u][:, 0:F].unsqueeze(1),
                                                rows[:, 0:1], ALU.add).then_inc(kept, 1)
                c(nc.vector.tensor_scalar(inv[:], m.sums[:, :, F:F + HEADS], 1.0 / BIG, None, ALU.max))
                c(nc.vector.reciprocal(inv[:], inv[:]))
                with dve.Fori(0, NT) as t:
                    r = res[:, bass.ds(t, 1), :].rearrange("p t (h d) -> p (t h) d", h=HEADS)
                    nc.vector.tensor_tensor(r, m.sums[:, bass.ds(t, 1), 0:F].rearrange("p t (h d) -> p (t h) d", h=HEADS),
                                            inv[:, bass.ds(t, 1), :].rearrange("p t h -> p (t h)").unsqueeze(2).to_broadcast([P, HEADS, HD]),
                                            ALU.mult).then_inc(own, 1)
                c.n += NT
                dve.wait_ge(own, c.n)
                dve.wait_ge(kept, NT + U)
                for t in range(NT):
                    for j, part in enumerate((skip, res)):
                        c(nc.vector.tensor_tensor_reduce(out=junk[:], in0=part[:, t], in1=rows[:, 4 + j], scale=1.0, scalar=0.0,
                                                         op0=ALU.mult, op1=ALU.add, accum_out=dots[:, j, t:t + 1]))
                nc.vector.tensor_tensor(dots[:, 0], dots[:, 0], dots[:, 1], ALU.add).then_inc(z_ready, 1)
                c(nc.vector.tensor_tensor(skip[:], skip[:], res[:], ALU.subtract))
                dve.wait_ge(gate_ready, 1)
                with dve.Fori(0, NT) as t:
                    nc.vector.scalar_tensor_tensor(res[:, bass.ds(t, 1), :], skip[:, bass.ds(t, 1), :], g[:, bass.ds(t, 1)],
                                                   res[:, bass.ds(t, 1), :], ALU.mult, ALU.add).then_inc(own, 1)
                c.n += NT
                dve.wait_ge(own, c.n)
                with dve.Fori(0, NT) as t:
                    nc.vector.bn_stats(stats[:, bass.ds(t, 1), :], res[:, bass.ds(t, 1), :]).then_inc(own, 1)
                c.n += NT
                dve.wait_ge(own, c.n)
                mean_and_variance(nc, c, stats, mv, rstd)
                dve.sem_inc(var_ready, 1)
                dve.wait_ge(std_ready, 1)
                c(nc.vector.reciprocal(rstd[:], rstd[:]))
                with dve.Fori(0, NT) as t:
                    nc.vector.tensor_scalar(res[:, bass.ds(t, 1), :], res[:, bass.ds(t, 1), :], mv[:, bass.ds(t, 1), 0],
                                            rstd[:, bass.ds(t, 1)], ALU.subtract, ALU.mult).then_inc(own, 1)
                c.n += NT
                dve.wait_ge(own, c.n)
                c(nc.vector.tensor_tensor(res[:], res[:], row(1), ALU.mult))
                c(nc.vector.tensor_tensor(res[:], res[:], row(2), ALU.add))
                c(nc.vector.tensor_scalar(neg[:], res[:], 0.0, slope[:], ALU.min, ALU.mult))
                c(nc.vector.scalar_tensor_tensor(res[:], res[:], 0.0, neg[:], ALU.max, ALU.add))
                c(nc.vector.tensor_tensor(m.x[:], m.x[:], row(3), ALU.add))
                c(nc.vector.tensor_tensor(m.x[:], m.x[:], res[:], ALU.add))
                with dve.Fori(0, TU) as tt:
                    for u in range(U):
                        dve.wait_ge(projected, tt * U + u + 1)
                        x = m.x[:, bass.ds(tt * U + u, 1), :]
                        nc.vector.tensor_tensor(x, x, banks[u][:, 0:F].unsqueeze(1), ALU.add).then_inc(added, 1)


def softmax_rows(nc, c, act_exp, z, w, top, total):
    c(nc.vector.tensor_reduce(top[:], z[:], AX.X, ALU.max))
    c(nc.vector.tensor_tensor(z[:], z[:], top[:].unsqueeze(2).to_broadcast(list(z.shape)), ALU.subtract))
    act_exp()
    c(nc.vector.tensor_reduce(total[:], w[:], AX.X, ALU.add))
    c(nc.vector.reciprocal(total[:], total[:]))
    c(nc.vector.tensor_tensor(w[:], w[:], total[:].unsqueeze(2).to_broadcast(list(w.shape)), ALU.mult))


def soft_experts(nc, a, m, banks):
    CH = 2 * CW
    with Stage(nc, "soft") as st:
        wr = st.sb("wr", [P, FT, XQ])
        br = st.sb("br", [P, XQ])
        bo = st.sb("bo", [XQ, F])
        z = st.sb("z", [P, NT, XQ])
        w = st.sb("w", [P, NT, XQ])
        top = st.sb("top", [P, NT])
        total = st.sb("total", [P, NT])
        wT = st.sb("wT", [XQ, NP])
        raw = st.sb("raw", [P, 2, 5, XQ * FT])
        sc = st.sb("sc", [P, 2, XQ, FT])
        bi = st.sb("bi", [P, 2, XQ, FT])
        W = st.sb("W", [P, 2, 3, FT, F])
        h1 = st.sb("h1", [P, FT, CH])
        h2 = st.sb("h2", [P, FT, CH])
        loaded, own, logits, zs, exps, std, scales, wts, turned, wcopy = (
            st.sem(x) for x in ("loaded", "own", "logits", "zs", "exps", "std", "scales", "wts", "turned", "wcopy"))
        hid, relu, outs, summed, biased, w_used = (st.sem(x) for x in ("hid", "relu", "outs", "summed", "biased", "w_used"))
        begun, begun_act = st.sem("begun"), st.sem("begun_act")
        wload = [st.sem(f"wload{j}") for j in range(2)]
        HSLOTS = 2
        with nc.Block() as block:
            @block.sync
            def _(sp):
                sp.dma_start(wr[:], a["ffn_wr"]).then_inc(loaded, 16)
                sp.dma_start(br[:], a["ffn_br"]).then_inc(loaded, 16)
                sp.dma_start(bo[:], a["ffn_bo"]).then_inc(loaded, 16)
                for j in range(2):
                    sp.dma_start(raw[:, j], a[f"ffn_bn{j + 1}"]).then_inc(loaded, 16)
                sp.wait_ge(loaded, 80)
                with sp.Fori(0, XQ // 2) as ee:
                    for j in range(2):
                        sp.wait_ge(w_used, ee * 2 + j + 1)
                        for k, x in enumerate(("ffn_w1", "ffn_w2", "ffn_wo")):
                            sp.dma_start(W[:, j, k], a[x][bass.ds(ee * 2 + j, 1)].rearrange("e p f n -> p (e f) n")).then_inc(wload[j], 16)

            @block.gpsimd
            def _(pool):
                pool.sem_inc(w_used, 2)

            @block.tensor
            def _(pe):
                pe.wait_ge(loaded, 80)
                for t in range(NT):
                    for f in range(FT):
                        mm = nc.tensor.matmul(banks[0][:, t * XQ:(t + 1) * XQ], m.xT[:, f, t * P:(t + 1) * P], wr[:, f],
                                              start=f == 0, stop=f == FT - 1)
                mm.then_inc(logits, 1)
                pe.wait_ge(wts, 1)
                for tt in range(TU):
                    for u in range(U):
                        pe.wait_ge(wcopy, tt * U + u + 1)
                        nc.tensor.matmul(banks[4 + u % 2][0:XQ, 0:P], w[:, bass.ds(tt * U + u, 1), :].rearrange("p t e -> p (t e)"),
                                         m.ident[:], start=True, stop=True).then_inc(turned, 1)
                        pe.wait_ge(wcopy, tt * U + u + 3)
                        pe.wait_ge(biased, tt * U + u + 2)
                        nc.tensor.matmul(banks[6 + u % 2][:, 0:F], wT[:, bass.ds((tt * U + u) * P, P)], bo[:],
                                         start=True, stop=True).then_inc(turned, 1)
                pe.wait_ge(biased, NT + 2)
                with pe.Fori(0, XQ // 2) as ee:
                    for j in range(2):
                        pe.wait_ge(wload[j], ee * 48 + 48)
                        pe.sem_inc(begun, 1)
                        with pe.Fori(0, TU) as ch:
                            n = (ee * 2 + j) * TU + ch
                            for layer, (src, dst) in enumerate(((m.xT, h1), (h1, h2))):
                                for hf in range(2):
                                    for c in range(FT):
                                        k = layer * 4 + hf * 2 + c
                                        pe.wait_ge(relu, n * 8 + k + 1)
                                        if layer:
                                            pe.wait_ge(relu, n * 8 + HSLOTS + hf * 2 + 2)
                                        for f in range(FT):
                                            cols = m.xT[:, f, bass.ds(ch * CH + hf * CW, CW)] if layer == 0 else h1[:, f, hf * CW:(hf + 1) * CW]
                                            mm = nc.tensor.matmul(banks[k % HSLOTS][:, 0:CW], W[:, j, layer, f, c * P:(c + 1) * P], cols,
                                                                  start=f == 0, stop=f == FT - 1)
                                        mm.then_inc(hid, 1)
                            for u in range(U):
                                pe.wait_ge(relu, n * 8 + HSLOTS + (6 if u < 2 else 8))
                                pe.wait_ge(summed, n * U + u + 1)
                                for f in range(FT):
                                    mm = nc.tensor.matmul(banks[HSLOTS + u][:, 0:F], h2[:, f, u * P:(u + 1) * P], W[:, j, 2, f],
                                                          start=f == 0, stop=f == FT - 1)
                                mm.then_inc(outs, 1)
                        pe.wait_ge(outs, (ee * 2 + j) * (TU * U) + TU * U)
                        pe.sem_inc(w_used, 1)

            @block.scalar
            def _(act):
                act.sem_inc(relu, HSLOTS)
                act.wait_ge(std, 1)
                nc.scalar.activation(sc[:], sc[:], ACT.Sqrt).then_inc(std, 1)
                act.wait_ge(zs, 1)
                nc.scalar.activation(w[:], z[:], ACT.Exp).then_inc(exps, 1)
                act.sem_inc(wcopy, 2)
                with act.Fori(0, TU) as tt:
                    for u in range(U):
                        act.wait_ge(turned, tt * (2 * U) + 2 * u + 1)
                        nc.scalar.activation(wT[:, bass.ds((tt * U + u) * P, P)], banks[4 + u % 2][0:XQ, 0:P], ACT.Copy).then_inc(wcopy, 1)
                act.wait_ge(scales, 1)
                with act.Fori(0, XQ) as e:
                    with act.Fori(0, TU) as ch:
                        n = e * TU + ch
                        for layer, dst in enumerate((h1, h2)):
                            for hf in range(2):
                                for c in range(FT):
                                    k = layer * 4 + hf * 2 + c
                                    act.wait_ge(hid, n * 8 + k + 1)
                                    act.sem_inc(begun_act, 1)
                                    nc.scalar.activation(dst[:, c, hf * CW:(hf + 1) * CW], banks[k % HSLOTS][:, 0:CW], ACT.Relu,
                                                         scale=sc[:, layer, bass.ds(e, 1), c], bias=bi[:, layer, bass.ds(e, 1), c]).then_inc(relu, 1)

            @block.vector
            def _(dve):
                c = Chain(dve, own)
                dve.sem_inc(summed, U)
                dve.sem_inc(biased, 2)
                dve.wait_ge(loaded, 80)
                scv, biv = (x[:].rearrange("p l e c -> p l (e c)") for x in (sc, bi))
                nc.vector.tensor_scalar(scv, raw[:, :, 4], BN_EPS, None, ALU.add).then_inc(std, 1)
                dve.wait_ge(std, 2)
                c(nc.vector.reciprocal(scv, scv))
                c(nc.vector.tensor_tensor(scv, scv, raw[:, :, 1], ALU.mult))
                c(nc.vector.tensor_tensor(biv, raw[:, :, 0], raw[:, :, 3], ALU.subtract))
                c(nc.vector.tensor_tensor(biv, biv, scv, ALU.mult))
                nc.vector.tensor_tensor(biv, biv, raw[:, :, 2], ALU.add).then_inc(scales, 1)
                dve.wait_ge(logits, 1)
                c(nc.vector.tensor_tensor(z[:], banks[0][:, 0:NT * XQ].rearrange("p (t e) -> p t e", e=XQ),
                                          br[:].unsqueeze(1).to_broadcast([P, NT, XQ]), ALU.add))

                def act_exp():
                    dve.sem_inc(zs, 1)
                    dve.wait_ge(exps, 1)
                softmax_rows(nc, c, act_exp, z, w, top, total)
                dve.sem_inc(wts, 1)
                with dve.Fori(0, TU) as tt:
                    for u in range(U):
                        dve.wait_ge(turned, tt * (2 * U) + 2 * u + 2)
                        x = m.x[:, bass.ds(tt * U + u, 1), :]
                        nc.vector.tensor_tensor(x, x, banks[6 + u % 2][:, 0:F].unsqueeze(1), ALU.add).then_inc(biased, 1)
                with dve.Fori(0, XQ) as e:
                    with dve.Fori(0, TU) as ch:
                        n = e * TU + ch
                        for u in range(U):
                            dve.wait_ge(outs, n * U + u + 1)
                            x = m.x[:, bass.ds(ch * U + u, 1), :]
                            nc.vector.scalar_tensor_tensor(x, banks[HSLOTS + u][:, 0:F].unsqueeze(1), w[:, bass.ds(ch * U + u, 1), bass.ds(e, 1)].rearrange("p t e -> p (t e)"),
                                                           x, ALU.mult, ALU.add).then_inc(summed, 1)


def edge_convolution(nc, a, m, banks):
    with Stage(nc, "conv") as st:
        w = st.sb("w", [P, EC, F])
        b = st.sb("b", [P, F])
        ix = st.sb("ix", [P, G], I32)
        eT = st.sb("eT", [P, G, EC, P])
        h = st.sb("h", [P, G, F])
        be = st.sb("be", [P, 2, F])
        msg = st.sb("msg", [P, G, F])
        hot = st.sb("hot", [P, G, P])
        loaded, index, made, ready, multiplied, summed, kept, own = (
            st.sem(x) for x in ("w", "index", "made", "ready", "multiplied", "summed", "kept", "own"))
        gathers = st.sem("gathers")
        gathered = [st.gather_sem(f"gathered{g}") for g in range(G)]
        arrived = [st.sem(f"arrived{g}") for g in range(G)]
        acc = banks[0][:, 0:F]

        def edge_bank(g):
            return banks[1 + g][:, 0:F]
        with nc.Block() as block:
            @block.sync
            def _(sp):
                sp.dma_start(w[:], a["gnn1_wedge"]).then_inc(loaded, 16)
                sp.dma_start(b[:], a["gnn1_bedge"]).then_inc(loaded, 16)
                sp.wait_ge(loaded, 32)
                with sp.Fori(0, NT) as t:
                    first, end, shift = steps_of(sp, m, t)
                    with sp.Fori(first, end) as s:
                        i = tile_of_step(sp, s, shift)
                        for g in range(G):
                            sp.wait_ge(made, s * G + g + 1)
                            sp.dma_start(eT[:, g], a["edges"][bass.ds(i + g, 1)].rearrange("t p c e -> p (t c) e")).then_inc(arrived[g], 16)

            @block.scalar
            def _(act):
                act.sem_inc(kept, 1)
                with act.Fori(0, NT) as t:
                    first, end, shift = steps_of(act, m, t)
                    with act.Fori(first, end) as s:
                        i = tile_of_step(act, s, shift)
                        for g in range(G):
                            act.wait_ge(ready, s * G + g + 1)
                            nc.scalar.activation(ix[:, g:g + 1], m.src[:, bass.ds(i + g, 1)], ACT.Copy).then_inc(index, 1)

            @block.gpsimd
            def _(pool):
                with pool.Fori(0, NT) as t:
                    first, end, shift = steps_of(pool, m, t)
                    with pool.Fori(first, end) as s:
                        for g in range(G):
                            pool.wait_ge(index, s * G + g + 1)
                            pool.wait_ge(ready, s * G + g + 1)
                            pool.sem_inc(gathers, 1)
                            nc.gpsimd.indirect_dma_start(
                                out=h[:, g, :], out_offset=None, in_=m.d_h,
                                in_offset=bass.IndirectOffsetOnAxis(ap=ix[:, g:g + 1], axis=0)
                            ).then_inc(gathered[g], 16)

            @block.vector
            def _(dve):
                dve.sem_inc(ready, G)
                dve.wait_ge(loaded, 32)
                with dve.Fori(0, NT) as t:
                    first, end, shift = steps_of(dve, m, t)
                    with dve.Fori(first, end) as s:
                        i = tile_of_step(dve, s, shift)
                        for g in range(G):
                            dve.wait_ge(made, s * G + g + 1 + G)
                            nc.vector.tensor_tensor(be[:, g % 2], edge_bank(g), b[:], ALU.add).then_inc(own, 1)
                            dve.wait_ge(multiplied, s * G + g + 1)
                            nc.vector.tensor_scalar(hot[:, g], m.node_no[:, bass.ds(t * P, P)],
                                                    m.dst[:, bass.ds(i + g, 1)], None, ALU.is_equal)
                            dve.wait_ge(own, s * G + g + 1)
                            dve.wait_ge(gathered[g], (s + 1) * 16)
                            nc.vector.tensor_tensor(msg[:, g], be[:, g % 2], h[:, g], ALU.mult).then_inc(ready, 1)
                    dve.wait_ge(summed, t + 1)
                    nc.vector.tensor_copy(m.sums[:, bass.ds(t, 1), 0:F], acc.unsqueeze(1)).then_inc(kept, 1)

            @block.tensor
            def _(pe):
                pe.sem_inc(made, G)
                pe.sem_inc(multiplied, G)
                pe.wait_ge(loaded, 32)
                with pe.Fori(0, NT) as t:
                    first, end, shift = steps_of(pe, m, t)
                    pe.wait_ge(kept, t + 1)
                    nc.tensor.matmul(acc, m.zeros[:, 0:P], m.zeros[:, 0:F], start=True, stop=False)

                    def project(s, g):
                        pe.wait_ge(arrived[g], (s + 1) * 16)
                        pe.wait_ge(ready, s * G + g + 1)
                        for c in range(EC):
                            mm = nc.tensor.matmul(edge_bank(g), eT[:, g, c], w[:, c], start=c == 0, stop=c == EC - 1)
                        mm.then_inc(made, 1)

                    def add_up(s, g):
                        pe.wait_ge(ready, s * G + g + 1 + G)
                        nc.tensor.matmul(acc, hot[:, g], msg[:, g], start=False, stop=False).then_inc(multiplied, 1)
                    project(first, 0)
                    last = last_step(pe, m, t)
                    with pe.Fori(first, last) as s:
                        for g in range(G):
                            project(s + (g + 1) // G, (g + 1) % G)
                            add_up(s, g)
                    for g in range(1, G):
                        project(last, g)
                        add_up(last, g - 1)
                    add_up(last, G - 1)
                    nc.tensor.matmul(acc, m.zeros[:, 0:P], m.zeros[:, 0:F], start=False, stop=True).then_inc(summed, 1)


KS = 7


def spline_layer(nc, a, m, banks):
    with Stage(nc, "spline") as st:
        wb = st.sb("wb", [P, FT, F])
        ws = st.sb("ws", [P, FT, KS, F])
        scaler = st.sb("scaler", [P, FT, F])
        knot = st.sb("knot", [P, KS + 2])
        sT = st.sb("sT", [P, 2, FT * P])
        base = st.sb("base", [P, 2, FT, P])
        near = st.sb("near", [P, 2, KS, FT * P])
        wide = st.sb("wide", [P, 2, KS, FT * P])
        spl = st.sb("spl", [P, 2, KS, FT * P])
        loaded, turned, copied, own, own_act, parts, bases, made, added, knots = (
            st.sem(x) for x in ("loaded", "turned", "copied", "own", "own_act", "parts", "bases", "made", "added", "knots"))

        def staggered(eng, front, back, unroll=False):
            def pair(t):
                front(t + 1, 1)
                back(t, 0)
                front(t + 2, 0)
                back(t + 1, 1)
            front(0, 0)
            if unroll:
                for t in range(0, NT - 1, 2):
                    pair(t)
            else:
                with eng.Fori(0, NT // 2) as half:
                    t = half * 2
                    pair(t)
            back(NT - 1, 0)
        with nc.Block() as block:
            @block.sync
            def _(sp):
                for to, x in ((wb, "base_w"), (ws, "spline_w"), (scaler, "spline_scaler")):
                    sp.dma_start(to[:], a[x]).then_inc(loaded, 16)
                sp.wait_ge(loaded, 48)

            @block.tensor
            def _(pe):
                pe.wait_ge(loaded, 48)
                pe.sem_inc(made, 2)

                def turn(t, u):
                    pe.wait_ge(copied, t + 1)
                    for f in range(FT):
                        tr = nc.tensor.transpose(banks[0][:, f * P:(f + 1) * P], m.sums[:, bass.ds(t, 1), f * P:(f + 1) * P], m.ident[:])
                    tr.then_inc(turned, 1)

                def products(t, u):
                    pe.wait_ge(bases, t + 3)
                    pe.wait_ge(added, t + 1)
                    for f in range(FT):
                        nc.tensor.matmul(banks[2 + u][:, 0:F], base[:, u, f], wb[:, f], start=f == 0, stop=False)
                    for f in range(FT):
                        for k in range(KS):
                            mm = nc.tensor.matmul(banks[2 + u][:, 0:F], spl[:, u, k, f * P:(f + 1) * P], ws[:, f, k],
                                                  start=False, stop=f == FT - 1 and k == KS - 1)
                    mm.then_inc(made, 1)
                staggered(pe, turn, products, unroll=True)

            @block.scalar
            def _(act):
                act.sem_inc(copied, 1)
                act.wait_ge(knots, 1)

                def body(t, u):
                    act.wait_ge(turned, t + 1)
                    act.wait_ge(made, t + 1)
                    nc.scalar.activation(sT[:, u], banks[0][:, 0:FT * P], ACT.Copy).then_inc(copied, 1)
                    act.wait_ge(copied, t + 2)
                    nc.scalar.activation(base[:, u].rearrange("p f n -> p (f n)"), sT[:, u], ACT.Silu)
                    for k in range(KS):
                        nc.scalar.activation(near[:, u, k], sT[:, u], ACT.Abs, scale=2.0, bias=knot[:, k:k + 1]).then_inc(own_act, 1)
                    act.wait_ge(own_act, t * 8 + 7)
                    nc.scalar.activation(wide[:, u], near[:, u], ACT.Relu, scale=-1.0, bias=knot[:, KS:KS + 1]).then_inc(own_act, 1)
                    act.wait_ge(own_act, t * 8 + 8)
                    nc.scalar.activation(spl[:, u], wide[:, u], ACT.Square)
                    nc.scalar.activation(near[:, u], near[:, u], ACT.Relu, scale=-1.0, bias=knot[:, KS + 1:KS + 2]).then_inc(parts, 1)
                with act.Fori(0, NT // 2) as half:
                    t = half * 2
                    body(t, 0)
                    body(t + 1, 1)
                body(NT - 1, 0)

            @block.vector
            def _(dve):
                c = Chain(dve, own)
                for k in range(KS):
                    c(nc.vector.memset(knot[:, k:k + 1], 3.0 - k))
                for k in range(2):
                    c(nc.vector.memset(knot[:, KS + k:KS + k + 1], 2.0 - k))
                dve.sem_inc(knots, 1)
                dve.sem_inc(added, 2)
                dve.sem_inc(bases, 2)
                dve.wait_ge(loaded, 48)
                c(nc.vector.tensor_scalar(scaler[:], scaler[:], 1.0 / 6.0, None, ALU.mult))
                for f in range(FT):
                    c(nc.vector.tensor_tensor(ws[:, f], ws[:, f], scaler[:, f].unsqueeze(1).to_broadcast([P, KS, F]), ALU.mult))
                done = c.n

                def compute(t, u):
                    dve.wait_ge(parts, t + 1)
                    nc.vector.tensor_tensor(spl[:, u], spl[:, u], wide[:, u], ALU.mult).then_inc(own, 1)
                    dve.wait_ge(own, t * 3 + done + 1)
                    nc.vector.tensor_tensor(wide[:, u], near[:, u], near[:, u], ALU.mult).then_inc(own, 1)
                    dve.wait_ge(own, t * 3 + done + 2)
                    nc.vector.scalar_tensor_tensor(wide[:, u], wide[:, u], -4.0, near[:, u], ALU.mult, ALU.mult).then_inc(own, 1)
                    dve.wait_ge(own, t * 3 + done + 3)
                    nc.vector.tensor_tensor(spl[:, u], spl[:, u], wide[:, u], ALU.add).then_inc(bases, 1)

                def add(t, u):
                    dve.wait_ge(made, t + 3)
                    x = m.x[:, bass.ds(t, 1), :]
                    nc.vector.tensor_tensor(x, x, banks[2 + u][:, 0:F].unsqueeze(1), ALU.add).then_inc(added, 1)
                staggered(dve, compute, add)


def ball_attention(nc, a, m, banks):
    WC = 2 * MC
    OC = MG * 32
    OT = OC // P
    TAIL = N - (NC - 1) * CW
    with Stage(nc, "ball") as st:
        w = st.sb("w", [P, FT, MC])
        gb = st.sb("gb", [P, 2, MT])
        wdw = st.sb("wdw", [P, MT])
        mix = st.sb("mix", [P, MT, 2, P])
        wres = st.sb("wres", [P, OT, F])
        bres = st.sb("bres", [P, F])
        norm = st.sb("norm", [P, NT])
        f1 = st.sb("f1", [P, NT])
        f2 = st.sb("f2", [P, NT])
        small = st.sb("small", [P, NT])
        junk = st.sb("junk", [P, 2, 3, 512])
        junk2 = st.sb("junk2", [P, 512])
        stats = st.sb("stats", [P, MT, NC, 6])
        mv = st.sb("mv", [P, MT, 2])
        sc = st.sb("sc", [P, MT])
        bi = st.sb("bi", [P, MT])
        rT = st.sb("rT", [P, 2, MT, P])
        sq = st.sb("sq", [P, 2, 4])
        z = st.sb("z", [P, 2, WC])
        zq = st.sb("zq", [P, OC])
        ksum = st.sb("ksum", [P, MG])
        out = st.sb("out", [P, NT, OC])
        oT = st.sb("oT", [P, 2, OC])
        loaded, own, own_act = st.sem("loaded"), st.sem("own"), st.sem("own_act")
        (sq_done, root_in, root, lns, ln, scaled, turned, tcopied, h_made, h_seen, var_in, var_out, tables,
         pre, relued, wide_made, wide_sq, fin, fout, wide_out, z_ready, o_ready) = (
            st.sem(x) for x in ("sq", "root_in", "root", "lns", "ln", "scaled", "turned", "tcopied", "h_made", "h_seen",
                                "var_in", "var_out", "tables", "pre", "relued", "wide_made", "wide_sq", "fin", "fout",
                                "wide_out", "z_ready", "o_ready"))
        nsq, nroot, orot, ocopy, resed, ftd, tanh = (st.sem(x) for x in ("nsq", "nroot", "orot", "ocopy", "resed", "ftd", "tanh"))
        with nc.Block() as block:
            @block.sync
            def _(sp):
                for to, x in ((w[:], "ball_w"), (gb[:], "ball_bn"), (wdw[:], "ball_wdw"), (mix[:, :, 1], "ball_wpw"),
                              (wres[:], "ball_wres"), (bres[:], "ball_bres")):
                    sp.dma_start(to, a[x]).then_inc(loaded, 16)
                sp.wait_ge(loaded, 16 * 6)

            @block.scalar
            def _(act):
                with act.Fori(0, NT) as t:
                    nc.scalar.activation(out[:, bass.ds(t, 1), 0:F].rearrange("p t f -> p (t f)"),
                                         m.rows[:, bass.ds(t, 1), :].rearrange("p t f -> p (t f)"), ACT.Square,
                                         accum_out=norm[:, bass.ds(t, 1)]).then_inc(sq_done, 1)
                act.wait_ge(sq_done, NT)
                nc.scalar.activation(norm[:], norm[:], ACT.Sqrt).then_inc(root, 1)
                act.wait_ge(lns, 1)
                nc.scalar.activation(f1[:], f1[:], ACT.Ln).then_inc(ln, 1)
                act.sem_inc(tcopied, 4)
                with act.Fori(0, TU) as tt:
                    for u in range(U):
                        act.wait_ge(turned, tt * U + u + 1)
                        nc.scalar.activation(m.xT[:, :, bass.ds((tt * U + u) * P, P)],
                                             banks[u][:, 0:F].rearrange("p (f n) -> p f n", f=FT), ACT.Copy).then_inc(tcopied, 1)
                act.wait_ge(var_in, 1)
                nc.scalar.activation(sc[:], sc[:], ACT.Sqrt).then_inc(var_out, 1)
                act.wait_ge(tables, 1)
                act.sem_inc(relued, 2)

                def body(t, u):
                    act.wait_ge(pre, t + 1)
                    act.wait_ge(wide_made, t + 1)
                    for k in range(MT):
                        b, o = divmod(k * P, 512)
                        ins = nc.scalar.activation(rT[:, u, k], banks[b][:, o:o + P], ACT.Relu, scale=sc[:, k:k + 1], bias=bi[:, k:k + 1])
                    ins.then_inc(relued, 1)
                    act.wait_ge(wide_made, t + 3)
                    for b in range(3):
                        ins = nc.scalar.activation(junk[:, u, b], banks[2 + b][:, :], ACT.Square, accum_out=sq[:, u, b:b + 1])
                    ins.then_inc(wide_sq, 1)
                    act.wait_ge(fin, t + 1)
                    nc.scalar.activation(sq[:, u, 3:4], sq[:, u, 3:4], ACT.Sqrt).then_inc(fout, 1)
                with act.Fori(0, NT // 2) as half:
                    t = half * 2
                    body(t, 0)
                    body(t + 1, 1)
                body(NT - 1, 0)
                act.wait_ge(o_ready, NT)
                act.sem_inc(nsq, 1)
                with act.Fori(0, NT) as t:
                    act.wait_ge(nsq, t + 1)
                    nc.scalar.activation(junk[:, 0, 0], out[:, bass.ds(t, 1), :].rearrange("p t c -> p (t c)"), ACT.Square,
                                         accum_out=norm[:, bass.ds(t, 1)]).then_inc(nsq, 1)
                act.wait_ge(nsq, NT + 1)
                nc.scalar.activation(norm[:], norm[:], ACT.Sqrt).then_inc(nroot, 1)
                act.sem_inc(ocopy, 2)

                def turn_copy(t, u):
                    act.wait_ge(orot, t + 1)
                    act.wait_ge(resed, t + 1)
                    nc.scalar.activation(oT[:, u], banks[u][:, :], ACT.Copy).then_inc(ocopy, 1)
                with act.Fori(0, NT // 2) as half:
                    t = half * 2
                    turn_copy(t, 0)
                    turn_copy(t + 1, 1)
                turn_copy(NT - 1, 0)
                act.wait_ge(ftd, 2 + NT)
                with act.Fori(0, NT) as t:
                    nc.scalar.activation(out[:, bass.ds(t, 1), 0:F].rearrange("p t f -> p (t f)"),
                                         m.rows[:, bass.ds(t, 1), :].rearrange("p t f -> p (t f)"), ACT.Square,
                                         accum_out=f1[:, bass.ds(t, 1)]).then_inc(own_act, 1)
                act.wait_ge(own_act, NT)
                nc.scalar.activation(f1[:], f1[:], ACT.Sqrt).then_inc(tanh, 1)
                act.wait_ge(tanh, 2)
                nc.scalar.activation(f2[:], f1[:], ACT.Tanh).then_inc(tanh, 1)

            @block.vector
            def _(dve):
                c = Chain(dve, own)
                dve.wait_ge(root, 1)
                c(nc.vector.tensor_scalar(f2[:], norm[:], MAX_NORM, None, ALU.min))
                c(nc.vector.tensor_scalar(f1[:], f2[:], -1.0, 1.0, ALU.mult, ALU.add))
                c(nc.vector.reciprocal(f1[:], f1[:]))
                c(nc.vector.scalar_tensor_tensor(f1[:], f2[:], 1.0, f1[:], ALU.add, ALU.mult))
                dve.sem_inc(lns, 1)
                c(nc.vector.tensor_scalar(norm[:], norm[:], MIN_NORM, None, ALU.max))
                c(nc.vector.reciprocal(norm[:], norm[:]))
                c(nc.vector.tensor_tensor(small[:], f2[:], f2[:], ALU.mult))
                c(nc.vector.tensor_scalar(junk2[:, 0:NT], small[:], 0.2, 1.0 / 3.0, ALU.mult, ALU.add))
                c(nc.vector.tensor_tensor(small[:], small[:], junk2[:, 0:NT], ALU.mult))
                c(nc.vector.tensor_scalar(small[:], small[:], 1.0, None, ALU.add))
                c(nc.vector.tensor_scalar(f2[:], f2[:], 0.05, None, ALU.is_lt))
                dve.wait_ge(ln, 1)
                c(nc.vector.scalar_tensor_tensor(f1[:], f1[:], 0.5, norm[:], ALU.mult, ALU.mult))
                c(nc.vector.tensor_tensor(small[:], small[:], f1[:], ALU.subtract))
                c(nc.vector.tensor_tensor(small[:], small[:], f2[:], ALU.mult))
                c(nc.vector.tensor_tensor(f1[:], f1[:], small[:], ALU.add))
                with dve.Fori(0, NT) as t:
                    nc.vector.tensor_scalar(m.rows[:, bass.ds(t, 1), :], m.rows[:, bass.ds(t, 1), :], f1[:, bass.ds(t, 1)], None,
                                            ALU.mult).then_inc(scaled, 1)
                dve.sem_inc(h_seen, 2)
                dve.wait_ge(loaded, 96)
                for k in range(MT):
                    c(nc.vector.tensor_copy(mix[:, k, 0], m.ident[:]))
                    c(nc.vector.tensor_scalar(mix[:, k, 1], mix[:, k, 1], wdw[:, k:k + 1], None, ALU.mult))
                for k in range(MT):
                    with dve.Fori(0, NC // 2) as ii:
                        for u in range(2):
                            dve.wait_ge(h_made, ii * 2 + u + 1 + k * NC)
                            nc.vector.bn_stats(stats[:, k, bass.ds(ii * 2 + u, 1), :], banks[6 + u][:, 0:CW].unsqueeze(1)).then_inc(h_seen, 1)
                    dve.wait_ge(h_seen, 2 + (k + 1) * NC + k)
                    nc.vector.bn_stats(stats[:, k, NC - 1, :], banks[7][:, 0:TAIL]).then_inc(h_seen, 1)
                dve.wait_ge(h_seen, 2 + MT * (NC + 1))
                for k in range(MT):
                    c(nc.vector.bn_aggr(mv[:, k], stats[:, k].rearrange("p i s -> p (i s)")))
                nc.vector.tensor_scalar(sc[:], mv[:, :, 1], 1e-5, None, ALU.add).then_inc(var_in, 1)
                dve.wait_ge(var_out, 1)
                c(nc.vector.reciprocal(sc[:], sc[:]))
                c(nc.vector.tensor_tensor(sc[:], sc[:], gb[:, 0], ALU.mult))
                c(nc.vector.tensor_tensor(bi[:], mv[:, :, 0], sc[:], ALU.mult))
                c(nc.vector.tensor_tensor(bi[:], gb[:, 1], bi[:], ALU.subtract))
                dve.sem_inc(tables, 1)
                dve.sem_inc(z_ready, 1)
                start = c.n

                def body(t, u):
                    k = start

                    def dep(ins):
                        nonlocal k
                        k += 1
                        ins.then_inc(own, 1)
                        dve.wait_ge(own, t * PER + k)
                    dve.wait_ge(wide_sq, t + 1)
                    dep(nc.vector.tensor_reduce(sq[:, u, 3:4], sq[:, u, 0:3], AX.X, ALU.add))
                    dve.sem_inc(fin, 1)
                    dve.wait_ge(fout, t + 1)
                    dep(nc.vector.tensor_scalar(sq[:, u, 3:4], sq[:, u, 3:4], MIN_NORM, None, ALU.max))
                    dep(nc.vector.reciprocal(sq[:, u, 3:4], sq[:, u, 3:4]))
                    dep(nc.vector.tensor_scalar(sq[:, u, 3:4], sq[:, u, 3:4], REACH, 1.0, ALU.mult, ALU.min))
                    for b in range(3):
                        to = z[:, u].rearrange("p (h k n) -> p h k n", h=2, k=MT)[:, :, 2 * b:2 * b + 2]
                        ins = nc.vector.tensor_scalar(to, banks[2 + b][:, :].rearrange("p (k h n) -> p h k n", k=2, h=2),
                                                      sq[:, u, 3:4], None, ALU.mult)
                        if b == 2:
                            nc_ins = ins
                    nc_ins.then_inc(z_ready, 1)
                    dve.wait_ge(z_ready, t + 2)
                    g = z[:, u].rearrange("p (g x) -> p g x", g=MG)
                    qv, kv, vv = (g[:, :, j * 32:(j + 1) * 32] for j in range(3))
                    zz = zq[:].rearrange("p (g x) -> p g x", g=MG)
                    dep(nc.vector.tensor_scalar(zz, kv, 0.0, None, ALU.max))
                    dep(nc.vector.tensor_reduce(ksum[:], zz, AX.X, ALU.add))
                    dep(nc.vector.tensor_scalar(zz, vv, MIN_NORM, None, ALU.add))
                    dep(nc.vector.reciprocal(zz, zz))
                    dep(nc.vector.scalar_tensor_tensor(qv, qv, 0.0, ksum[:].unsqueeze(2).to_broadcast([P, MG, 32]), ALU.max, ALU.mult))
                    dep(nc.vector.tensor_tensor(qv, qv, vv, ALU.mult))
                    nc.vector.tensor_tensor(out[:, bass.ds(t, 1), :].rearrange("p t (g x) -> p (t g) x", g=MG), qv, zz, ALU.mult).then_inc(o_ready, 1)
                    assert k - start == PER
                PER = 10
                with dve.Fori(0, NT // 2) as half:
                    t = half * 2
                    body(t, 0)
                    body(t + 1, 1)
                body(NT - 1, 0)
                c.n = start + PER * NT
                dve.wait_ge(nroot, 1)
                c(nc.vector.tensor_scalar(norm[:], norm[:], MIN_NORM, None, ALU.max))
                c(nc.vector.reciprocal(norm[:], norm[:]))
                c(nc.vector.tensor_scalar(norm[:], norm[:], REACH, 1.0, ALU.mult, ALU.min))
                dve.sem_inc(ftd, 2)

                def residual(t, u):
                    dve.wait_ge(resed, t + 3)
                    nc.vector.scalar_tensor_tensor(m.rows[:, bass.ds(t, 1), :], banks[2 + u][:, 0:F].unsqueeze(1), norm[:, bass.ds(t, 1)],
                                                   bres[:].unsqueeze(1), ALU.mult, ALU.add).then_inc(ftd, 1)
                with dve.Fori(0, NT // 2) as half:
                    t = half * 2
                    residual(t, 0)
                    residual(t + 1, 1)
                residual(NT - 1, 0)
                dve.wait_ge(tanh, 1)
                c(nc.vector.tensor_scalar(f1[:], f1[:], MIN_NORM, None, ALU.max))
                dve.sem_inc(tanh, 1)
                dve.wait_ge(tanh, 3)
                c(nc.vector.reciprocal(f1[:], f1[:]))
                c(nc.vector.scalar_tensor_tensor(f1[:], f2[:], MAX_NORM, f1[:], ALU.min, ALU.mult))
                with dve.Fori(0, NT) as t:
                    x = m.x[:, bass.ds(t, 1), :]
                    nc.vector.scalar_tensor_tensor(x, m.rows[:, bass.ds(t, 1), :], f1[:, bass.ds(t, 1)], x, ALU.mult, ALU.add)

            @block.tensor
            def _(pe):
                pe.wait_ge(loaded, 96)
                pe.sem_inc(tcopied, 1)
                for tt in range(TU):
                    for u in range(U):
                        pe.wait_ge(scaled, tt * U + u + 1)
                        pe.wait_ge(tcopied, tt * U + u + 1)
                        for f in range(FT):
                            tr = nc.tensor.transpose(banks[u][:, f * P:(f + 1) * P], m.rows[:, bass.ds(tt * U + u, 1), f * P:(f + 1) * P], m.ident[:])
                        tr.then_inc(turned, 1)
                pe.wait_ge(tcopied, NT + 5)
                for k in range(MT):
                    with pe.Fori(0, NC // 2) as ii:
                        for u in range(2):
                            pe.wait_ge(h_seen, ii * 2 + u + 1 + k * (NC + 1))
                            for f in range(FT):
                                mm = nc.tensor.matmul(banks[6 + u][:, 0:CW], w[:, f, k * P:(k + 1) * P], m.xT[:, f, bass.ds((ii * 2 + u) * CW, CW)],
                                                      start=f == 0, stop=f == FT - 1)
                            mm.then_inc(h_made, 1)
                pe.wait_ge(tables, 1)
                pe.sem_inc(wide_made, 2)

                def front(t, u):
                    pe.wait_ge(relued, t + 2)
                    for k in range(MT):
                        b, o = divmod(k * P, 512)
                        for f in range(FT):
                            mm = nc.tensor.matmul(banks[b][:, o:o + P], w[:, f, k * P:(k + 1) * P], m.xT[:, f, bass.ds(t * P, P)],
                                                  start=f == 0, stop=f == FT - 1)
                    mm.then_inc(pre, 1)

                def back(t, u):
                    pe.wait_ge(relued, t + 3)
                    pe.wait_ge(z_ready, t + 1)
                    for k in range(MT):
                        mm = nc.tensor.matmul(banks[2 + k // 2][:, (k % 2) * F:(k % 2) * F + F], rT[:, u, k],
                                              mix[:, k].rearrange("p h n -> p (h n)"), start=True, stop=True)
                    mm.then_inc(wide_made, 1)
                front(0, 0)
                with pe.Fori(0, NT // 2) as half:
                    t = half * 2
                    back(t, 0)
                    front(t + 1, 1)
                    back(t + 1, 1)
                    front(t + 2, 0)
                back(NT - 1, 0)
                pe.wait_ge(o_ready, NT)
                pe.sem_inc(resed, 2)

                def turn(t, u):
                    pe.wait_ge(ocopy, t + 1)
                    for k in range(OT):
                        tr = nc.tensor.transpose(banks[u][:, k * P:(k + 1) * P],
                                                 out[:, bass.ds(t, 1), k * P:(k + 1) * P].rearrange("p t c -> p (t c)"), m.ident[:])
                    tr.then_inc(orot, 1)

                def project(t, u):
                    pe.wait_ge(ocopy, t + 3)
                    pe.wait_ge(ftd, t + 1)
                    for k in range(OT):
                        mm = nc.tensor.matmul(banks[2 + u][:, 0:F], oT[:, u, k * P:(k + 1) * P], wres[:, k], start=k == 0, stop=k == OT - 1)
                    mm.then_inc(resed, 1)
                turn(0, 0)
                for t in range(0, NT - 1, 2):
                    turn(t + 1, 1)
                    project(t, 0)
                    turn(t + 2, 0)
                    project(t + 1, 1)
                project(NT - 1, 0)


def top_expert(nc, a, m, banks):
    CH = U * P
    SLOTS = (NP + XQ * (P - 1)) // P
    QT = 4
    QUADS = SLOTS // QT
    QW = QT * P
    assert SLOTS % (2 * QT) == 0
    with Stage(nc, "top") as st:
        w1 = st.sb("w1", [P, FT, HID])
        b1 = st.sb("b1", [P, HT])
        wg = st.sb("wg", [P, HT, XQ])
        bg = st.sb("bg", [P, XQ])
        bd = st.sb("bd", [P, XQ, F])
        wd = st.sb("wd", [P, XQ, HT, F])
        hT = st.sb("hT", [P, HT, CH])
        z = st.sb("z", [P, NT, XQ])
        p = st.sb("p", [P, NT, XQ])
        order = st.sb("order", [P, NT, XQ])
        before = st.sb("before", [P, P])
        ones = st.sb("ones", [P, P])
        sel = st.sb("sel", [P, NT, XQ])
        seen = st.sb("seen", [P, NT, XQ])
        top = st.sb("top", [P, NT])
        total = st.sb("total", [P, NT])
        tiles = st.sb("tiles", [P, 2, XQ])
        tiles_i = st.sb("tiles_i", [P, XQ], I32)
        slot = st.sb("slot", [P, NT], I32)
        tile_no = st.sb("tile_no", [1, SLOTS, XQ])
        expert_f = st.sb("expert_f", [1, SLOTS])
        expert = st.sb("expert", [1, SLOTS], I32)
        sorted_rows = nc.dram_tensor("sorted_rows", (SLOTS * P, F), F32, kind="Internal").ap()
        sorted_out = nc.dram_tensor("sorted_out", (SLOTS * P, F), F32, kind="Internal").ap()
        loaded, own, hid, gelu, logits, z_kept, zs, exps, chosen, counted, placed, zeroed, made = (
            st.sem(x) for x in ("loaded", "own", "hid", "gelu", "logits", "z_kept", "zs", "exps", "chosen", "counted",
                                "placed", "zeroed", "made"))
        experts, scattered = st.sem("experts"), st.gather_sem("scattered")
        BANKS = 4
        with nc.Block() as block:
            @block.sync
            def _(sp):
                for to, x in ((w1, "top_w1"), (b1, "top_b1"), (wg, "top_wg"), (bg, "top_bg"), (bd, "top_bd")):
                    sp.dma_start(to[:], a[x]).then_inc(loaded, 16)
                for e in range(XQ):
                    sp.dma_start(wd[:, e], a["top_wd"][e]).then_inc(experts, 16)
                for j in range(0, SLOTS, 2):
                    sp.dma_start(sorted_rows[j * P:(j + 2) * P, :].rearrange("(j p) f -> p j f", p=P),
                                 m.zeros[:].rearrange("p (j f) -> p j f", j=2)).then_inc(zeroed, 16)
                sp.wait_ge(zeroed, 16 * (SLOTS // 2))
                sp.wait_ge(experts, 16 * XQ)

            @block.gpsimd
            def _(pool):
                nc.gpsimd.memset(ones[:], 1.0).then_inc(made, 1)
                pool.wait_ge(made, 1)
                nc.gpsimd.affine_select(out=before[:], in_=ones[:], compare_op=ALU.is_gt, fill=0.0,
                                        base=0, pattern=[[1, P]], channel_multiplier=-1).then_inc(made, 1)
                nc.gpsimd.iota(order[:], [[0, NT], [-1, XQ]], base=XQ, channel_multiplier=0,
                               allow_small_or_imprecise_dtypes=True).then_inc(made, 1)
                nc.gpsimd.iota(tile_no[:], [[1, SLOTS], [0, XQ]], base=0, channel_multiplier=0,
                               allow_small_or_imprecise_dtypes=True).then_inc(made, 1)
                pool.wait_ge(placed, 1)
                pool.wait_ge(zeroed, 16 * (SLOTS // 2))
                for t in range(NT):
                    nc.gpsimd.indirect_dma_start(
                        out=sorted_rows, out_offset=bass.IndirectOffsetOnAxis(ap=slot[:, t:t + 1], axis=0),
                        in_=m.rows[:, t], in_offset=None).then_inc(scattered, 16)
                pool.wait_ge(scattered, 16 * NT)

            @block.tensor
            def _(pe):
                pe.wait_ge(loaded, 16 * 5)
                with pe.Fori(0, TU) as ch:
                    for k in range(HT):
                        for hf in range(2):
                            n = k * 2 + hf
                            pe.wait_ge(gelu, ch * 16 + n + 1)
                            for f in range(FT):
                                mm = nc.tensor.matmul(banks[n % BANKS][:, 0:CW], w1[:, f, k * P:(k + 1) * P],
                                                      m.xT[:, f, bass.ds(ch * CH + hf * CW, CW)], start=f == 0, stop=f == FT - 1)
                            mm.then_inc(hid, 1)
                    pe.wait_ge(gelu, ch * 16 + 16 + BANKS)
                    pe.wait_ge(z_kept, ch + 1)
                    for u in range(U):
                        for k in range(HT):
                            mm = nc.tensor.matmul(banks[7][:, u * XQ:(u + 1) * XQ], hT[:, k, u * P:(u + 1) * P], wg[:, k],
                                                  start=k == 0, stop=k == HT - 1)
                    mm.then_inc(logits, 1)
                pe.wait_ge(made, 4)
                pe.wait_ge(chosen, 1)
                flat = sel[:].rearrange("p t e -> p (t e)")
                nc.tensor.matmul(banks[5][:, 0:NT * XQ], before[:], flat, start=True, stop=True).then_inc(counted, 1)
                nc.tensor.matmul(banks[6][:, 0:NT * XQ], ones[:], flat, start=True, stop=True).then_inc(counted, 1)

            @block.scalar
            def _(act):
                act.sem_inc(gelu, BANKS)
                act.wait_ge(loaded, 16 * 5)
                with act.Fori(0, TU) as ch:
                    act.wait_ge(logits, ch + 1)
                    for k in range(HT):
                        for hf in range(2):
                            act.wait_ge(hid, ch * 16 + k * 2 + hf + 1)
                            nc.scalar.activation(hT[:, k, hf * CW:(hf + 1) * CW], banks[(k * 2 + hf) % BANKS][:, 0:CW], ACT.Gelu,
                                                 bias=b1[:, k:k + 1]).then_inc(gelu, 1)
                act.wait_ge(zs, 1)
                nc.scalar.activation(p[:], z[:], ACT.Exp).then_inc(exps, 1)

            @block.vector
            def _(dve):
                dve.sem_inc(z_kept, 1)
                dve.sem_inc(logits, 1)
                dve.wait_ge(loaded, 16 * 5)
                c = Chain(dve, own)
                with dve.Fori(0, TU) as ch:
                    dve.wait_ge(logits, ch + 2)
                    nc.vector.tensor_tensor(z[:, bass.ds(ch * U, U), :], banks[7][:, 0:U * XQ].rearrange("p (t e) -> p t e", e=XQ),
                                            bg[:].unsqueeze(1).to_broadcast([P, U, XQ]), ALU.add).then_inc(z_kept, 1)
                dve.wait_ge(z_kept, 1 + TU)

                def act_exp():
                    dve.sem_inc(zs, 1)
                    dve.wait_ge(exps, 1)
                softmax_rows(nc, c, act_exp, z, p, top, total)
                whole = [P, NT, XQ]
                dve.wait_ge(made, 4)
                c(nc.vector.tensor_reduce(top[:], p[:], AX.X, ALU.max))
                c(nc.vector.tensor_tensor(sel[:], p[:], top[:].unsqueeze(2).to_broadcast(whole), ALU.is_equal))
                c(nc.vector.tensor_tensor(sel[:], sel[:], order[:], ALU.mult))
                c(nc.vector.tensor_reduce(total[:], sel[:], AX.X, ALU.max))
                c(nc.vector.tensor_tensor(sel[:], sel[:], total[:].unsqueeze(2).to_broadcast(whole), ALU.is_equal))
                dve.sem_inc(chosen, 1)
                dve.wait_ge(counted, 2)
                c(nc.vector.tensor_copy(z[:], banks[6][:, 0:NT * XQ].rearrange("p (t e) -> p t e", e=XQ)))
                for e in range(XQ):
                    c(nc.vector.tensor_tensor_scan(seen[:, :, e], ones[:, 0:NT], z[:, :, e], 0.0, ALU.mult, ALU.add))
                c(nc.vector.tensor_scalar(tiles_i[:], seen[:, NT - 1], float(P - 1), None, ALU.add))
                c(nc.vector.tensor_scalar(tiles_i[:], tiles_i[:], P.bit_length() - 1, None, ALU.arith_shift_right))
                c(nc.vector.tensor_copy(tiles[:, 0], tiles_i[:]))
                c(nc.vector.tensor_tensor_scan(tiles[:, 1], ones[:, 0:XQ], tiles[:, 0], 0.0, ALU.mult, ALU.add))
                c(nc.vector.tensor_tensor(seen[:], seen[:], z[:], ALU.subtract))
                c(nc.vector.tensor_tensor(seen[:], seen[:], banks[5][:, 0:NT * XQ].rearrange("p (t e) -> p t e", e=XQ), ALU.add))
                c(nc.vector.tensor_tensor(tiles[:, 0], tiles[:, 1], tiles[:, 0], ALU.subtract))
                c(nc.vector.scalar_tensor_tensor(seen[:], tiles[:, 0].unsqueeze(1).to_broadcast(whole), float(P), seen[:], ALU.mult, ALU.add))
                c(nc.vector.tensor_tensor(seen[:], seen[:], sel[:], ALU.mult))
                c(nc.vector.tensor_reduce(total[:], seen[:], AX.X, ALU.add))
                c(nc.vector.tensor_copy(slot[:], total[:]))
                dve.sem_inc(placed, 1)
                c(nc.vector.tensor_tensor(tile_no[:], tile_no[:], tiles[0:1, 1].unsqueeze(1).to_broadcast([1, SLOTS, XQ]), ALU.is_ge))
                c(nc.vector.tensor_reduce(expert_f[:], tile_no[:], AX.X, ALU.add))
                c(nc.vector.tensor_scalar(expert_f[:], expert_f[:], float(XQ - 1), None, ALU.min))
                c(nc.vector.tensor_copy(expert[:], expert_f[:]))

        xs = st.sb("xs", [P, 2, QT, F])
        xsT = st.sb("xsT", [P, FT, QW])
        y = st.sb("y", [P, 2, QT, F])
        RING = 2 * QT
        yx = xs[:].rearrange("p u j f -> p (u j) f")
        arrived = [st.sem(f"arrived{u}") for u in range(2)]
        y_stored = [st.sem(f"y_stored{u}") for u in range(2)]
        turned, copied, hid2, gelu2, y_made, y_kept, stored, added, own2 = (
            st.sem(x) for x in ("turned", "copied", "hid2", "gelu2", "y_made", "y_kept", "stored", "added", "own2"))
        gathered = [st.gather_sem(f"gathered{u}") for u in range(RING)]

        def slots(table, q):
            return table[bass.ds(q * QW, QW), :].rearrange("(j p) f -> p j f", p=P)
        with nc.Block() as block:
            @block.sync
            def _(sp):
                for u in range(2):
                    sp.sem_inc(y_stored[u], 16)
                    sp.dma_start(xs[:, u], slots(sorted_rows, u)).then_inc(arrived[u], 16)
                with sp.Fori(0, QUADS // 2 - 1) as qq:
                    for u in range(2):
                        sp.wait_ge(turned, qq * 2 + u + 1)
                        sp.dma_start(xs[:, u], slots(sorted_rows, qq * 2 + u + 2)).then_inc(arrived[u], 16)
                        sp.wait_ge(y_kept, (qq * 2 + u) * QT + QT + 4)
                        sp.dma_start(slots(sorted_out, qq * 2 + u), y[:, u]).then_inc(y_stored[u], 16)
                for u in range(2):
                    sp.wait_ge(y_kept, (QUADS - 2 + u) * QT + QT + 4)
                    sp.dma_start(slots(sorted_out, QUADS - 2 + u), y[:, u]).then_inc(y_stored[u], 16)
                for t in range(0, NT - 1, U):
                    n = min(U, NT - 1 - t)
                    sp.wait_ge(added, t + n)
                    sp.dma_start(m.out[t * P:(t + n) * P, :].rearrange("(t p) f -> p t f", p=P), m.x[:, t:t + n, :]).then_inc(stored, 16)
                sp.wait_ge(added, NT)
                sp.dma_start(m.out[(NT - 1) * P:N, :], m.x[0:N - (NT - 1) * P, NT - 1, :]).then_inc(stored, 16)
                sp.wait_ge(stored, 16 * (-(-(NT - 1) // U) + 1))

            @block.tensor
            def _(pe):
                pe.sem_inc(y_made, 1)
                with pe.Fori(0, QUADS // 2) as qq:
                    for u in range(2):
                        q = qq * 2 + u
                        pe.wait_ge(arrived[u], (qq + 1) * 16)
                        pe.wait_ge(copied, q * FT + FT)
                        for f in range(FT):
                            for j in range(QT):
                                tr = nc.tensor.transpose(banks[f][:, j * P:(j + 1) * P], xs[:, u, j, f * P:(f + 1) * P], m.ident[:])
                        tr.then_inc(turned, 1)
                        pe.wait_ge(copied, q * FT + 2 * FT)
                        for k in range(HT):
                            pe.wait_ge(gelu2, q * HT + k + 1)
                            for f in range(FT):
                                mm = nc.tensor.matmul(banks[2 + k % 2][:, 0:QW], w1[:, f, k * P:(k + 1) * P], xsT[:, f],
                                                      start=f == 0, stop=f == FT - 1)
                            mm.then_inc(hid2, 1)
                        for j in range(QT):
                            e = pe.value_load(expert[0:1, bass.ds(q * QT + j, 1)], min_val=0, max_val=XQ - 1)
                            if j == 0:
                                pe.wait_ge(gelu2, q * HT + HT + 2)
                            pe.wait_ge(y_kept, q * QT + j + 1)
                            for k in range(HT):
                                mm = nc.tensor.matmul(banks[4 + j][:, 0:F], hT[:, k, j * P:(j + 1) * P],
                                                      wd[:, bass.ds(e, 1), k].rearrange("p e f -> p (e f)"), start=k == 0, stop=k == HT - 1)
                            mm.then_inc(y_made, 1)

            @block.scalar
            def _(act):
                act.sem_inc(copied, FT)
                act.sem_inc(gelu2, 2)
                with act.Fori(0, QUADS // 2) as qq:
                    for u in range(2):
                        q = qq * 2 + u
                        act.wait_ge(turned, q + 1)
                        act.wait_ge(hid2, q * HT + 1)
                        for f in range(FT):
                            nc.scalar.activation(xsT[:, f], banks[f][:, 0:QW], ACT.Copy).then_inc(copied, 1)
                        act.wait_ge(y_made, q * QT + 1)
                        for k in range(HT):
                            act.wait_ge(hid2, q * HT + k + 2)
                            nc.scalar.activation(hT[:, k, 0:QW], banks[2 + k % 2][:, 0:QW], ACT.Gelu, bias=b1[:, k:k + 1]).then_inc(gelu2, 1)

            @block.gpsimd
            def _(pool):
                for u in range(2):
                    pool.wait_ge(y_stored[u], 16 + 16 * (QUADS // 2))
                for t in range(NT):
                    if t >= RING:
                        pool.wait_ge(added, t - RING + 1)
                    nc.gpsimd.indirect_dma_start(
                        out=yx[:, t % RING, :], out_offset=None, in_=sorted_out,
                        in_offset=bass.IndirectOffsetOnAxis(ap=slot[:, t:t + 1], axis=0)).then_inc(gathered[t % RING], 16)

            @block.vector
            def _(dve):
                dve.sem_inc(y_kept, 4)
                dve.sem_inc(hid2, 1)
                with dve.Fori(0, QUADS // 2) as qq:
                    for u in range(2):
                        dve.wait_ge(y_stored[u], qq * 16 + 16)
                        for j in range(QT):
                            q = qq * 2 + u
                            e = dve.value_load(expert[0:1, bass.ds(q * QT + j, 1)], min_val=0, max_val=XQ - 1)
                            dve.wait_ge(y_made, q * QT + j + 2)
                            nc.vector.tensor_tensor(y[:, u, j].unsqueeze(1), banks[4 + j][:, 0:F].unsqueeze(1), bd[:, bass.ds(e, 1), :], ALU.add).then_inc(y_kept, 1)
                for t in range(NT):
                    dve.wait_ge(gathered[t % RING], 16 * (t // RING + 1))
                    nc.vector.scalar_tensor_tensor(m.x[:, t], yx[:, t % RING], top[:, t:t + 1], m.x[:, t], ALU.mult, ALU.add).then_inc(added, 1)


class Memory:
    pass


def network(nc, a, out, stages=99):
    ctx = ExitStack()
    with ctx:
        m = Memory()

        def sb(name, shape, dt=F32):
            return ctx.enter_context(nc.sbuf_tensor(name, shape, dt))
        banks = [ctx.enter_context(nc.psum_tensor(f"bank{i}", [P, 512], F32)) for i in range(8)]
        m.out = out
        m.ident = sb("ident", [P, P])
        m.zeros = sb("zeros", [P, 512])
        m.x = sb("x", [P, NT, F])
        m.rows = sb("rows", [P, NT, F])
        m.xT = sb("xT", [P, FT, NP])
        edge_ctx = ctx.enter_context(ExitStack())
        m.node_no, m.src, m.dst, m.ranges, m.unsorted, m.sums = (
            edge_ctx.enter_context(nc.sbuf_tensor(name, shape, dt)) for name, shape, dt in (
                ("node_no", [P, NP], F32), ("src", [P, ET], I32), ("dst", [P, ET], F32),
                ("ranges", [1, NT * 4], I32), ("unsorted", [1, 1], I32), ("sums", [P, NT, F + HEADS], F32)))
        m.d_rows = nc.dram_tensor("score_rows", (ET // ROW_TILES, HEADS * ROW_TILES * P), F32, kind="Internal").ap()
        m.d_best = nc.dram_tensor("best_scores", (NP, HEADS), F32, kind="Internal").ap()
        m.d_q, m.d_k, m.d_v, m.d_h = (nc.dram_tensor(f"table_{x}", (NP, F), F32, kind="Internal").ap() for x in "qkvh")

        constants(nc, a, m, banks)
        layer_norm(nc, "norm0", m.x, m.rows, m.xT, m.ident, banks)
        with nc.sbuf_tensor("probs", [P, ET, HEADS], F32) as m.probs, nc.sbuf_tensor("scores", [P, HEADS, ET], F32) as m.scores:
            node_tables(nc, "qkv", m.xT, [a["gnn_wq"], a["gnn_wk"], a["gnn_wv"]], [a["gnn_bq"], a["gnn_bk"], a["gnn_bv"]],
                        [m.d_q, m.d_k, m.d_v], banks)
            edge_scores(nc, a, m, banks)
            largest_scores(nc, a, m, banks)
            attention_sums(nc, a, m, banks)
        with nc.sbuf_tensor("big", [P, FT, NP], F32) as m.big:
            with nc.sbuf_tensor("context", [P, FT, P], F32) as m.context, nc.sbuf_tensor("gain", [P, 2, FT], F32) as gain:
                linear_attention(nc, a, m, banks)
                load_small(nc, gain, a["mix_ln"])
                layer_norm(nc, "norm_mix", m.rows, m.rows, m.big, m.ident, banks, gain[:, 0], gain[:, 1])
                gated_mix(nc, a, m, banks)
            first_update(nc, a, m, banks)
        if stages > 1:
            layer_norm(nc, "norm1", m.x, m.rows, m.xT, m.ident, banks)
            soft_experts(nc, a, m, banks)
        recycle_semaphores(nc)
        if stages > 2:
            layer_norm(nc, "norm2", m.x, m.rows, m.xT, m.ident, banks)
            node_tables(nc, "h", m.xT, [a["gnn1_wnode"]], [a["gnn1_bnode"]], [m.d_h], banks)
            edge_convolution(nc, a, m, banks)
        if stages > 3:
            spline_layer(nc, a, m, banks)
            edge_ctx.close()
            recycle_semaphores(nc)
        if stages > 4:
            ball_attention(nc, a, m, banks)
        if stages > 5:
            layer_norm(nc, "norm3", m.x, m.rows, m.xT, m.ident, banks)
            top_expert(nc, a, m, banks)
        else:
            with Stage(nc, "dbg") as st:
                s = st.sem("s")
                with nc.Block() as block:
                    @block.sync
                    def _(sp):
                        src = m.sums if stages == 3 else m.x
                        sp.dma_start(m.out[0:24 * P, :].rearrange("(t p) f -> p t f", p=P), src[:, 0:24, 0:F]).then_inc(s, 16)
                        sp.dma_start(m.out[24 * P:N, :], src[0:N - 24 * P, 24, 0:F]).then_inc(s, 16)
                        sp.wait_ge(s, 32)


def load_small(nc, to, src):
    with Stage(nc, "small") as st:
        loaded = st.sem("loaded")
        with nc.Block() as block:
            @block.sync
            def _(sp):
                sp.dma_start(to[:], src).then_inc(loaded, 16)
                sp.wait_ge(loaded, 16)



def _kxn(w):
    k, n = w.shape
    return w.reshape(k // P, P, n).transpose(1, 0, 2)


def _col(v):
    v = v.reshape(v.shape[:-1] + (v.shape[-1] // P, P))
    return np.moveaxis(v, -1, 0)


def _row(v):
    return np.broadcast_to(v, (P,) + v.shape)


def _layouts(i):
    f = {k: np.asarray(v) for k, v in i.items()}
    a = {}
    a["x"] = np.concatenate([f["x"], np.zeros((NP - N, F), np.float32)])
    src = np.concatenate([f["src"], np.zeros(EP - E, np.int32)])
    dst = np.concatenate([f["dst"], np.full(EP - E, NOWHERE, np.int32)])
    a["src_tiles"], a["dst_tiles"] = src.reshape(ET, P).T, dst.reshape(ET, P).T
    end = np.full(1, -1, np.int32)
    a["dst_scan"] = dst.reshape(-1, ROW_TILES * P)
    a["before_scan"] = np.concatenate([end, dst[:-1]]).reshape(-1, ROW_TILES * P)
    a["after_scan"] = np.concatenate([dst[1:], end]).reshape(-1, ROW_TILES * P)
    e = np.concatenate([f["edge_attr_384"], np.zeros((EP - E, ED), np.float32)])
    a["edges"] = e.reshape(ET, P, EC, P).transpose(0, 3, 2, 1)
    for n in "qkv":
        a[f"gnn_w{n}"], a[f"gnn_b{n}"] = _kxn(f[f"L0_gnn_W{n}"].T), _row(f[f"L0_gnn_b{n}"])
    a["gnn_wskip"], a["gnn_bskip"] = _kxn(f["L0_gnn_Wskip"].T), _row(f["L0_gnn_bskip"])
    a["gnn_wgate"] = _row(f["L0_gnn_Wgate"].reshape(3, F))
    a["gnn_bgate"], a["gnn_slope"] = _row(f["L0_gnn_bgate"]), _row(f["L0_gnn_prelu_a"].reshape(1))
    a["gnn_ln_w"], a["gnn_ln_b"] = _row(f["L0_gnn_ln_w"]), _row(f["L0_gnn_ln_b"])
    for j, n in enumerate("qkv"):
        a[f"mix_w{n}"] = _kxn(f["L0_mix_Wqkv"][:, j * F:(j + 1) * F])
    a["mix_wproj"], a["mix_bproj"] = _kxn(f["L0_mix_Wproj"]), _row(f["L0_mix_bproj"])
    a["mix_ln"] = _col(np.stack([f["L0_mix_ln_g"], f["L0_mix_ln_b"]]))
    a["mix_wg1"], a["mix_bg1"] = _kxn(f["L0_mix_Wg1"]), f["L0_mix_bg1"][:, None]
    a["mix_wg2"], a["mix_bg2"] = f["L0_mix_Wg2"], _col(f["L0_mix_bg2"])
    a["ffn_wr"], a["ffn_br"] = _kxn(f["L0_ffn_Wr"]), _row(f["L0_ffn_br"])
    for x, n in (("w1", "W1"), ("w2", "W2"), ("wo", "Wo")):
        a[f"ffn_{x}"] = np.stack([_kxn(w) for w in f[f"L0_ffn_{n}"]])
    for j in "12":
        raw = np.stack([f[f"L0_ffn_{n}{j}"] for n in ("b", "g", "be", "m", "v")])
        a[f"ffn_bn{j}"] = _col(raw).reshape(P, 5, XQ * FT)
    a["ffn_bo"] = f["L0_ffn_bo"]
    a["gnn1_wedge"], a["gnn1_bedge"] = _kxn(f["L1_gnn_W_edge"].T), _row(f["L1_gnn_b_edge"])
    a["gnn1_wnode"], a["gnn1_bnode"] = _kxn(f["L1_gnn_W_node"].T), _row(f["L1_gnn_b_node"])
    a["base_w"] = _kxn(f["L1_gnn_base_weight"].T)
    a["spline_w"] = f["L1_gnn_spline_weight"].transpose(1, 2, 0).reshape(FT, P, KS, F).transpose(1, 0, 2, 3)
    a["spline_scaler"] = _kxn(f["L1_gnn_spline_scaler"].T)
    a["ball_w"] = _kxn(f["L1_mix_w_qkv"][:, :, 2].T)
    a["ball_bn"] = _col(np.stack([f["L1_mix_bn_gamma"], f["L1_mix_bn_beta"]]))
    a["ball_wdw"] = _col(f["L1_mix_w_dw"][:, 0, 2])
    pw = np.zeros((MT, P, P), np.float32)
    w = f["L1_mix_w_pw"][:, :, 0].reshape(MT, P // 32, 32, 32)
    for b in range(P // 32):
        pw[:, b * 32:(b + 1) * 32, b * 32:(b + 1) * 32] = w[:, b].transpose(0, 2, 1)
    a["ball_wpw"] = pw.transpose(1, 0, 2)
    a["ball_wres"], a["ball_bres"] = _kxn(f["L1_mix_w_res"][:, :, 0].T), _row(f["L1_mix_b_res"])
    a["top_w1"], a["top_b1"] = _kxn(f["L1_ffn_W1"]), _col(f["L1_ffn_b1"])
    a["top_wg"], a["top_bg"] = _kxn(f["L1_ffn_Wg"]), _row(f["L1_ffn_bg"])
    a["top_wd"] = np.stack([_kxn(w) for w in f["L1_ffn_Wd"]])
    a["top_bd"] = _row(f["L1_ffn_bd"])
    return {k: np.ascontiguousarray(v) for k, v in a.items()}


STAGES = 99


def kernel(**inputs):
    import concourse.bacc as bacc
    from concourse.bass_utils import run_bass_kernel_spmd

    arrays = _layouts(inputs)
    nc = bacc.Bacc("TRN2", target_bir_lowering=False, num_devices=1)
    aps = {k: nc.dram_tensor(f"in_{k}", v.shape, mybir.dt.from_np(v.dtype), kind="ExternalInput").ap()
           for k, v in arrays.items()}
    out = nc.dram_tensor("out", (N, F), F32, kind="ExternalOutput").ap()
    network(nc, aps, out, STAGES)
    r = run_bass_kernel_spmd(nc, [{f"in_{k}": v for k, v in arrays.items()}], core_ids=[0])
    return r.results[0]["out"]
```
